# Optimizing a Trainium2 kernel written in Bass

```python
import numpy as np
import jax
import jax.numpy as jnp

def _softmax(x, axis=-1):
    return jax.nn.softmax(x, axis=axis)

def _gelu(x):
    return jax.nn.gelu(x, approximate=True)

def _silu(x):
    return jax.nn.silu(x)

def _sigmoid(x):
    return jax.nn.sigmoid(x)

def _layernorm(x, axis=-1, eps=1e-05):
    m = jnp.mean(x, axis=axis, keepdims=True)
    v = jnp.var(x, axis=axis, keepdims=True)
    return (x - m) / jnp.sqrt(v + eps)

def _scatter_add(tgt, idx, src, axis=0):
    return tgt.at[idx].add(src)

def _segment_sum(src, seg, n):
    return jax.ops.segment_sum(src, seg, n)
kernel_name = 'mk_gnn_preln_d4_gnn_r8_354eee'

def setup_inputs(seed: int=0):
    np.random.seed(seed)
    _w = jnp.asarray

    def _rec_inputs():
        import jax
        import jax.numpy as jnp
        _gk = jax.random.key(seed)
        x = -0.000202 + 1 * jax.random.normal(jax.random.fold_in(_gk, 1), (12500, 128), jnp.float32)
        src = jax.random.randint(jax.random.fold_in(_gk, 2), (200000,), 0, 12500, jnp.int32)
        dst = jax.random.randint(jax.random.fold_in(_gk, 3), (200000,), 0, 12500, jnp.int32)
        _o = jnp.argsort(dst, stable=True)
        src = src[_o]
        dst = dst[_o]
        edge_attr_128 = 5.93493e-05 + 1.00006 * jax.random.normal(jax.random.fold_in(_gk, 11), (200000, 128), jnp.float32)
        return (x, src, dst, edge_attr_128)
    x, src, dst, edge_attr_128 = _rec_inputs()

    def _L0_gnn_setup():
        import jax, jax.numpy as jnp
        import numpy as np
        BN_EPS = 1e-05

        def _bn(x, g, b):
            mu = jnp.mean(x, axis=0)
            var = jnp.mean(jnp.square(x - mu), axis=0)
            return g * (x - mu) * jax.lax.rsqrt(var + BN_EPS) + b
        key = jax.random.key(seed)
        ks = jax.random.split(key, 18)
        N, E, Cin, H, L, Cout = (6250, 75000, 128, 128, 3, 128)
        s_in = 1.0 / np.sqrt(Cin)
        s_h = 1.0 / np.sqrt(H)
        s_2h = 1.0 / np.sqrt(2 * H)
        return {'x': jax.random.normal(ks[0], (N, Cin), jnp.float32), 'edge_index': jax.random.randint(ks[1], (2, E), 0, N, jnp.int32), 'edge_attr': jax.random.normal(ks[2], (E, Cin), jnp.float32), 'W_atom': jax.random.normal(ks[3], (Cin, H), jnp.float32) * s_in, 'b_atom': jnp.zeros((H,), jnp.float32), 'W_bond': jax.random.normal(ks[4], (Cin, H), jnp.float32) * s_in, 'b_bond': jnp.zeros((H,), jnp.float32), 'eps': jnp.zeros((L,), jnp.float32), 'W1': jax.random.normal(ks[5], (L, H, 2 * H), jnp.float32) * s_h, 'b1': jnp.zeros((L, 2 * H), jnp.float32), 'g1': jnp.ones((L, 2 * H), jnp.float32), 'be1': jnp.zeros((L, 2 * H), jnp.float32), 'W2': jax.random.normal(ks[6], (L, 2 * H, H), jnp.float32) * s_2h, 'b2': jnp.zeros((L, H), jnp.float32), 'gn': jnp.ones((L, H), jnp.float32), 'bet': jnp.zeros((L, H), jnp.float32), 'W_out': jax.random.normal(ks[7], (H, Cout), jnp.float32) * s_h, 'b_out': jnp.zeros((Cout,), jnp.float32)}
    _L0_gnn_all = _L0_gnn_setup()
    _L0_gnn_in = {k: v for k, v in _L0_gnn_all.items() if k in ('W_atom', 'b_atom', 'W_bond', 'b_bond', 'eps', 'W1', 'b1', 'g1', 'be1', 'W2', 'b2', 'gn', 'bet', 'W_out', 'b_out')}
    del _L0_gnn_all

    def _L1_gnn_setup():
        import jax, jax.numpy as jnp
        import numpy as np
        N_NODES = 12500
        N_EDGES = 78125
        D_IN = 128
        D_OUT = 128
        key = jax.random.key(seed)
        k1, k2, k3, k4, k5 = jax.random.split(key, 5)
        scale = 1.0 / np.sqrt(D_IN)
        x = jax.random.normal(k1, (N_NODES, D_IN), dtype=jnp.float32)
        edge_index = jax.random.randint(k2, (2, N_EDGES), 0, N_NODES, dtype=jnp.int64)
        W_l = jax.random.normal(k3, (D_IN, D_OUT), dtype=jnp.float32) * scale
        b_l = jax.random.normal(k4, (D_OUT,), dtype=jnp.float32) * scale
        W_r = jax.random.normal(k5, (D_IN, D_OUT), dtype=jnp.float32) * scale
        return {'x': x, 'edge_index': edge_index, 'W_l': W_l, 'b_l': b_l, 'W_r': W_r}
    _L1_gnn_all = _L1_gnn_setup()
    _L1_gnn_in = {k: v for k, v in _L1_gnn_all.items() if k in ('W_l', 'b_l', 'W_r')}
    del _L1_gnn_all

    def _L2_gnn_setup():
        import jax, jax.numpy as jnp
        import numpy as np
        N = 12500
        E = 200000
        IN_DIM = 128
        HEADS = 4
        OUT_DIM = 32
        ALPHA = 0.2
        EPS = 1e-08
        key = jax.random.key(seed)
        k1, k2, k3, k4, k5, k6 = jax.random.split(key, 6)
        x = jax.random.normal(k1, (N, IN_DIM), dtype=jnp.float32)
        edge_index = jax.random.randint(k2, (2, E), 0, N, dtype=jnp.int64)
        W = jax.random.normal(k3, (IN_DIM, HEADS * OUT_DIM), dtype=jnp.float32) * (2.0 / IN_DIM) ** 0.5
        A_left = jax.random.normal(k4, (HEADS, OUT_DIM, 1), dtype=jnp.float32) * (2.0 / OUT_DIM) ** 0.5
        A_right = jax.random.normal(k5, (HEADS, OUT_DIM, 1), dtype=jnp.float32) * (2.0 / OUT_DIM) ** 0.5
        residual_projection = jax.random.normal(k6, (IN_DIM, HEADS * OUT_DIM), dtype=jnp.float32) * (2.0 / IN_DIM) ** 0.5
        return {'x': x, 'edge_index': edge_index, 'W': W, 'A_left': A_left, 'A_right': A_right, 'residual_projection': residual_projection}
    _L2_gnn_all = _L2_gnn_setup()
    _L2_gnn_in = {k: v for k, v in _L2_gnn_all.items() if k in ('W', 'A_left', 'A_right', 'residual_projection')}
    del _L2_gnn_all

    def _L3_gnn_setup():
        import jax, jax.numpy as jnp
        import numpy as np
        N_NODES = 6250
        C_IN = 128
        C_OUT = 128
        N_EDGES = 100000
        NEG_SLOPE_GAT = 0.2
        NEG_SLOPE_ACT = 0.01
        EPS = 1e-05

        def _gatv2_block(x, edge_index, W_l, W_r, att, bias, ln_w, ln_b):
            n = x.shape[0]
            loop = jnp.arange(n, dtype=edge_index.dtype)
            src = jnp.concatenate([edge_index[0], loop])
            dst = jnp.concatenate([edge_index[1], loop])
            x_l = x @ W_l
            x_r = x @ W_r
            m = x_l[src] + x_r[dst]
            logits = jax.nn.leaky_relu(m, NEG_SLOPE_GAT) @ att
            seg_max = jax.ops.segment_max(logits, dst, num_segments=n)
            expv = jnp.exp(logits - seg_max[dst])
            denom = jax.ops.segment_sum(expv, dst, num_segments=n)
            alpha = expv / denom[dst]
            out = jax.ops.segment_sum(alpha[:, None] * x_l[src], dst, num_segments=n) + bias
            out = jax.nn.leaky_relu(out, NEG_SLOPE_ACT)
            mu = out.mean()
            out = out - mu
            std = jnp.sqrt((out * out).mean())
            out = out / (std + EPS)
            return out * ln_w + ln_b
        key = jax.random.key(seed)
        ks = jax.random.split(key, 8)
        s_in = 1.0 / np.sqrt(C_IN)
        x = jax.random.normal(ks[0], (N_NODES, C_IN), dtype=jnp.float32)
        edge_index = jax.random.randint(ks[1], (2, N_EDGES), 0, N_NODES, dtype=jnp.int64)
        W_l = jax.random.uniform(ks[2], (C_IN, C_OUT), jnp.float32, -s_in, s_in)
        W_r = jax.random.uniform(ks[3], (C_IN, C_OUT), jnp.float32, -s_in, s_in)
        att = jax.random.uniform(ks[4], (C_OUT,), jnp.float32, -1.0 / np.sqrt(C_OUT), 1.0 / np.sqrt(C_OUT))
        bias = jnp.zeros((C_OUT,), jnp.float32)
        ln_w = jnp.ones((C_OUT,), jnp.float32)
        ln_b = jnp.zeros((C_OUT,), jnp.float32)
        return {'x': x, 'edge_index': edge_index, 'W_l': W_l, 'W_r': W_r, 'att': att, 'bias': bias, 'ln_w': ln_w, 'ln_b': ln_b}
    _L3_gnn_all = _L3_gnn_setup()
    _L3_gnn_in = {k: v for k, v in _L3_gnn_all.items() if k in ('W_l', 'W_r', 'att', 'bias', 'ln_w', 'ln_b')}
    del _L3_gnn_all
    return {'x': x, 'src': src, 'dst': dst, 'edge_attr_128': edge_attr_128, 'L0_gnn_W_atom': _L0_gnn_in['W_atom'], 'L0_gnn_b_atom': _L0_gnn_in['b_atom'], 'L0_gnn_W_bond': _L0_gnn_in['W_bond'], 'L0_gnn_b_bond': _L0_gnn_in['b_bond'], 'L0_gnn_eps': _L0_gnn_in['eps'], 'L0_gnn_W1': _L0_gnn_in['W1'], 'L0_gnn_b1': _L0_gnn_in['b1'], 'L0_gnn_g1': _L0_gnn_in['g1'], 'L0_gnn_be1': _L0_gnn_in['be1'], 'L0_gnn_W2': _L0_gnn_in['W2'], 'L0_gnn_b2': _L0_gnn_in['b2'], 'L0_gnn_gn': _L0_gnn_in['gn'], 'L0_gnn_bet': _L0_gnn_in['bet'], 'L0_gnn_W_out': _L0_gnn_in['W_out'], 'L0_gnn_b_out': _L0_gnn_in['b_out'], 'L1_gnn_W_l': _L1_gnn_in['W_l'], 'L1_gnn_b_l': _L1_gnn_in['b_l'], 'L1_gnn_W_r': _L1_gnn_in['W_r'], 'L2_gnn_W': _L2_gnn_in['W'], 'L2_gnn_A_left': _L2_gnn_in['A_left'], 'L2_gnn_A_right': _L2_gnn_in['A_right'], 'L2_gnn_residual_projection': _L2_gnn_in['residual_projection'], 'L3_gnn_W_l': _L3_gnn_in['W_l'], 'L3_gnn_W_r': _L3_gnn_in['W_r'], 'L3_gnn_att': _L3_gnn_in['att'], 'L3_gnn_bias': _L3_gnn_in['bias'], 'L3_gnn_ln_w': _L3_gnn_in['ln_w'], 'L3_gnn_ln_b': _L3_gnn_in['ln_b']}

def reference(x, src, dst, edge_attr_128, L0_gnn_W_atom, L0_gnn_b_atom, L0_gnn_W_bond, L0_gnn_b_bond, L0_gnn_eps, L0_gnn_W1, L0_gnn_b1, L0_gnn_g1, L0_gnn_be1, L0_gnn_W2, L0_gnn_b2, L0_gnn_gn, L0_gnn_bet, L0_gnn_W_out, L0_gnn_b_out, L1_gnn_W_l, L1_gnn_b_l, L1_gnn_W_r, L2_gnn_W, L2_gnn_A_left, L2_gnn_A_right, L2_gnn_residual_projection, L3_gnn_W_l, L3_gnn_W_r, L3_gnn_att, L3_gnn_bias, L3_gnn_ln_w, L3_gnn_ln_b):
    import jax
    import jax.numpy as jnp

    def _L0_gnn_ref(x, edge_index, edge_attr, W_atom, b_atom, W_bond, b_bond, eps, W1, b1, g1, be1, W2, b2, gn, bet, W_out, b_out):
        import jax, jax.numpy as jnp
        import numpy as np
        BN_EPS = 1e-05

        def _bn(x, g, b):
            mu = jnp.mean(x, axis=0)
            var = jnp.mean(jnp.square(x - mu), axis=0)
            return g * (x - mu) * jax.lax.rsqrt(var + BN_EPS) + b
        N = x.shape[0]
        L = eps.shape[0]
        src, dst = (edge_index[0], edge_index[1])
        h = x @ W_atom + b_atom
        ea = edge_attr @ W_bond + b_bond
        for i in range(L):
            msg = jax.nn.relu(h[src] + ea)
            agg = jax.ops.segment_sum(msg, dst, num_segments=N)
            z = (1.0 + eps[i]) * h + agg
            z = z @ W1[i] + b1[i]
            z = jax.nn.relu(_bn(z, g1[i], be1[i]))
            z = z @ W2[i] + b2[i]
            h = jax.nn.relu(_bn(z, gn[i], bet[i]))
        return h @ W_out + b_out

    def _L1_gnn_ref(x, edge_index, W_l, b_l, W_r):
        import jax, jax.numpy as jnp
        import numpy as np
        N_NODES = 12500
        N_EDGES = 78125
        D_IN = 128
        D_OUT = 128
        src = edge_index[0]
        dst = edge_index[1]
        n = x.shape[0]
        msgs = x[src]
        agg = jax.ops.segment_sum(msgs, dst, num_segments=n)
        deg = jax.ops.segment_sum(jnp.ones_like(dst, dtype=x.dtype), dst, num_segments=n)
        mean = agg / jnp.maximum(deg, 1.0)[:, None]
        return mean @ W_l + b_l + x @ W_r

    def _L2_gnn_ref(x, edge_index, W, A_left, A_right, residual_projection):
        import jax, jax.numpy as jnp
        import numpy as np
        N = 12500
        E = 200000
        IN_DIM = 128
        HEADS = 4
        OUT_DIM = 32
        ALPHA = 0.2
        EPS = 1e-08
        n = x.shape[0]
        H = jnp.matmul(x, W).reshape(n, HEADS, OUT_DIM).transpose(1, 0, 2)
        H_s = jnp.einsum('hnd,hd->hn', H, A_left[..., 0])
        H_t = jnp.einsum('hnd,hd->hn', H, A_right[..., 0])
        src = edge_index[0]
        tgt = edge_index[1]
        s = H_s[:, src] + H_t[:, tgt]
        s = jnp.where(s >= 0, s, ALPHA * s)
        s = jnp.exp(s - jnp.max(s))
        denom = jnp.zeros((HEADS, n), dtype=s.dtype).at[:, src].add(s)
        alpha = s / (denom[:, src] + EPS)
        H_sf = H[:, tgt]
        agg = jnp.zeros((HEADS, n, OUT_DIM), dtype=H.dtype).at[:, src].add(alpha[..., None] * H_sf)
        agg = agg + jnp.matmul(x, residual_projection).reshape(n, HEADS, OUT_DIM).transpose(1, 0, 2)
        res = agg.transpose(1, 0, 2).reshape(n, HEADS * OUT_DIM)
        return jax.nn.elu(res)

    def _L3_gnn_ref(x, edge_index, W_l, W_r, att, bias, ln_w, ln_b):
        import jax, jax.numpy as jnp
        import numpy as np
        N_NODES = 6250
        C_IN = 128
        C_OUT = 128
        N_EDGES = 100000
        NEG_SLOPE_GAT = 0.2
        NEG_SLOPE_ACT = 0.01
        EPS = 1e-05

        def _gatv2_block(x, edge_index, W_l, W_r, att, bias, ln_w, ln_b):
            n = x.shape[0]
            loop = jnp.arange(n, dtype=edge_index.dtype)
            src = jnp.concatenate([edge_index[0], loop])
            dst = jnp.concatenate([edge_index[1], loop])
            x_l = x @ W_l
            x_r = x @ W_r
            m = x_l[src] + x_r[dst]
            logits = jax.nn.leaky_relu(m, NEG_SLOPE_GAT) @ att
            seg_max = jax.ops.segment_max(logits, dst, num_segments=n)
            expv = jnp.exp(logits - seg_max[dst])
            denom = jax.ops.segment_sum(expv, dst, num_segments=n)
            alpha = expv / denom[dst]
            out = jax.ops.segment_sum(alpha[:, None] * x_l[src], dst, num_segments=n) + bias
            out = jax.nn.leaky_relu(out, NEG_SLOPE_ACT)
            mu = out.mean()
            out = out - mu
            std = jnp.sqrt((out * out).mean())
            out = out / (std + EPS)
            return out * ln_w + ln_b
        return _gatv2_block(x, edge_index, W_l, W_r, att, bias, ln_w, ln_b)
    edge_index = jnp.stack([src, dst])
    h = jnp.maximum(_layernorm(x, axis=-1), 0.0)
    x = x + _L0_gnn_ref(h, edge_index, edge_attr_128, L0_gnn_W_atom, L0_gnn_b_atom, L0_gnn_W_bond, L0_gnn_b_bond, L0_gnn_eps, L0_gnn_W1, L0_gnn_b1, L0_gnn_g1, L0_gnn_be1, L0_gnn_W2, L0_gnn_b2, L0_gnn_gn, L0_gnn_bet, L0_gnn_W_out, L0_gnn_b_out)
    h = jnp.maximum(_layernorm(x, axis=-1), 0.0)
    x = x + _L1_gnn_ref(h, edge_index, L1_gnn_W_l, L1_gnn_b_l, L1_gnn_W_r)
    h = jnp.maximum(_layernorm(x, axis=-1), 0.0)
    x = x + _L2_gnn_ref(h, edge_index, L2_gnn_W, L2_gnn_A_left, L2_gnn_A_right, L2_gnn_residual_projection)
    h = jnp.maximum(_layernorm(x, axis=-1), 0.0)
    x = x + _L3_gnn_ref(h, edge_index, L3_gnn_W_l, L3_gnn_W_r, L3_gnn_att, L3_gnn_bias, L3_gnn_ln_w, L3_gnn_ln_b)
    return x

_drawn_inputs = setup_inputs


def setup_inputs(seed=0):
    import zlib

    import numpy as np

    out = dict(_drawn_inputs(seed))
    spreads = {'L0_gnn_b_atom': (0.0, 0.293),
     'L0_gnn_b_bond': (0.0, 0.1),
     'L0_gnn_eps': (0.0, 0.8),
     'L0_gnn_b1': (0.0, 0.8),
     'L0_gnn_g1': (1.0, 0.2),
     'L0_gnn_be1': (0.0, 0.1),
     'L0_gnn_b2': (0.0, 0.8),
     'L0_gnn_gn': (1.0, 0.2),
     'L0_gnn_bet': (0.0, 0.1),
     'L0_gnn_b_out': (0.0, 0.1),
     'L3_gnn_bias': (0.0, 0.1),
     'L3_gnn_ln_w': (1.0, 0.2),
     'L3_gnn_ln_b': (0.0, 0.1)}
    factors = {'L3_gnn_W_r': 8.0, 'L3_gnn_att': 3.244}
    for name, (base, spread) in spreads.items():
        noise = np.random.default_rng([zlib.crc32(name.encode()), seed]).standard_normal(out[name].shape)
        drawn = base * np.exp(spread * noise) if base else spread * noise
        out[name] = jnp.asarray(drawn.astype(out[name].dtype))
    for name, factor in factors.items():
        out[name] = (out[name] * factor).astype(out[name].dtype)
    return out
```

```python
from contextlib import ExitStack, contextmanager

import concourse.bass as bass
from concourse import mybir

P = 128
N, E, D = 12500, 200000, 128
BLOCKS = -(-N // P)
NP = BLOCKS * P
TILES = -(-E // P)
UNROLL = 16
ROUNDS = -(-(TILES + BLOCKS - 1) // UNROLL)
STEPS = ROUNDS * UNROLL
G = 4
JG = UNROLL // G
TW = STEPS + 2 * UNROLL
KT = STEPS // P
SORT_ROUNDS = -(-TILES // UNROLL)
TPAD = SORT_ROUNDS * UNROLL
PAD_SRC = NP
PAD_DST = 20000
LAST_ROWS = N - (BLOCKS - 1) * P
W = 132
NB = 7
NR = BLOCKS // NB
L = 3
HID = 256
HEADS = 4
HD = 32
BN_EPS = 1e-5
LN_EPS = 1e-5
REC = STEPS * P + (TPAD - TILES + 1) * P
LAST = None
SKIP = ()

ALU = mybir.AluOpType
ACT = mybir.ActivationFunctionType
F32 = mybir.dt.float32
BF16 = mybir.dt.bfloat16
I32 = mybir.dt.int32
AX = mybir.AxisListType.X
ds = bass.ds


class Kept:
    pass


class Stop(Exception):
    pass


class Soft:

    def __init__(self, sem):
        self.sem, self.base = sem, 0


SOFT = []


@contextmanager
def phase(nc, name, sems, soft=()):
    with ExitStack() as ctx:
        names = sems.split() + ["gate"]
        first = SOFT[-1].sem.num + 1
        handles = [nc.alloc_semaphore(f"{name}_{n}", num=first + i) for i, n in enumerate(names)]
        s = {**dict(zip(names, handles)), **dict(zip(dict(soft), SOFT))}

        def sb(n, shape, dt=F32):
            return ctx.enter_context(nc.sbuf_tensor(f"{name}_{n}", shape, dt))

        def ps(n, shape, dt=F32):
            return ctx.enter_context(nc.psum_tensor(f"{name}_{n}", shape, dt))

        with ExitStack() as inner:
            yield (lambda: inner.enter_context(nc.Block())), s, sb, ps
        nc.all_engine_barrier(sems_to_clear=range(first, first + len(names)))
        for c, total in zip(SOFT, dict(soft).values()):
            c.base += total
        for h in handles:
            nc.release_semaphore(h)
    if LAST == name:
        raise Stop


def await_(eng, s, sem, value):
    if isinstance(sem, Soft):
        sem, value = sem.sem, value + sem.base
    eng.wait_ge(sem, value)
    eng.sem_inc(s["gate"], 1)


def wait_soft(eng, soft, value):
    eng.wait_ge(soft.sem, soft.base + value)


def along(ap, n):
    return ap.unsqueeze(2).to_broadcast([ap.shape[0], ap.shape[1], n])


def across(ap, k):
    return ap.unsqueeze(1).to_broadcast([ap.shape[0], k, ap.shape[1]])


def load_registers(eng, row, name, lo, hi):
    n = row.shape[1]
    regs = [eng.alloc_register(f"{name}{j}") for j in range(n)]
    eng.load(regs, row)
    return [eng.snap(r, min_val=lo, max_val=hi) for r in regs], regs


def constants(nc, k):
    with phase(nc, "const", "zeroed iota ones") as (block, s, sb, ps):
        blk = block()

        @blk.gpsimd
        def _(pool):
            nc.gpsimd.memset(k.ident[:, :], 0.0).then_inc(s["zeroed"], 1)
            nc.gpsimd.memset(k.ones[:, :], 1.0).then_inc(s["zeroed"], 1)
            nc.gpsimd.iota(k.iota_i[:, :], pattern=[[1, P]], base=0, channel_multiplier=0).then_inc(s["zeroed"], 1)
            nc.gpsimd.iota(k.step_i[:, :], pattern=[[P, KT]], base=0, channel_multiplier=1).then_inc(s["zeroed"], 1)
            pool.wait_ge(s["zeroed"], 4)
            nc.gpsimd.affine_select(out=k.ident[:, :], in_=k.ident[:, :], compare_op=ALU.not_equal, fill=1.0,
                                    base=0, pattern=[[-1, P]], channel_multiplier=1).then_inc(s["iota"], 1)
            nc.gpsimd.affine_select(out=k.not_before[:, :], in_=k.ones[:, :], compare_op=ALU.is_ge, fill=0.0,
                                    base=0, pattern=[[-1, P]], channel_multiplier=1).then_inc(s["iota"], 1)
            pool.wait_ge(s["iota"], 2)

        @blk.vector
        def _(dve):
            nc.vector.memset(k.zeros[:, :], 0.0).then_inc(s["ones"], 1)
            dve.wait_ge(s["zeroed"], 4)
            nc.vector.tensor_copy(k.iota[:, :], k.iota_i[:, :]).then_inc(s["ones"], 1)
            nc.vector.tensor_copy(k.step_f[:, :], k.step_i[:, :]).then_inc(s["ones"], 1)
            dve.wait_ge(s["iota"], 2)
            nc.vector.tensor_copy(k.tri_rest[:, :], k.not_before[:, :]).then_inc(s["ones"], 1)
            nc.vector.tensor_scalar(k.tri[:, :], k.not_before[:, :], -1.0, 1.0, ALU.mult,
                                    ALU.add).then_inc(s["ones"], 1)
            dve.wait_ge(s["ones"], 5)


def histogram(nc, k, name, cols_dram, tiled):
    with phase(nc, name, "keys cnt sums m rows row_in done") as (block, s, sb, ps):
        keys = sb("keys", [P, TPAD], I32)
        keysf = sb("keysf", [P, TPAD])
        junk = sb("junk", [P, TPAD])
        thr = sb("thr", [P, BLOCKS + 1])
        cnt = sb("cnt", [P, BLOCKS + 1])
        start = sb("start", [P, BLOCKS + 1])
        lo_i = sb("lo_i", [P, BLOCKS + 1], I32)
        hi_i = sb("hi_i", [P, BLOCKS + 1], I32)
        lo = sb("lo", [P, BLOCKS + 1])
        hi = sb("hi", [P, BLOCKS + 1])
        some = sb("some", [P, BLOCKS])
        ntile = sb("ntile", [P, BLOCKS])
        incl = sb("incl", [P, BLOCKS])
        first = sb("first", [P, BLOCKS])
        m = sb("m", [P, KT, BLOCKS])
        m2 = sb("m2", [P, KT, BLOCKS])
        count = sb("count", [P, KT])
        firstsel = sb("firstsel", [P, KT])
        tilesel = sb("tilesel", [P, KT])
        over = sb("over", [P, KT])
        blk_i = sb("blk_i", [P, KT], I32)
        tile_i = k.tile_i
        locbase = k.locbase
        sums = ps("sums", [P, 512])
        dve_steps = [0]
        blk = block()

        @blk.sync
        def _(sp):
            sp.dma_start(keys[:, :], cols_dram).then_inc(s["keys"], 16)
            sp.wait_ge(s["rows"], 1)
            sp.dma_start(k.blk_dram.rearrange("(i p) -> p i", p=P), blk_i[:, :],
                         allow_slow_non_contiguous=True).then_inc(s["row_in"], 16)
            sp.wait_ge(s["row_in"], 16)
            if tiled:
                sp.dma_start(k.tile_dram.rearrange("(i p) -> p i", p=P), tile_i[:, :],
                             allow_slow_non_contiguous=True).then_inc(s["row_in"], 16)
                sp.wait_ge(s["row_in"], 32)
                sp.dma_start(k.tilerow[:, 0:STEPS], k.tile_dram.rearrange("(a c) -> a c", a=1)).then_inc(s["done"], 16)
            sp.dma_start(k.blockrow[:, 0:STEPS], k.blk_dram.rearrange("(a c) -> a c", a=1)).then_inc(s["done"], 16)
            sp.wait_ge(s["done"], 32 if tiled else 16)

        @blk.tensor
        def _(pe):
            pe.wait_ge(s["cnt"], BLOCKS + 1)
            nc.tensor.matmul(sums[:, 0:BLOCKS + 1], k.ones[:, :], cnt[:, :], start=True, stop=True).then_inc(s["sums"], 1)

        @blk.vector
        def _(dve):
            def then(ins):
                dve_steps[0] += 1
                ins.then_inc(s["m"], 1)
                dve.wait_ge(s["m"], dve_steps[0])

            then(nc.vector.tensor_scalar(thr[:, 0:BLOCKS + 1], k.iota[:, 0:BLOCKS + 1], float(P), None, ALU.mult))
            dve.wait_ge(s["keys"], 16)
            then(nc.vector.tensor_copy(keysf[:, :], keys[:, :]))
            for b in range(BLOCKS + 1):
                nc.vector.tensor_scalar(junk[:, :], keysf[:, :], thr[:, b:b + 1], 0.0, ALU.is_lt, ALU.add,
                                        accum_out=cnt[:, b:b + 1]).then_inc(s["cnt"], 1)
                dve.wait_ge(s["cnt"], b + 1)
            dve.wait_ge(s["sums"], 1)
            then(nc.vector.tensor_copy(start[:, :], sums[:, 0:BLOCKS + 1]))
            if tiled:
                then(nc.vector.tensor_copy(lo_i[:, :], start[:, :]))
                then(nc.vector.tensor_scalar(hi[:, :], start[:, :], float(P - 1), None, ALU.add))
                then(nc.vector.tensor_copy(hi_i[:, :], hi[:, :]))
                then(nc.vector.tensor_scalar(lo_i[:, :], lo_i[:, :], 7, None, ALU.arith_shift_right))
                then(nc.vector.tensor_scalar(hi_i[:, :], hi_i[:, :], 7, None, ALU.arith_shift_right))
                then(nc.vector.tensor_copy(lo[:, :], lo_i[:, :]))
                then(nc.vector.tensor_copy(hi[:, :], hi_i[:, :]))
                then(nc.vector.tensor_tensor(some[:, :], start[:, 1:BLOCKS + 1], start[:, 0:BLOCKS], ALU.is_gt))
                then(nc.vector.tensor_tensor(ntile[:, :], hi[:, 1:BLOCKS + 1], lo[:, 0:BLOCKS], ALU.subtract))
                then(nc.vector.tensor_tensor(ntile[:, :], ntile[:, :], some[:, :], ALU.mult))
            else:
                then(nc.vector.tensor_tensor(hi[:, 0:BLOCKS], start[:, 1:BLOCKS + 1], start[:, 0:BLOCKS], ALU.subtract))
                then(nc.vector.tensor_scalar(hi[:, 0:BLOCKS], hi[:, 0:BLOCKS], float(P - 1), None, ALU.add))
                then(nc.vector.tensor_copy(hi_i[:, 0:BLOCKS], hi[:, 0:BLOCKS]))
                then(nc.vector.tensor_scalar(hi_i[:, 0:BLOCKS], hi_i[:, 0:BLOCKS], 7, None, ALU.arith_shift_right))
                then(nc.vector.tensor_copy(ntile[:, :], hi_i[:, 0:BLOCKS]))
            then(nc.vector.tensor_tensor_scan(incl[:, :], ntile[:, :], k.zeros[:, 0:BLOCKS], 0.0, ALU.add, ALU.add))
            then(nc.vector.tensor_tensor(first[:, :], incl[:, :], ntile[:, :], ALU.subtract))
            then(nc.vector.tensor_tensor(m[:, :, :], across(first[:, :], KT), along(k.step_f[:, :], BLOCKS), ALU.is_le))
            then(nc.vector.tensor_reduce(count[:, :], m[:, :, :], AX, ALU.add))
            then(nc.vector.tensor_scalar(count[:, :], count[:, :], -1.0, None, ALU.add))
            then(nc.vector.tensor_copy(blk_i[:, :], count[:, :]))
            if tiled:
                then(nc.vector.tensor_tensor(m2[:, :, :], m[:, :, :], across(first[:, :], KT), ALU.mult))
                then(nc.vector.tensor_reduce(firstsel[:, :], m2[:, :, :], AX, ALU.max))
                then(nc.vector.tensor_tensor(m2[:, :, :], m[:, :, :], across(lo[:, 0:BLOCKS], KT), ALU.mult))
                then(nc.vector.tensor_reduce(tilesel[:, :], m2[:, :, :], AX, ALU.max))
                then(nc.vector.tensor_tensor(tilesel[:, :], tilesel[:, :], firstsel[:, :], ALU.subtract))
                then(nc.vector.tensor_tensor(tilesel[:, :], tilesel[:, :], k.step_f[:, :], ALU.add))
                then(nc.vector.tensor_scalar(tilesel[:, :], tilesel[:, :], float(TILES - 1), None, ALU.min))
                then(nc.vector.tensor_copy(tile_i[:, :], tilesel[:, :]))
                then(nc.vector.tensor_scalar(over[:, :], k.step_f[:, :], incl[:, BLOCKS - 1:BLOCKS], 1e6,
                                             ALU.is_ge, ALU.mult))
                then(nc.vector.scalar_tensor_tensor(locbase[:, :], count[:, :], float(P), over[:, :],
                                                    ALU.mult, ALU.add))
            else:
                then(nc.vector.tensor_scalar(k.sort_base[:, 0:BLOCKS], first[:, :], float(P), None, ALU.mult))
                then(nc.vector.memset(k.sort_base[:, BLOCKS:BLOCKS + 1], float(STEPS * P)))
            then(nc.vector.memset(k.blockrow[:, STEPS:TW], 0))
            then(nc.vector.memset(k.tilerow[:, STEPS:TW], 0))
            nc.vector.tensor_copy(junk[0:1, 0:1], k.zeros[0:1, 0:1]).then_inc(s["rows"], 1)
            dve.wait_ge(s["rows"], 1)


def step_tables(nc, k, name, from_sort):
    with phase(nc, name, "stored conv turned out tail kept",
               soft=() if from_sort else {"rows": 32 * KT}) as (block, s, sb, ps):
        n = 2
        raw = sb("raw", [P, 2, 2 * P], F32 if from_sort else I32)
        val = sb("val", [P, 2, 2 * P])
        ends = sb("ends", [1, 1], I32)
        turned = ps("turned", [P, 2, 4, P])
        blk = block()

        if from_sort:
            @blk.sync
            def _(sp):
                for i in range(KT):
                    if i >= n:
                        sp.wait_ge(s["conv"], 2 * (i - n + 1))
                    sp.dma_start(raw[:, i % n, :], k.rec_dram[i * P * P:(i + 1) * P * P, :].rearrange(
                        "(p e) c -> p (e c)", p=P)).then_inc(s["stored"], 16)
                    sp.wait_ge(s["stored"], 16 * (i + 1))
        else:
            @blk.gpsimd
            def _(pool):
                for i in range(KT):
                    if i >= n:
                        pool.wait_ge(s["conv"], 2 * (i - n + 1))
                        pool.wait_ge(s["kept"], 16 * (i - n + 1))
                    off = bass.IndirectOffsetOnAxis(ap=k.tile_i[:, i:i + 1], axis=0)
                    pool.indirect_dma_start(raw[:, i % n, 0:P], None, k.src_rows, off).then_inc(s["rows"].sem, 16)
                    pool.indirect_dma_start(raw[:, i % n, P:2 * P], None, k.dst_rows, off).then_inc(s["rows"].sem, 16)
                    wait_soft(pool, s["rows"], 32 * (i + 1))

            @blk.sync
            def _(sp):
                line = k.key_dram[1:1 + STEPS * P].rearrange("(i p e) -> i p e", p=P, e=P)
                for i in range(KT):
                    wait_soft(sp, s["rows"], 32 * (i + 1))
                    sp.dma_start(line[i], raw[:, i % n, P:2 * P]).then_inc(s["kept"], 16)
                    sp.wait_ge(s["kept"], 16 * (i + 1))
                sp.wait_ge(s["tail"], 3)
                sp.dma_start(k.key_dram[0:1].rearrange("(a c) -> a c", a=1), ends[:, :]).then_inc(s["kept"], 16)
                sp.dma_start(k.key_dram[1 + STEPS * P:2 + STEPS * P].rearrange("(a c) -> a c", a=1),
                             ends[:, :]).then_inc(s["kept"], 16)
                sp.wait_ge(s["kept"], 16 * (KT + 2))

        @blk.vector
        def _(dve):
            for i in range(KT):
                if i >= n:
                    dve.wait_ge(s["turned"], i - n + 1)
                if from_sort:
                    dve.wait_ge(s["stored"], 16 * (i + 1))
                else:
                    wait_soft(dve, s["rows"], 32 * (i + 1))
                if from_sort:
                    r = raw[:, i % n, :].rearrange("p (e c) -> p c e", c=2)
                    nc.vector.tensor_copy(val[:, i % n, 0:P], r[:, 0, :]).then_inc(s["conv"], 1)
                    nc.vector.tensor_copy(val[:, i % n, P:2 * P], r[:, 1, :]).then_inc(s["conv"], 1)
                else:
                    nc.vector.tensor_scalar(val[:, i % n, 0:P], raw[:, i % n, 0:P], float(N - 1), None,
                                            ALU.min).then_inc(s["conv"], 1)
                    nc.vector.tensor_scalar(val[:, i % n, P:2 * P], raw[:, i % n, P:2 * P], k.locbase[:, i:i + 1],
                                            None, ALU.subtract).then_inc(s["conv"], 1)
            nc.vector.memset(k.idx[:, STEPS:TW], N if from_sort else 0).then_inc(s["tail"], 1)
            nc.vector.memset(k.loc[:, STEPS:TW], -1.0).then_inc(s["tail"], 1)
            nc.vector.memset(ends[:, :], -1).then_inc(s["tail"], 1)
            dve.wait_ge(s["tail"], 3)

        @blk.tensor
        def _(pe):
            for i in range(KT):
                pe.wait_ge(s["conv"], 2 * (i + 1))
                if i >= n:
                    pe.wait_ge(s["out"], 2 * (i - n + 1))
                nc.tensor.transpose(turned[:, i % n, 0, :], val[:, i % n, 0:P], k.ident[:, :])
                nc.tensor.transpose(turned[:, i % n, 1, :], val[:, i % n, P:2 * P], k.ident[:, :]).then_inc(s["turned"], 1)

        @blk.scalar
        def _(act):
            for i in range(KT):
                act.wait_ge(s["turned"], i + 1)
                nc.scalar.copy(k.idx[:, i * P:(i + 1) * P], turned[:, i % n, 0, :]).then_inc(s["out"], 1)
                nc.scalar.copy(k.loc[:, i * P:(i + 1) * P], turned[:, i % n, 1, :]).then_inc(s["out"], 1)
            act.wait_ge(s["out"], 2 * KT)


def sort_by_source(nc, k):
    with phase(nc, "sort", "keys ints blkf prefill filled hot rank place rest "
               "base conv free", soft={f"scat{q}": 64 * SORT_ROUNDS for q in range(JG)}) as (block, s, sb, ps):
        src = sb("src", [P, TPAD], I32)
        dst = sb("dst", [P, TPAD], I32)
        blk_i = sb("blk_i", [P, TPAD], I32)
        blkf = sb("blkf", [P, TPAD + 1])
        rec = sb("rec", [P, TPAD, 2])
        fill = sb("fill", [P, REC // P, 2])
        hot = sb("hot", [P, 2, BLOCKS + 1], BF16)
        junk = sb("junk", [P, BLOCKS + 1])
        place = sb("place", [P, JG, G])
        place_i = sb("place_i", [P, JG, G], I32)
        rec4 = sb("rec4", [P, JG, G, 2])
        run = ps("run", [P, 512])
        scat = [s["scat0"], s["scat1"], s["scat2"], s["scat3"]]
        blk = block()

        @blk.sync
        def _(sp):
            sp.dma_start(src[:, :], k.src_cols).then_inc(s["keys"], 16)
            sp.dma_start(dst[:, :], k.dst_cols).then_inc(s["keys"], 16)
            sp.wait_ge(s["prefill"], 2)
            sp.dma_start(k.rec_dram.rearrange("(p e) c -> p (e c)", p=P),
                         fill[:, :, :].rearrange("p e c -> p (e c)")).then_inc(s["filled"], 16)
            sp.wait_ge(s["filled"], 16)

        @blk.tensor
        def _(pe):
            def tile(t, j):
                await_(pe, s, s["hot"], t + 1)
                nc.tensor.matmul(run[:, 0:BLOCKS + 1], k.tri[:, :], hot[:, j % 2, :], start=False, stop=False,
                                 skip_group_check=True).then_inc(s["rank"], 1)
                await_(pe, s, s["place"], t + 1)
                nc.tensor.matmul(run[:, 0:BLOCKS + 1], k.tri_rest[:, :], hot[:, j % 2, :], start=False, stop=False,
                                 skip_group_check=True).then_inc(s["rest"], 1)

            pe.sem_inc(s["rest"], 2)
            nc.tensor.matmul(run[:, 0:BLOCKS + 1], k.ident[:, :], k.sort_base[:, :], start=True, stop=False,
                             skip_group_check=True).then_inc(s["base"], 1)
            with pe.Fori(0, SORT_ROUNDS) as r:
                for j in range(UNROLL):
                    tile(r * UNROLL + j, j)

        @blk.vector
        def _(dve):
            nc.vector.memset(fill[:, :, 0:1], float(N)).then_inc(s["prefill"], 1)
            nc.vector.memset(fill[:, :, 1:2], -1.0).then_inc(s["prefill"], 1)
            dve.wait_ge(s["keys"], 32)
            nc.vector.tensor_scalar(blk_i[:, :], src[:, :], 7, None, ALU.arith_shift_right).then_inc(s["ints"], 1)
            nc.vector.tensor_scalar(rec[:, :, 0], dst[:, :], float(N - 1), None, ALU.min).then_inc(s["ints"], 1)
            dve.wait_ge(s["ints"], 2)
            nc.vector.memset(blkf[:, TPAD:TPAD + 1], -1.0).then_inc(s["ints"], 1)
            nc.vector.tensor_copy(blkf[:, 0:TPAD], blk_i[:, :]).then_inc(s["blkf"], 1)
            dve.wait_ge(s["ints"], 3)
            dve.wait_ge(s["blkf"], 1)
            nc.vector.scalar_tensor_tensor(rec[:, :, 1], blkf[:, 0:TPAD], float(-P), src[:, :], ALU.mult,
                                           ALU.add).then_inc(s["blkf"], 1)
            dve.wait_ge(s["blkf"], 2)

            def one_hot(t, j):
                await_(dve, s, s["rest"], t + 1)
                nc.vector.tensor_scalar(hot[:, j % 2, :], k.iota[:, 0:BLOCKS + 1], blkf[:, ds(t, 1)], None,
                                        ALU.is_equal).then_inc(s["hot"], 1)

            def places(t, j):
                await_(dve, s, s["rank"], t + 1)
                nc.vector.tensor_tensor_reduce(junk[:, :], run[:, 0:BLOCKS + 1], hot[:, j % 2, :], 1.0, 0.0,
                                               ALU.mult, ALU.add, place[:, j // G, j % G:j % G + 1]
                                               ).then_inc(s["place"], 1)

            dve.wait_ge(s["base"], 1)
            one_hot(0, 0)
            with dve.Fori(0, SORT_ROUNDS) as r:
                for j in range(UNROLL):
                    t = r * UNROLL + j
                    one_hot(t + 1, j + 1)
                    places(t, j)
                    if j % G == G - 1:
                        g = r * JG + j // G
                        await_(dve, s, s["place"], t + 1)
                        await_(dve, s, s["free"], g + 1)
                        nc.vector.tensor_copy(place_i[:, j // G, :], place[:, j // G, :]).then_inc(s["conv"], 1)
                        nc.vector.tensor_copy(rec4[:, j // G, :, :], rec[:, ds(r * UNROLL + (j // G) * G, G), :]
                                              ).then_inc(s["conv"], 1)

        @blk.gpsimd
        def _(pool):
            def scatter(g, q):
                await_(pool, s, s["conv"], g * 2 + 2)
                for u in range(G):
                    pool.indirect_dma_start(k.rec_dram, bass.IndirectOffsetOnAxis(
                        ap=place_i[:, q, u:u + 1], axis=0), rec4[:, q, u, :], None).then_inc(scat[q].sem, 16)

            def retire(r, q):
                await_(pool, s, scat[q], r * 64 + 64)
                pool.sem_inc(s["free"], 1)

            pool.sem_inc(s["free"], JG)
            pool.wait_ge(s["filled"], 16)
            for q in range(JG - 1):
                scatter(q, q)
            with pool.Fori(0, SORT_ROUNDS - 1) as r:
                for q in range(JG):
                    scatter(r * JG + q + JG - 1, (q + JG - 1) % JG)
                    retire(r, q)
            scatter(SORT_ROUNDS * JG - 1, JG - 1)
            for q in range(JG):
                retire(SORT_ROUNDS - 1, q)


def program(nc, t, out):
    def sb(name, shape, dt=F32):
        return nc.alloc_sbuf_tensor(name, shape, dt)

    k = Kept()
    first = min(nc.free_semaphores)
    SOFT[:] = [Soft(nc.alloc_semaphore(f"soft{i}", num=first + i)) for i in range(JG)]
    k.ident, k.ones = sb("ident", [P, P]), sb("ones", [P, P])
    k.iota_i, k.iota = sb("iota_i", [P, P], I32), sb("iota", [P, P])
    k.not_before = sb("not_before", [P, P])
    k.tri, k.tri_rest = sb("tri", [P, P], BF16), sb("tri_rest", [P, P], BF16)
    k.step_i, k.step_f = sb("step_i", [P, KT], I32), sb("step_f", [P, KT])
    k.tile_i, k.locbase = sb("tile_i", [P, KT], I32), sb("locbase", [P, KT])
    k.sort_base = sb("sort_base", [P, BLOCKS + 1])
    k.zeros = sb("zeros", [P, P])
    k.idx, k.loc = sb("idx", [P, TW], I32), sb("loc", [P, TW])
    k.blockrow, k.tilerow = sb("blockrow", [1, TW], I32), sb("tilerow", [1, TW], I32)
    k.acc = sb("acc", [P, BLOCKS * W])
    k.rec_dram = nc.dram_tensor("rec_dram", (REC, 2), F32).ap()
    k.blk_dram = nc.dram_tensor("blk_dram", (STEPS,), I32).ap()
    k.tile_dram = nc.dram_tensor("tile_dram", (STEPS,), I32).ap()
    k.key_dram = nc.dram_tensor("key_dram", (STEPS * P + 2,), I32).ap()
    k.line_dram = nc.dram_tensor("line_dram", (STEPS * P,), F32).ap()
    k.seg_dram = nc.dram_tensor("seg_dram", (STEPS * P,), F32).ap()
    k.table = nc.dram_tensor("table", (NP, D), F32).ap()
    k.table_gat = nc.dram_tensor("table_gat", (NP, W), F32).ap()
    k.x_dram = nc.dram_tensor("x_dram", (NP, D), F32).ap()
    k.res_dram = nc.dram_tensor("res_dram", (NP, D), F32).ap()
    k.rows_dram = nc.dram_tensor("rows_dram", (ROUNDS * JG + 1, P, G * P), F32).ap()
    k.tables_dram = [(nc.dram_tensor(f"idx_dram{n}", (P, TW), I32).ap(),
                      nc.dram_tensor(f"loc_dram{n}", (P, TW), F32).ap(),
                      nc.dram_tensor(f"row_dram{n}", (1, TW), I32).ap()) for n in range(2)]
    k.src_rows, k.dst_rows, k.src_cols, k.dst_cols = t["src_rows"], t["dst_rows"], t["src_cols"], t["dst_cols"]
    k.deg = sb("deg", [P, BLOCKS])
    try:
        constants(nc, k)
        histogram(nc, k, "hist_s", t["src_cols"], False)
        sort_by_source(nc, k)
        step_tables(nc, k, "tab_s", True)
        move_tables(nc, k, "keep_s", True, 1)
        histogram(nc, k, "hist_d", t["dst_cols"], True)
        step_tables(nc, k, "tab_d", False)
        move_tables(nc, k, "keep_d", True, 0)
        layers(nc, k, t, out)
    except Stop:
        pass


def rows_of(dram, i):
    return dram.rearrange("(b p) f -> p b f", p=P)[:, ds(i * NB, NB), :]


def row_vector(v):
    return v.partition_broadcast(P)


class Chain:

    def __init__(self, eng, s, sem, i, per):
        self.eng, self.s, self.sem, self.i, self.per, self.n = eng, s, sem, i, per, 0

    def __call__(self, ins):
        self.n += 1
        ins.then_inc(self.sem, 1)
        await_(self.eng, self.s, self.sem, self.i * self.per + self.n)

    def end(self):
        assert self.n == self.per, (self.n, self.per)


def layer_norm_relu(nc, s, dve, then, i, x, c, sq, st, out):
    then(nc.vector.tensor_reduce(st[:, 0, :], x, AX, ALU.add))
    then(nc.vector.tensor_scalar(st[:, 0, :], st[:, 0, :], 1.0 / D, None, ALU.mult))
    then(nc.vector.tensor_tensor(c, x, along(st[:, 0, :], D), ALU.subtract))
    then(nc.vector.tensor_tensor(sq, c, c, ALU.mult))
    then(nc.vector.tensor_reduce(st[:, 1, :], sq, AX, ALU.add))
    nc.vector.tensor_scalar(st[:, 1, :], st[:, 1, :], 1.0 / D, LN_EPS, ALU.mult, ALU.add).then_inc(s["var"], 1)
    await_(dve, s, s["std"], i + 1)
    then(nc.vector.reciprocal(st[:, 3, :], st[:, 2, :]))
    then(nc.vector.scalar_tensor_tensor(out, c, 0.0, along(st[:, 3, :], D), ALU.max, ALU.mult))


LN_VECTOR = 7


def layer_norm_std(nc, s, act, i, st):
    await_(act, s, s["var"], i + 1)
    nc.scalar.activation(st[:, 2, :], st[:, 1, :], ACT.Sqrt).then_inc(s["std"], 1)


def blocks(ap, stride=P, width=P, n=NB):
    return ap.rearrange("p (b w) -> p b w", w=stride)[:, :, 0:width]


def node_input(nc, k, t):
    with phase(nc, "nin", "w x_free var std hn turned copied prod v stored used",
               soft={"x_in": 16 * NR}) as (block, s, sb, ps):
        x, c, sq, h = (sb(n, [P, NB, P]) for n in ("x", "c", "sq", "h"))
        st = sb("st", [P, 4, NB])
        hT = sb("hT", [P, NB * P])
        tab = sb("tab", [P, NB, P])
        w = sb("w", [P, P])
        b_atom, b_bond = sb("b_atom", [P, P]), sb("b_bond", [P, P])
        eps = sb("eps", [P, L])
        turned, prod = ps("turned", [P, 2, 512]), ps("prod", [P, 2, 512])
        blk = block()
        PER = LN_VECTOR + 3

        @blk.sync
        def _(sp):
            sp.dma_start(w[:, :], t["L0_gnn_W_atom"]).then_inc(s["w"], 16)
            sp.dma_start(b_atom[:, :], row_vector(t["L0_gnn_b_atom"])).then_inc(s["w"], 16)
            sp.dma_start(b_bond[:, :], row_vector(t["L0_gnn_b_bond"])).then_inc(s["w"], 16)
            sp.dma_start(eps[:, :], row_vector(t["L0_gnn_eps"])).then_inc(s["w"], 16)
            with sp.Fori(0, NR) as i:
                await_(sp, s, s["v"], (i + 1) * PER)
                sp.dma_start(rows_of(k.table, i), tab[:, :, :]).then_inc(s["stored"], 16)
                await_(sp, s, s["stored"], (i + 1) * 16)
                sp.sem_inc(s["used"], 1)

        @blk.gpsimd
        def _(pool):
            pool.sem_inc(s["x_free"], 1)
            with pool.Fori(0, NR) as i:
                await_(pool, s, s["x_free"], i + 1)
                pool.dma_start(x[:, :, :], rows_of(t["x"], i)).then_inc(s["x_in"].sem, 16)

        @blk.vector
        def _(dve):
            dve.wait_ge(s["w"], 64)
            with dve.Fori(0, NR) as i:
                then = Chain(dve, s, s["v"], i, PER)
                await_(dve, s, s["x_in"], 16 * i + 16)
                layer_norm_relu(nc, s, dve, then, i, x[:, :, :], c[:, :, :], sq[:, :, :], st, h[:, :, :])
                dve.sem_inc(s["hn"], 1)
                dve.sem_inc(s["x_free"], 1)
                await_(dve, s, s["prod"], i + 1)
                p = blocks(prod[:, :, :].rearrange("p a b -> p (a b)")[:, 0:NB * P])
                then(nc.vector.tensor_tensor(h[:, :, :], p, across(b_atom[:, :], NB), ALU.add))
                then(nc.vector.scalar_tensor_tensor(acc_rows(k, i), h[:, :, :], eps[:, 0:1], h[:, :, :],
                                                    ALU.mult, ALU.add))
                await_(dve, s, s["used"], i + 1)
                then(nc.vector.tensor_tensor(tab[:, :, :], h[:, :, :], across(b_bond[:, :], NB), ALU.add))
                then.end()

        @blk.scalar
        def _(act):
            act.sem_inc(s["used"], 1)
            with act.Fori(0, NR) as i:
                layer_norm_std(nc, s, act, i, st)
                await_(act, s, s["turned"], i + 1)
                nc.scalar.copy(hT[:, :], turned[:, :, :].rearrange("p a b -> p (a b)")[:, 0:NB * P]
                               ).then_inc(s["copied"], 1)

        @blk.tensor
        def _(pe):
            pe.wait_ge(s["w"], 64)
            tv = turned[:, :, :].rearrange("p a b -> p (a b)")
            pv = prod[:, :, :].rearrange("p a b -> p (a b)")
            with pe.Fori(0, NR) as i:
                await_(pe, s, s["hn"], i + 1)
                for b in range(NB):
                    ins = nc.tensor.transpose(tv[:, b * P:(b + 1) * P], h[:, b, :], k.ident[:, :])
                ins.then_inc(s["turned"], 1)
                await_(pe, s, s["copied"], i + 1)
                for b in range(NB):
                    ins = nc.tensor.matmul(pv[:, b * P:(b + 1) * P], hT[:, b * P:(b + 1) * P], w[:, :],
                                           start=True, stop=True)
                ins.then_inc(s["prod"], 1)


def acc_rows(k, i, width=D, first=0):
    return k.acc[:, ds(i * (NB * W), NB * W)].rearrange("p (b w) -> p b w", w=W)[:, :, first:first + width]


def flat(psum):
    return psum.rearrange("p a b -> p (a b)")


HALVES = ((0, 512), (512, NB * P - 512))


def batch_norm(nc, s, dve, stats, agg, scale, bias, gain, shift, n, first):
    step = [first]

    def then(ins):
        step[0] += 1
        ins.then_inc(s["bn"], 1)
        dve.wait_ge(s["bn"], step[0])

    for h in range(n):
        then(nc.vector.bn_aggr(agg[:, h, 0:2], stats[:, h, :, :].rearrange("p c s -> p (c s)")))
    nc.vector.tensor_scalar(agg[:, 0:n, 2], agg[:, 0:n, 1], BN_EPS, None, ALU.add).then_inc(s["bn_var"], 1)
    dve.wait_ge(s["bn_std"], 1 if first == 0 else 2)
    then(nc.vector.reciprocal(agg[:, 0:n, 2], agg[:, 0:n, 3]))
    then(nc.vector.tensor_tensor(scale, agg[:, 0:n, 2], gain, ALU.mult))
    then(nc.vector.tensor_tensor(agg[:, 0:n, 3], agg[:, 0:n, 0], scale, ALU.mult))
    then(nc.vector.tensor_tensor(bias, shift, agg[:, 0:n, 3], ALU.subtract))
    dve.sem_inc(s["bn_out"], 1)
    return step[0]


def mlp(nc, k, t, layer):
    last = layer == L - 1
    with phase(nc, f"mlp{layer}", "w staged turned copied mm1 ev1 bn bn_var bn_std bn_out act1 mm2 ev2 act2 rows done "
               "stored used x_free var std hn turned2 copied2 prod v bnst st_free",
               soft={"x_in": 16 * NR} if last else ()) as (block, s, sb, ps):
        z1 = sb("z1", [P, 2, NP])
        w1, w2 = sb("w1", [P, HID]), sb("w2", [P, 2, D])
        cols = sb("cols", [P, 3, 2])
        cols2 = sb("cols2", [P, 3])
        zT = sb("zT", [P, NB * P])
        r1 = sb("r1", [P, 2, NB * P])
        stats1 = sb("stats1", [P, 2, 2 * NR, 6])
        stats2 = sb("stats2", [P, 1, 2 * NR + 1, 6])
        agg = sb("agg", [P, 2, 4])
        norm = sb("norm", [P, 2, 2])
        norm2 = sb("norm2", [P, 2, 1])
        rowv = sb("rowv", [P, 2, P])
        eps = sb("eps", [P, L])
        tab = sb("tab", [P, NB, P])
        turned = ps("turned", [P, 2, 512])
        z = ps("z", [P, 4, 512])
        prod = ps("prod", [P, 2, 512])
        hT = zT
        if last:
            zf = z1[:, :, :].rearrange("p a b -> p (a b)")
            n = NB * P
            x, c, sq, hn = (zf[:, j * n:(j + 1) * n].rearrange("p (b f) -> p b f", f=P) for j in range(4))
            wo, wr = zf[:, 4 * n:4 * n + P], zf[:, 4 * n + P:4 * n + 2 * P]
            bo, bl = zf[:, 4 * n + 2 * P:4 * n + 3 * P], zf[:, 4 * n + 3 * P:4 * n + 4 * P]
            hT2 = zf[:, 5 * n:6 * n]
            st = sb("st", [P, 4, NB])
        full = [(i, b, n) for i in range(NR) for b, n in ((0, 4), (4, 3))]
        blk = block()
        NW = 3 + 6 + 3 + 2

        @blk.sync
        def _(sp):
            sp.dma_start(w1[:, :], t["L0_gnn_W1"][layer]).then_inc(s["w"], 16)
            sp.dma_start(w2[:, :, :], t["L0_gnn_W2"][layer].rearrange("(h p) n -> p h n", p=P)).then_inc(s["w"], 16)
            sp.dma_start(eps[:, :], row_vector(t["L0_gnn_eps"])).then_inc(s["w"], 16)
            for n, v in enumerate((t["L0_gnn_b1"], t["L0_gnn_g1"], t["L0_gnn_be1"])):
                for h in range(2):
                    sp.dma_start(cols[:, n, h:h + 1], v[layer, h * P:(h + 1) * P].rearrange("(p a) -> p a", a=1)
                                 ).then_inc(s["w"], 16)
            for n, v in enumerate((t["L0_gnn_b2"], t["L0_gnn_gn"], t["L0_gnn_bet"])):
                sp.dma_start(cols2[:, n:n + 1], v[layer].rearrange("(p a) -> p a", a=1)).then_inc(s["w"], 16)
            sp.dma_start(rowv[:, 0, :], row_vector(t["L0_gnn_b_bond"])).then_inc(s["w"], 16)
            sp.dma_start(rowv[:, 1, :], row_vector(t["L0_gnn_b_bond"])).then_inc(s["w"], 16)
            if last:
                sp.wait_ge(s["ev2"], NR + 1)
                sp.dma_start(wo, t["L0_gnn_W_out"]).then_inc(s["w"], 16)
                sp.dma_start(wr, t["L1_gnn_W_r"]).then_inc(s["w"], 16)
                sp.dma_start(bo, row_vector(t["L0_gnn_b_out"])).then_inc(s["w"], 16)
                sp.dma_start(bl, row_vector(t["L1_gnn_b_l"])).then_inc(s["w"], 16)
            with sp.Fori(0, NR) as i:
                if last:
                    await_(sp, s, s["hn"], i + 1)
                    sp.dma_start(rows_of(k.table, i), hn).then_inc(s["stored"], 16)
                    await_(sp, s, s["done"], i + 1)
                    sp.dma_start(rows_of(k.x_dram, i), tab[:, :, :]).then_inc(s["stored"], 16)
                    await_(sp, s, s["stored"], (i + 1) * 32)
                else:
                    await_(sp, s, s["done"], i + 1)
                    sp.dma_start(rows_of(k.table, i), tab[:, :, :]).then_inc(s["stored"], 16)
                    await_(sp, s, s["stored"], (i + 1) * 16)
                sp.sem_inc(s["used"], 1)

        if last:
            @blk.gpsimd
            def _(pool):
                pool.sem_inc(s["x_free"], 1)
                pool.wait_ge(s["ev2"], NR + 1)
                with pool.Fori(0, NR) as i:
                    await_(pool, s, s["x_free"], i + 1)
                    pool.dma_start(x, rows_of(t["x"], i)).then_inc(s["x_in"].sem, 16)

        @blk.tensor
        def _(pe):
            pe.wait_ge(s["w"], 16 * NW)
            tv, zv, pv = flat(turned[:, :, :]), z, flat(prod[:, :, :])
            with pe.Fori(0, NR) as i:
                await_(pe, s, s["staged"], i + 1)
                for b in range(NB):
                    ins = nc.tensor.transpose(tv[:, b * P:(b + 1) * P], tab[:, b, :], k.ident[:, :])
                ins.then_inc(s["turned"], 1)
                await_(pe, s, s["copied"], i + 1)
                await_(pe, s, s["ev1"], 2 * i + 2)
                for h in range(2):
                    for j, (c0, n) in enumerate(HALVES):
                        ins = nc.tensor.matmul(z[:, 2 * h + j, 0:n], w1[:, h * P:(h + 1) * P], zT[:, c0:c0 + n],
                                               start=True, stop=True)
                ins.then_inc(s["mm1"], 1)
            with pe.Fori(0, NR) as i:
                await_(pe, s, s["act1"], i + 1)
                await_(pe, s, s["ev2"], i + 1)
                for j, (c0, n) in enumerate(HALVES):
                    for h in range(2):
                        ins = nc.tensor.matmul(z[:, j, 0:n], w2[:, h, :], r1[:, h, c0:c0 + n],
                                               start=h == 0, stop=h == 1)
                ins.then_inc(s["mm2"], 1)
            if last:
                pe.wait_ge(s["w"], 16 * (NW + 4))
            with pe.Fori(0, NR) as i:
                await_(pe, s, s["act2"], i + 1)
                await_(pe, s, s["rows"], i + 1)
                for b in range(NB):
                    if last:
                        ins = nc.tensor.matmul(pv[:, b * P:(b + 1) * P], hT[:, b * P:(b + 1) * P], wo,
                                               start=True, stop=True)
                    else:
                        ins = nc.tensor.transpose(pv[:, b * P:(b + 1) * P], hT[:, b * P:(b + 1) * P], k.ident[:, :])
                ins.then_inc(s["prod"], 1)
                if last:
                    await_(pe, s, s["hn"], i + 1)
                    for b in range(NB):
                        ins = nc.tensor.transpose(tv[:, b * P:(b + 1) * P], hn[:, b, :], k.ident[:, :])
                    ins.then_inc(s["turned2"], 1)
                    await_(pe, s, s["copied2"], i + 1)
                    for b in range(NB):
                        ins = nc.tensor.matmul(z[:, b // 4, b % 4 * P:b % 4 * P + P], hT2[:, b * P:(b + 1) * P], wr,
                                               start=True, stop=True)
                    ins.then_inc(s["mm2"], 1)

        @blk.scalar
        def _(act):
            act.sem_inc(s["ev1"], 2)
            act.sem_inc(s["ev2"], 1)
            act.sem_inc(s["rows"], 1)
            act.sem_inc(s["used"], 1)
            act.wait_ge(s["w"], 16 * NW)
            with act.Fori(0, NR) as i:
                await_(act, s, s["turned"], i + 2)
                nc.scalar.copy(zT[:, :], flat(turned[:, :, :])[:, 0:NB * P]).then_inc(s["copied"], 1)
                await_(act, s, s["mm1"], i + 1)
                for h in range(2):
                    nc.scalar.activation(z1[:, h, ds(i * (NB * P), NB * P)],
                                         flat(z[:, 2 * h:2 * h + 2, :])[:, 0:NB * P], ACT.Identity,
                                         bias=cols[:, 0, h:h + 1]).then_inc(s["ev1"], 1)
            act.wait_ge(s["bn_var"], 1)
            nc.scalar.activation(agg[:, 0:2, 3], agg[:, 0:2, 2], ACT.Sqrt).then_inc(s["bn_std"], 1)
            act.wait_ge(s["bn_out"], 1)
            with act.Fori(0, NR) as i:
                for h in range(2):
                    ins = nc.scalar.activation(r1[:, h, :], z1[:, h, ds(i * (NB * P), NB * P)], ACT.Relu,
                                               bias=norm[:, 1, h:h + 1], scale=norm[:, 0, h:h + 1])
                ins.then_inc(s["act1"], 1)
                await_(act, s, s["mm2"], i + 1)
                nc.scalar.activation(acc_rows(k, i), blocks(flat(z[:, 0:2, :])[:, 0:NB * P]), ACT.Identity,
                                     bias=cols2[:, 0:1]).then_inc(s["ev2"], 1)
            act.wait_ge(s["bn_var"], 2)
            nc.scalar.activation(agg[:, 0:1, 3], agg[:, 0:1, 2], ACT.Sqrt).then_inc(s["bn_std"], 1)
            act.wait_ge(s["bn_out"], 2)
            with act.Fori(0, NR) as i:
                await_(act, s, s["bnst"], i + 1)
                nc.scalar.activation(blocks(hT[:, :]), acc_rows(k, i), ACT.Relu,
                                     bias=norm2[:, 1, 0:1], scale=norm2[:, 0, 0:1]).then_inc(s["act2"], 1)
                await_(act, s, s["prod"], i + 1)
                act.sem_inc(s["bnst"], 1)
                if last:
                    layer_norm_std(nc, s, act, i, st)
                    await_(act, s, s["turned2"], i + 1)
                    nc.scalar.copy(hT2, flat(turned[:, :, :])[:, 0:NB * P]).then_inc(s["copied2"], 1)

        @blk.vector
        def _(dve):
            dve.sem_inc(s["bnst"], 1)
            dve.wait_ge(s["w"], 16 * NW)

            def stats_1(i, c, n=NB * P // 2):
                for h in range(2):
                    nc.vector.bn_stats(stats1[:, h, ds(2 * i + c, 1), :].rearrange("p a s -> p (a s)"),
                                       z1[:, h, ds(i * (NB * P) + c * (NB * P // 2), n)]).then_inc(s["st_free"], 1)

            def stage(i):
                await_(dve, s, s["turned"], i + 1)
                nc.vector.tensor_copy(tab[:, :, :], acc_rows(k, i)).then_inc(s["staged"], 1)

            dve.sem_inc(s["turned"], 1)
            stage(0)
            with dve.Fori(0, NR - 1) as i:
                stage(i + 1)
                await_(dve, s, s["ev1"], 2 * i + 4)
                stats_1(i, 0)
                stats_1(i, 1)
            dve.wait_ge(s["ev1"], 2 * NR + 2)
            stats_1(NR - 1, 0)
            stats_1(NR - 1, 1, N - (NR - 1) * NB * P - NB * P // 2)
            dve.wait_ge(s["st_free"], 4 * NR)
            n = batch_norm(nc, s, dve, stats1, agg, norm[:, 0, :], norm[:, 1, :], cols[:, 1, :], cols[:, 2, :], 2, 0)

            def stats_2(i, g, b, n, w=P, m=None):
                nc.vector.bn_stats(stats2[:, 0, ds(g, 1), :].rearrange("p a s -> p (a s)"),
                                   acc_rows(k, i)[:, b:b + n, 0:w]).then_inc(s["st_free"], 1)

            with dve.Fori(0, NR - 1) as i:
                await_(dve, s, s["ev2"], i + 2)
                stats_2(i, 2 * i, 0, 4)
                stats_2(i, 2 * i + 1, 4, 3)
            dve.wait_ge(s["ev2"], NR + 1)
            stats_2(NR - 1, 2 * NR - 2, 0, 4)
            stats_2(NR - 1, 2 * NR - 1, 4, 2)
            stats_2(NR - 1, 2 * NR, 6, 1, LAST_ROWS)
            dve.wait_ge(s["st_free"], 6 * NR + 1)
            n = batch_norm(nc, s, dve, stats2, agg, norm2[:, 0, :], norm2[:, 1, :], cols2[:, 1:2], cols2[:, 2:3], 1, n)
            PER = LN_VECTOR + 4 if last else 2
            if last:
                dve.wait_ge(s["w"], 16 * (NW + 4))
            with dve.Fori(0, NR) as i:
                then = Chain(dve, s, s["v"], i, PER)
                await_(dve, s, s["prod"], i + 1)
                p = blocks(flat(prod[:, :, :])[:, 0:NB * P])
                if last:
                    await_(dve, s, s["x_in"], 16 * i + 16)
                    await_(dve, s, s["used"], i + 1)
                    then(nc.vector.tensor_tensor(x, x, p, ALU.add))
                    dve.sem_inc(s["rows"], 1)
                    then(nc.vector.tensor_tensor(tab[:, :, :], x, across(bo, NB), ALU.add))
                    layer_norm_relu(nc, s, dve, then, i, tab[:, :, :], c, sq, st, hn)
                    dve.sem_inc(s["hn"], 1)
                    dve.sem_inc(s["x_free"], 1)
                    await_(dve, s, s["mm2"], NR + i + 1)
                    then(nc.vector.tensor_tensor(tab[:, :, :], tab[:, :, :], across(bl, NB), ALU.add))
                    then(nc.vector.tensor_tensor(tab[:, :, :], tab[:, :, :], blocks(flat(z[:, 0:2, :])[:, 0:NB * P]),
                                                 ALU.add))
                else:
                    then(nc.vector.tensor_scalar(acc_rows(k, i), p, eps[:, layer + 1:layer + 2], None, ALU.mult))
                    then(nc.vector.tensor_tensor(acc_rows(k, i), acc_rows(k, i), p, ALU.add))
                    await_(dve, s, s["used"], i + 1)
                    nc.vector.tensor_tensor(tab[:, :, :], p, across(rowv[:, 0, :], NB), ALU.add).then_inc(s["rows"], 1)
                    await_(dve, s, s["rows"], i + 2)
                dve.sem_inc(s["done"], 1)
                then.end()
            if last:
                nc.vector.memset(k.acc[:, :], 0.0).then_inc(s["bn"], 1)
                dve.wait_ge(s["bn"], n + 1)


def ring_counts(lead):
    return {f"gat{q}": 64 * (ROUNDS + (1 if q < lead else 0)) for q in range(JG)}


def gather_ring(nc, s, pool, k, idxs, rows, table, lead, width):
    gat = [s["gat0"], s["gat1"], s["gat2"], s["gat3"]]

    def gather(g, q):
        await_(pool, s, s["idx_ready"], g + 1)
        for u in range(G):
            pool.indirect_dma_start(rows[:, q, u, 0:width], None, table,
                                    bass.IndirectOffsetOnAxis(ap=idxs[:, q, u:u + 1], axis=0)).then_inc(gat[q].sem, 16)

    for g in range(lead):
        gather(g, g)
    with pool.Fori(0, ROUNDS) as r:
        for q in range(JG):
            gather(r * JG + q + lead, (q + lead) % JG)
    for q in range(JG):
        wait_soft(pool, gat[q], 64 * (ROUNDS + (1 if q < lead else 0)))


def refill(nc, s, k, act, idxs, m, q):
    nc.scalar.copy(idxs[:, q, :], k.idx[:, ds(m * G, G)]).then_inc(s["idx_ready"], 1)


def edges_gine(nc, k, t, layer):
    with phase(nc, f"gine{layer}", "w ea0 ea1 ea2 ea3 idx_ready hot bond added relu seg accd",
               soft=ring_counts(1)) as (block, s, sb, ps):
        rows = sb("rows", [P, JG, G, P])
        ea = sb("ea", [P, JG, G, P])
        idxs = sb("idxs", [P, JG, G], I32)
        hot = sb("hot", [P, 2, G, P])
        msg = sb("msg", [P, 2, G, P])
        w = sb("w", [P, P])
        bond, seg = ps("bond", [P, 2, 512]), ps("seg", [P, 2, 512])
        ea_in = [s["ea0"], s["ea1"], s["ea2"], s["ea3"]]
        gat = [s["gat0"], s["gat1"], s["gat2"], s["gat3"]]
        blk = block()

        @blk.sync
        def _(sp):
            sp.dma_start(w[:, :], t["L0_gnn_W_bond"]).then_inc(s["w"], 16)

            def load(g, q, tiles):
                await_(sp, s, s["bond"], g + 1)
                for u in range(G):
                    sp.dma_start(ea[:, q, u, :], t["edge_t"][ds(tiles[u], 1), :, :].rearrange("a f e -> (a f) e")
                                 ).then_inc(ea_in[q], 16)

            tiles, _ = load_registers(sp, k.tilerow[0:1, 0:G], f"t0_{layer}", 0, TILES - 1)
            load(0, 0, tiles)
            with sp.Fori(0, ROUNDS) as r:
                tiles, _ = load_registers(sp, k.tilerow[0:1, ds(r * UNROLL + G, UNROLL)], f"t_{layer}", 0, TILES - 1)
                for j in range(JG):
                    load(r * JG + j + 1, (j + 1) % JG, tiles[j * G:(j + 1) * G])

        @blk.gpsimd
        def _(pool):
            gather_ring(nc, s, pool, k, idxs, rows, k.table, 1, D)

        @blk.tensor
        def _(pe):
            def edge_product(r, g, j):
                d = j % 2
                await_(pe, s, ea_in[j % JG], (r + j // JG) * 64 + 64)
                await_(pe, s, s["added"], g + 1)
                for u in range(G):
                    ins = nc.tensor.matmul(bond[:, d, u * P:(u + 1) * P], ea[:, j % JG, u, :], w[:, :],
                                           start=True, stop=True)
                ins.then_inc(s["bond"], 1)

            def segment_sums(g, j):
                d = j % 2
                await_(pe, s, s["hot"], g + 1)
                await_(pe, s, s["relu"], g + 1)
                await_(pe, s, s["accd"], g * G + G)
                for u in range(G):
                    ins = nc.tensor.matmul(seg[:, d, u * P:(u + 1) * P], hot[:, d, u, :], msg[:, d, u, :],
                                           start=True, stop=True)
                ins.then_inc(s["seg"], 1)

            pe.sem_inc(s["bond"], JG)
            pe.sem_inc(s["seg"], 2)
            pe.wait_ge(s["w"], 16)
            edge_product(0, 0, 0)
            with pe.Fori(0, ROUNDS) as r:
                for j in range(JG):
                    g = r * JG + j
                    edge_product(r, g + 1, j + 1)
                    segment_sums(g, j)

        @blk.scalar
        def _(act):
            def relu(g, j):
                await_(act, s, s["added"], g + 3)
                nc.scalar.activation(msg[:, j % 2], msg[:, j % 2], ACT.Relu).then_inc(s["relu"], 1)
                refill(nc, s, k, act, idxs, g + JG, j % JG)

            for m in range(JG):
                refill(nc, s, k, act, idxs, m, m)
            relu(0, 0)
            with act.Fori(0, ROUNDS) as r:
                for j in range(JG):
                    relu(r * JG + j + 1, j + 1)

        @blk.vector
        def _(dve):
            def messages(r, g, j):
                d = j % 2
                await_(dve, s, s["seg"], g + 1)
                nc.vector.tensor_tensor(hot[:, d], across(k.iota[:, :], G), along(k.loc[:, ds(g * G, G)], P),
                                        ALU.is_equal).then_inc(s["hot"], 1)
                await_(dve, s, s["bond"], g + JG + 1)
                await_(dve, s, gat[j % JG], (r + j // JG) * 64 + 64)
                nc.vector.tensor_tensor(msg[:, d], rows[:, j % JG], bond[:, d].rearrange("p (u f) -> p u f", f=P),
                                        ALU.add).then_inc(s["added"], 1)

            dve.sem_inc(s["added"], 2)
            dve.sem_inc(s["accd"], 2 * G)
            messages(0, 0, 0)
            with dve.Fori(0, ROUNDS) as r:
                where, _ = load_registers(dve, k.blockrow[0:1, ds(r * UNROLL, UNROLL)], f"b_{layer}", 0, BLOCKS - 1)
                for j in range(JG):
                    g = r * JG + j
                    messages(r, g + 1, j + 1)
                    accumulate(nc, s, dve, k, seg[:, j % 2], g, where[j * G:(j + 1) * G], D,
                               [u * P for u in range(G)])
            dve.wait_ge(s["accd"], STEPS + 2 * G)


def accumulate(nc, s, dve, k, seg, g, where, width, at, credits=2):
    await_(dve, s, s["seg"], g + 1 + credits)
    for u in range(G):
        a = k.acc[:, ds(where[u] * W, width)]
        dve.wait_ge(s["accd"], g * G + u + 2 * G)
        nc.vector.tensor_tensor(a, a, seg[:, at[u]:at[u] + width], ALU.add).then_inc(s["accd"], 1)


def bank_at(width):
    return [(u // 2) * 512 + (u % 2) * 256 for u in range(G)]


def edges_mean(nc, k):
    with phase(nc, "mean", "idx_ready hot seg accd one", soft=ring_counts(1)) as (block, s, sb, ps):
        rows = sb("rows", [P, JG, G, W])
        idxs = sb("idxs", [P, JG, G], I32)
        hot = sb("hot", [P, 2, G, P])
        seg = ps("seg", [P, 2, 1024])
        gat = [s["gat0"], s["gat1"], s["gat2"], s["gat3"]]
        at = bank_at(P + 1)
        blk = block()

        @blk.gpsimd
        def _(pool):
            gather_ring(nc, s, pool, k, idxs, rows, k.table, 1, D)

        @blk.tensor
        def _(pe):
            pe.sem_inc(s["seg"], 2)
            pe.wait_ge(s["one"], 1)
            with pe.Fori(0, ROUNDS) as r:
                for j in range(JG):
                    g, d = r * JG + j, j % 2
                    await_(pe, s, gat[j], r * 64 + 64)
                    await_(pe, s, s["hot"], g + 1)
                    await_(pe, s, s["accd"], g * G + G)
                    for u in range(G):
                        ins = nc.tensor.matmul(seg[:, d, at[u]:at[u] + P + 1], hot[:, d, u, :],
                                               rows[:, j, u, 0:P + 1], start=True, stop=True)
                    ins.then_inc(s["seg"], 1)

        @blk.scalar
        def _(act):
            for m in range(JG):
                refill(nc, s, k, act, idxs, m, m)
            with act.Fori(0, ROUNDS) as r:
                for j in range(JG):
                    g = r * JG + j
                    await_(act, s, s["seg"], g + 3)
                    refill(nc, s, k, act, idxs, g + JG, j)

        @blk.vector
        def _(dve):
            def one_hot(g, j):
                await_(dve, s, s["seg"], g + 1)
                nc.vector.tensor_tensor(hot[:, j % 2], across(k.iota[:, :], G), along(k.loc[:, ds(g * G, G)], P),
                                        ALU.is_equal).then_inc(s["hot"], 1)

            nc.vector.memset(rows[:, :, :, P:P + 1], 1.0).then_inc(s["one"], 1)
            dve.sem_inc(s["accd"], 2 * G)
            one_hot(0, 0)
            with dve.Fori(0, ROUNDS) as r:
                where, _ = load_registers(dve, k.blockrow[0:1, ds(r * UNROLL, UNROLL)], "b_mean", 0, BLOCKS - 1)
                for j in range(JG):
                    g = r * JG + j
                    one_hot(g + 1, j + 1)
                    accumulate(nc, s, dve, k, seg[:, j % 2], g, where[j * G:(j + 1) * G], P + 1, at)
            dve.wait_ge(s["accd"], STEPS + 2 * G)


def node_mean(nc, k, t):
    with phase(nc, "nmean", "w wa var std hn turned copied prod v stored used done staged deg tab_in "
               "moved row top", soft={"x_in": 16 * NR}) as (block, s, sb, ps):
        x, c, sq, h = (sb(n, [P, NB, P]) for n in ("x", "c", "sq", "h"))
        st = sb("st", [P, 4, NB])
        hT = sb("hT", [P, NB * P])
        tabg = sb("tabg", [P, NB, W])
        res = sb("res", [P, NB, P])
        wl, wrp = sb("wl", [P, P]), sb("wrp", [P, P])
        wcat = sb("wcat", [P, P + 2 * HEADS])
        av = sb("av", [P, 2, P])
        prodw = sb("prodw", [P, 2, P])
        rdeg = sb("rdeg", [P, NB])
        ht = sb("ht", [P, BLOCKS, HEADS])
        padmask = sb("padmask", [P, 1])
        top = sb("top", [P, HEADS])
        topr = sb("topr", [HEADS, 2])
        diag = sb("diag", [HEADS, HEADS])
        topb = sb("topb", [P, HEADS])
        turned, prod = ps("turned", [P, 2, 512]), ps("prod", [P, 2, 512])
        big = ps("big", [P, 3, 512])
        small = ps("small", [P, 512])
        blk = block()
        PER = 3 + LN_VECTOR + 1

        @blk.sync
        def _(sp):
            sp.dma_start(wl[:, :], t["L1_gnn_W_l"]).then_inc(s["w"], 16)
            sp.dma_start(wrp[:, :], t["L2_gnn_residual_projection"]).then_inc(s["w"], 16)
            sp.dma_start(wcat[:, 0:P], t["L2_gnn_W"]).then_inc(s["w"], 16)
            for n, a in enumerate((t["L2_gnn_A_right"], t["L2_gnn_A_left"])):
                sp.dma_start(av[:, n, :], row_vector(a.rearrange("h d a -> (h d a)"))).then_inc(s["w"], 16)
            with sp.Fori(0, NR) as i:
                await_(sp, s, s["hn"], i + 1)
                sp.dma_start(rows_of(k.x_dram, i), x[:, :, :]).then_inc(s["stored"], 16)
                await_(sp, s, s["done"], 3 * i + 3)
                sp.dma_start(rows_of(k.table_gat, i), tabg[:, :, :]).then_inc(s["stored"], 16)
                sp.dma_start(rows_of(k.res_dram, i), res[:, :, :]).then_inc(s["stored"], 16)
                await_(sp, s, s["stored"], 48 * i + 48)
                sp.sem_inc(s["used"], 1)
            sp.wait_ge(s["moved"], 1)
            sp.dma_start(k.table_gat[(BLOCKS - 1) * P:NP, D:W], ht[:, BLOCKS - 1, :]).then_inc(s["stored"], 16)
            sp.wait_ge(s["stored"], 48 * NR + 16)

        @blk.gpsimd
        def _(pool):
            with pool.Fori(0, NR) as i:
                await_(pool, s, s["used"], i + 1)
                pool.dma_start(x[:, :, :], rows_of(k.x_dram, i)).then_inc(s["x_in"].sem, 16)

        @blk.vector
        def _(dve):
            step = [0]

            def once(ins):
                step[0] += 1
                ins.then_inc(s["wa"], 1)
                dve.wait_ge(s["wa"], step[0])

            dve.wait_ge(s["w"], 80)
            for n in range(2):
                once(nc.vector.tensor_tensor(prodw[:, n, :], wcat[:, 0:P], av[:, n, :], ALU.mult))
                once(nc.vector.tensor_reduce(wcat[:, P + n * HEADS:P + (n + 1) * HEADS],
                                             prodw[:, n, :].rearrange("p (h d) -> p h d", d=HD), AX, ALU.add))
            once(nc.vector.tensor_scalar(padmask[:, :], k.step_f[:, 0:1], float(LAST_ROWS), -1e30, ALU.is_ge, ALU.mult))
            with dve.Fori(0, NR) as i:
                then = Chain(dve, s, s["v"], i, PER)
                nc.vector.tensor_copy(k.deg[:, ds(i * NB, NB)], acc_rows(k, i, 1, P).rearrange("p b a -> p (b a)")
                                      ).then_inc(s["deg"], 1)
                then(nc.vector.tensor_scalar(rdeg[:, :], acc_rows(k, i, 1, P).rearrange("p b a -> p (b a)"), 1.0, None,
                                             ALU.max))
                then(nc.vector.reciprocal(rdeg[:, :], rdeg[:, :]))
                nc.vector.tensor_tensor(h[:, :, :], acc_rows(k, i), along(rdeg[:, :], P), ALU.mult).then_inc(s["staged"], 1)
                await_(dve, s, s["x_in"], 16 * i + 16)
                await_(dve, s, s["prod"], 2 * i + 1)
                then(nc.vector.tensor_tensor(x[:, :, :], x[:, :, :], blocks(flat(prod[:, :, :])[:, 0:NB * P]), ALU.add))
                layer_norm_relu(nc, s, dve, then, i, x[:, :, :], c[:, :, :], sq[:, :, :], st, h[:, :, :])
                dve.sem_inc(s["hn"], 1)
                await_(dve, s, s["tab_in"], i + 1)
                then(nc.vector.tensor_copy(ht[:, ds(i * NB, NB), :], tabg[:, :, P:W]))
                dve.sem_inc(s["done"], 1)
                then.end()
            once(nc.vector.tensor_scalar(ht[:, BLOCKS - 1, :], ht[:, BLOCKS - 1, :], padmask[:, 0:1], None, ALU.add))
            dve.sem_inc(s["moved"], 1)
            nc.vector.tensor_reduce(top[:, :], ht[:, :, :].rearrange("p b h -> p h b"), AX, ALU.max).then_inc(s["top"], 1)
            dve.wait_ge(s["row"], 1)
            once(nc.vector.tensor_reduce(topr[:, 0:1], small[0:HEADS, 0:P], AX, ALU.max))
            nc.vector.tensor_scalar(diag[:, :], k.ident[0:HEADS, 0:HEADS], topr[:, 0:1], None, ALU.mult
                                    ).then_inc(s["top"], 1)
            dve.wait_ge(s["row"], 2)
            once(nc.vector.tensor_copy(topb[:, :], small[:, P:P + HEADS]))
            dve.wait_ge(s["done"], 3 * NR)
            dve.wait_ge(s["stored"], 48 * NR + 16)
            once(nc.vector.tensor_tensor(ht[:, :, :], k.hsn[:, :, 0:HEADS], across(topb[:, :], BLOCKS), ALU.add))
            nc.vector.memset(k.acc[:, :], 0.0).then_inc(s["top"], 1)
            once(nc.vector.scalar_tensor_tensor(k.hsn[:, :, HEADS:], ht[:, :, :], 0.2, ht[:, :, :], ALU.mult, ALU.max))
            once(nc.vector.memset(k.smax[:, :], -1e30))
            dve.wait_ge(s["top"], 3)

        @blk.scalar
        def _(act):
            act.sem_inc(s["used"], 1)
            with act.Fori(0, NR) as i:
                await_(act, s, s["turned"], 2 * i + 1)
                nc.scalar.copy(hT[:, :], flat(turned[:, :, :])[:, 0:NB * P]).then_inc(s["copied"], 1)
                layer_norm_std(nc, s, act, i, st)
                await_(act, s, s["turned"], 2 * i + 2)
                nc.scalar.copy(hT[:, :], flat(turned[:, :, :])[:, 0:NB * P]).then_inc(s["copied"], 1)
                await_(act, s, s["prod"], 2 * i + 2)
                await_(act, s, s["used"], i + 1)
                nc.scalar.copy(tabg[:, 0:6, :].rearrange("p (q r) c -> p q r c", r=3),
                               big[:, 0:2, 0:3 * (P + 8)].rearrange("p q (r c) -> p q r c", r=3)[:, :, :, 0:W])
                nc.scalar.copy(tabg[:, 6:7, :], big[:, 2:3, 0:W]).then_inc(s["tab_in"], 1)
                nc.scalar.copy(k.hsn[:, ds(i * NB, NB), :][:, 0:6, 0:HEADS].rearrange("p (q r) h -> p q r h", r=3),
                               big[:, 0:2, 0:3 * (P + 8)].rearrange("p q (r c) -> p q r c", r=3)[:, :, :, W:W + HEADS])
                nc.scalar.copy(k.hsn[:, ds(i * NB + 6, 1), 0:HEADS], big[:, 2:3, W:W + HEADS]).then_inc(s["done"], 1)
                nc.scalar.copy(res[:, :, :], blocks(flat(prod[:, :, :])[:, 0:NB * P])).then_inc(s["done"], 1)

        @blk.tensor
        def _(pe):
            pe.wait_ge(s["w"], 80)
            pe.wait_ge(s["wa"], 5)
            tv, pv = flat(turned[:, :, :]), flat(prod[:, :, :])
            with pe.Fori(0, NR) as i:
                await_(pe, s, s["staged"], i + 1)
                for b in range(NB):
                    ins = nc.tensor.transpose(tv[:, b * P:(b + 1) * P], h[:, b, :], k.ident[:, :])
                ins.then_inc(s["turned"], 1)
                await_(pe, s, s["copied"], 2 * i + 1)
                for b in range(NB):
                    ins = nc.tensor.matmul(pv[:, b * P:(b + 1) * P], hT[:, b * P:(b + 1) * P], wl[:, :],
                                           start=True, stop=True)
                ins.then_inc(s["prod"], 1)
                await_(pe, s, s["hn"], i + 1)
                for b in range(NB):
                    ins = nc.tensor.transpose(tv[:, b * P:(b + 1) * P], h[:, b, :], k.ident[:, :])
                ins.then_inc(s["turned"], 1)
                await_(pe, s, s["copied"], 2 * i + 2)
                for b in range(NB):
                    nc.tensor.matmul(big[:, b // 3, b % 3 * (P + 8):(b % 3 + 1) * (P + 8)], hT[:, b * P:(b + 1) * P],
                                     wcat[:, :], start=True, stop=True)
                    ins = nc.tensor.matmul(pv[:, b * P:(b + 1) * P], hT[:, b * P:(b + 1) * P], wrp[:, :],
                                           start=True, stop=True)
                ins.then_inc(s["prod"], 1)
                await_(pe, s, s["done"], 3 * i + 3)
            pe.wait_ge(s["top"], 1)
            nc.tensor.transpose(small[0:HEADS, 0:P], top[:, :], k.ident[:, :]).then_inc(s["row"], 1)
            pe.wait_ge(s["top"], 2)
            nc.tensor.matmul(small[:, P:P + HEADS], k.ones[0:HEADS, :], diag[:, :], start=True, stop=True
                             ).then_inc(s["row"], 1)


def edges_gat(nc, k):
    with phase(nc, "gat", "idx_ready hot turned copied left sc score_step score exped scaled seg accd",
               soft=ring_counts(1)) as (block, s, sb, ps):
        rows = sb("rows", [P, JG, G, W])
        idxs = sb("idxs", [P, JG, G], I32)
        hot, hotT = sb("hot", [P, 4, G, P]), sb("hotT", [P, 2, G, P])
        t0, sc, ex = (sb(n, [P, 2, G, HEADS]) for n in ("t0", "sc", "ex"))
        part = sb("part", [P, 2, G, W])
        turned, left = ps("turned", [P, 2, 512]), ps("left", [P, 2, 512])
        seg = ps("seg", [P, 2, 1024])
        gat = [s["gat0"], s["gat1"], s["gat2"], s["gat3"]]
        at = bank_at(W)
        blk = block()

        @blk.gpsimd
        def _(pool):
            gather_ring(nc, s, pool, k, idxs, rows, k.table_gat, 1, W)

        @blk.tensor
        def _(pe):
            def turn(g, j):
                await_(pe, s, s["hot"], g + 1)
                await_(pe, s, s["copied"], g + 1)
                for u in range(G):
                    ins = nc.tensor.transpose(turned[:, j % 2, u * P:(u + 1) * P], hot[:, j % 4, u, :], k.ident[:, :])
                ins.then_inc(s["turned"], 1)

            def left_scores(g, j, where):
                await_(pe, s, s["copied"], g + 3)
                await_(pe, s, s["score"], g + 1)
                for u in range(G):
                    ins = nc.tensor.matmul(left[:, j % 2, u * 8:(u + 1) * 8], hotT[:, j % 2, u, :],
                                           k.hsn[:, ds(where[u], 1), :].rearrange("p b h -> p (b h)"),
                                           start=True, stop=True)
                ins.then_inc(s["left"], 1)

            def segment_sums(g, j):
                d = j % 2
                await_(pe, s, s["scaled"], g + 1)
                await_(pe, s, s["accd"], g * G + G)
                for u in range(G):
                    ins = nc.tensor.matmul(seg[:, d, at[u]:at[u] + W], hot[:, j % 4, u, :], part[:, d, u, :],
                                           start=True, stop=True)
                ins.then_inc(s["seg"], 1)

            pe.sem_inc(s["seg"], 4)
            where, _ = load_registers(pe, k.blockrow[0:1, 0:2 * G], "pb0", 0, BLOCKS - 1)
            turn(0, 0)
            turn(1, 1)
            left_scores(0, 0, where[0:G])
            turn(2, 2)
            left_scores(1, 1, where[G:2 * G])
            segment_sums(0, 0)
            with pe.Fori(0, ROUNDS) as r:
                where, _ = load_registers(pe, k.blockrow[0:1, ds(r * UNROLL + 2 * G, UNROLL)], "pb", 0, BLOCKS - 1)
                for j in range(JG):
                    g = r * JG + j
                    turn(g + 3, j + 3)
                    left_scores(g + 2, j + 2, where[j * G:(j + 1) * G])
                    segment_sums(g + 1, j + 1)

        @blk.scalar
        def _(act):
            def copy_turned(g, j):
                d = j % 2
                await_(act, s, s["turned"], g + 1)
                await_(act, s, s["left"], g + 1)
                nc.scalar.copy(hotT[:, d], turned[:, d].rearrange("p (u e) -> p u e", e=P)).then_inc(s["copied"], 1)

            def weights_of(g, j):
                d = j % 2
                await_(act, s, s["sc"], g + 1)
                await_(act, s, s["seg"], g + 3)
                nc.scalar.activation(part[:, d, :, P:W], ex[:, d], ACT.Exp).then_inc(s["exped"], 1)

            def next_indices(g, j):
                await_(act, s, s["scaled"], g + 1)
                refill(nc, s, k, act, idxs, g + JG, j % JG)

            act.sem_inc(s["copied"], 2)
            act.sem_inc(s["left"], 2)
            for m in range(JG):
                refill(nc, s, k, act, idxs, m, m)
            for m in range(3):
                copy_turned(m, m)
            weights_of(0, 0)
            next_indices(0, 0)
            with act.Fori(0, ROUNDS) as r:
                for j in range(JG):
                    g = r * JG + j
                    copy_turned(g + 3, j + 3)
                    weights_of(g + 1, j + 1)
                    next_indices(g + 1, j + 1)

        @blk.vector
        def _(dve):
            def one_hot(g, j):
                await_(dve, s, s["seg"], g + 1)
                nc.vector.tensor_tensor(hot[:, j % 4], across(k.iota[:, :], G), along(k.loc[:, ds(g * G, G)], P),
                                        ALU.is_equal).then_inc(s["hot"], 1)

            def scores(r, g, j):
                d = j % 2
                lv = left[:, d, 0:G * 8].rearrange("p (u c) -> p u c", c=8)
                await_(dve, s, s["left"], g + 3)
                await_(dve, s, gat[j % JG], (r + j // JG) * 64 + 64)
                nc.vector.tensor_tensor(t0[:, d], rows[:, j % JG, :, P:W], lv[:, :, 0:HEADS], ALU.add
                                        ).then_inc(s["score_step"], 1)
                await_(dve, s, s["score_step"], 2 * g + 1)
                nc.vector.scalar_tensor_tensor(sc[:, d], t0[:, d], 0.2, t0[:, d], ALU.mult, ALU.max
                                               ).then_inc(s["score_step"], 1)
                await_(dve, s, s["score_step"], 2 * g + 2)
                nc.vector.tensor_tensor(ex[:, d], sc[:, d], lv[:, :, HEADS:8], ALU.subtract).then_inc(s["sc"], 1)
                await_(dve, s, s["score"], g + 2)
                nc.vector.tensor_tensor(k.smax[:, :], k.smax[:, :], sc[:, d].rearrange("p u h -> p (u h)"), ALU.max
                                        ).then_inc(s["score"], 1)

            def scale(g, j):
                await_(dve, s, s["exped"], g + 1)
                hv = rows[:, j % JG, :, 0:P].rearrange("p u (h c) -> p u h c", c=HD)
                ov = part[:, j % 2, :, 0:P].rearrange("p u (h c) -> p u h c", c=HD)
                wv = part[:, j % 2, :, P:W].unsqueeze(3).to_broadcast([P, G, HEADS, HD])
                nc.vector.tensor_tensor(ov, hv, wv, ALU.mult).then_inc(s["scaled"], 1)

            dve.sem_inc(s["score"], 2)
            dve.sem_inc(s["accd"], 2 * G)
            for m in range(3):
                one_hot(m, m)
            scores(0, 0, 0)
            scale(0, 0)
            with dve.Fori(0, ROUNDS) as r:
                where, _ = load_registers(dve, k.blockrow[0:1, ds(r * UNROLL, UNROLL)], "b_gat", 0, BLOCKS - 1)
                for j in range(JG):
                    g = r * JG + j
                    one_hot(g + 3, j + 3)
                    scores(r, g + 1, j + 1)
                    accumulate(nc, s, dve, k, seg[:, j % 2], g, where[j * G:(j + 1) * G], W, at, 4)
                    scale(g + 1, j + 1)
            dve.wait_ge(s["accd"], STEPS + 2 * G)
            dve.wait_ge(s["score"], ROUNDS * JG + 3)


def node_gat(nc, k, t):
    with phase(nc, "ngat", "w once row top var std hn turned copied prod v stored used done right_read low "
               "expd", soft={"x_in": 32 * NR}) as (block, s, sb, ps):
        x, c, sq, h, res = (sb(n, [P, NB, P]) for n in ("x", "c", "sq", "h", "res"))
        st = sb("st", [P, 4, NB])
        hT = sb("hT", [P, NB * P])
        tab = sb("tab", [P, NB, P])
        wl, wr, att = sb("wl", [P, P]), sb("wr", [P, P]), sb("att", [P, P])
        e1, den = sb("e1", [P, NB, HEADS]), sb("den", [P, NB, HEADS])
        top = sb("top", [P, 1])
        topr = sb("topr", [1, 1])
        topb = sb("topb", [P, 1])
        turned, prod = ps("turned", [P, 2, 512]), ps("prod", [P, 2, 512])
        right = ps("right", [P, 2, 512])
        small = ps("small", [P, 512])
        blk = block()
        PER = 7 + LN_VECTOR + 4

        @blk.sync
        def _(sp):
            sp.dma_start(wl[:, :], t["L3_gnn_W_l"]).then_inc(s["w"], 16)
            sp.dma_start(wr[:, :], t["L3_gnn_W_r"]).then_inc(s["w"], 16)
            sp.dma_start(att[:, :], row_vector(t["L3_gnn_att"])).then_inc(s["w"], 16)
            with sp.Fori(0, NR) as i:
                await_(sp, s, s["hn"], i + 1)
                sp.dma_start(rows_of(k.x_dram, i), x[:, :, :]).then_inc(s["stored"], 16)
                await_(sp, s, s["done"], 2 * i + 2)
                sp.dma_start(rows_of(k.table, i), tab[:, :, :]).then_inc(s["stored"], 16)
                await_(sp, s, s["stored"], 32 * i + 32)
                sp.sem_inc(s["used"], 1)

        @blk.gpsimd
        def _(pool):
            with pool.Fori(0, NR) as i:
                await_(pool, s, s["used"], i + 1)
                pool.dma_start(x[:, :, :], rows_of(k.x_dram, i)).then_inc(s["x_in"].sem, 16)
                pool.dma_start(res[:, :, :], rows_of(k.res_dram, i)).then_inc(s["x_in"].sem, 16)
                await_(pool, s, s["x_in"], 32 * i + 32)

        @blk.vector
        def _(dve):
            step = [0]

            def once(ins):
                step[0] += 1
                ins.then_inc(s["once"], 1)
                dve.wait_ge(s["once"], step[0])

            dve.wait_ge(s["w"], 48)
            nc.vector.tensor_reduce(top[:, :], k.smax[:, :], AX, ALU.max).then_inc(s["top"], 1)
            dve.wait_ge(s["row"], 1)
            nc.vector.tensor_reduce(topr[:, :], small[0:1, 0:P], AX, ALU.max).then_inc(s["top"], 1)
            dve.wait_ge(s["row"], 2)
            once(nc.vector.tensor_copy(topb[:, :], small[:, P:P + 1]))
            with dve.Fori(0, NR) as i:
                then = Chain(dve, s, s["v"], i, PER)
                then(nc.vector.tensor_scalar(e1[:, :, :], k.hsn[:, ds(i * NB, NB), HEADS:8], -1.0, topb[:, 0:1],
                                             ALU.mult, ALU.add))
                nc.vector.tensor_scalar(e1[:, :, :], e1[:, :, :], 80.0, None, ALU.min).then_inc(s["low"], 1)
                await_(dve, s, s["expd"], 2 * i + 1)
                then(nc.vector.scalar_tensor_tensor(den[:, :, :], e1[:, :, :], 1e-8, acc_rows(k, i, HEADS, P),
                                                    ALU.mult, ALU.add))
                then(nc.vector.reciprocal(den[:, :, :], den[:, :, :]))
                then(nc.vector.tensor_tensor(c[:, :, :].rearrange("p b (h d) -> p b h d", d=HD),
                                             acc_rows(k, i).rearrange("p b (h d) -> p b h d", d=HD),
                                             den[:, :, :].unsqueeze(3).to_broadcast([P, NB, HEADS, HD]), ALU.mult))
                await_(dve, s, s["x_in"], 32 * i + 32)
                then(nc.vector.tensor_tensor(c[:, :, :], c[:, :, :], res[:, :, :], ALU.add))
                nc.vector.tensor_scalar(sq[:, :, :], c[:, :, :], 0.0, None, ALU.min).then_inc(s["low"], 1)
                then(nc.vector.scalar_tensor_tensor(x[:, :, :], c[:, :, :], 0.0, x[:, :, :], ALU.max, ALU.add))
                await_(dve, s, s["expd"], 2 * i + 2)
                then(nc.vector.scalar_tensor_tensor(x[:, :, :], sq[:, :, :], -1.0, x[:, :, :], ALU.add, ALU.add))
                layer_norm_relu(nc, s, dve, then, i, x[:, :, :], c[:, :, :], sq[:, :, :], st, h[:, :, :])
                dve.sem_inc(s["hn"], 1)
                await_(dve, s, s["done"], 2 * i + 1)
                then(nc.vector.tensor_tensor(c[:, :, :], tab[:, :, :], blocks(flat(right[:, :, :])[:, 0:NB * P]),
                                             ALU.add))
                dve.sem_inc(s["right_read"], 1)
                then(nc.vector.scalar_tensor_tensor(sq[:, :, :], c[:, :, :], 0.2, c[:, :, :], ALU.mult, ALU.max))
                then(nc.vector.tensor_tensor(sq[:, :, :], sq[:, :, :], across(att[:, :], NB), ALU.mult))
                then(nc.vector.tensor_reduce(k.selfl[:, ds(i * NB, NB)], sq[:, :, :], AX, ALU.add))
                then.end()
            nc.vector.memset(k.acc[:, :], 0.0).then_inc(s["top"], 1)
            dve.wait_ge(s["top"], 3)

        @blk.scalar
        def _(act):
            act.sem_inc(s["used"], 1)
            with act.Fori(0, NR) as i:
                await_(act, s, s["low"], 2 * i + 1)
                nc.scalar.activation(e1[:, :, :], e1[:, :, :], ACT.Exp).then_inc(s["expd"], 1)
                await_(act, s, s["low"], 2 * i + 2)
                nc.scalar.activation(sq[:, :, :], sq[:, :, :], ACT.Exp).then_inc(s["expd"], 1)
                layer_norm_std(nc, s, act, i, st)
                await_(act, s, s["turned"], i + 1)
                nc.scalar.copy(hT[:, :], flat(turned[:, :, :])[:, 0:NB * P]).then_inc(s["copied"], 1)
                await_(act, s, s["prod"], i + 1)
                await_(act, s, s["used"], i + 1)
                nc.scalar.copy(tab[:, :, :], blocks(flat(prod[:, :, :])[:, 0:NB * P])).then_inc(s["done"], 1)
                await_(act, s, s["right_read"], i + 1)
                nc.scalar.copy(k.xr[:, ds(i * (NB * P), NB * P)], flat(right[:, :, :])[:, 0:NB * P]).then_inc(s["done"], 1)

        @blk.tensor
        def _(pe):
            pe.wait_ge(s["w"], 48)
            pe.wait_ge(s["top"], 1)
            nc.tensor.transpose(small[0:1, 0:P], top[:, :], k.ident[:, :]).then_inc(s["row"], 1)
            pe.wait_ge(s["top"], 2)
            nc.tensor.matmul(small[:, P:P + 1], k.ones[0:1, :], topr[:, :], start=True, stop=True).then_inc(s["row"], 1)
            tv, pv, rv = (flat(a[:, :, :]) for a in (turned, prod, right))
            with pe.Fori(0, NR) as i:
                await_(pe, s, s["hn"], i + 1)
                for b in range(NB):
                    ins = nc.tensor.transpose(tv[:, b * P:(b + 1) * P], h[:, b, :], k.ident[:, :])
                ins.then_inc(s["turned"], 1)
                await_(pe, s, s["copied"], i + 1)
                for b in range(NB):
                    nc.tensor.matmul(pv[:, b * P:(b + 1) * P], hT[:, b * P:(b + 1) * P], wl[:, :],
                                     start=True, stop=True)
                    ins = nc.tensor.matmul(rv[:, b * P:(b + 1) * P], hT[:, b * P:(b + 1) * P], wr[:, :],
                                           start=True, stop=True)
                ins.then_inc(s["prod"], 1)
                await_(pe, s, s["done"], 2 * i + 2)


def edges_logits(nc, k, t):
    with phase(nc, "logit", "w st0 st1 st2 st3 idx_ready hot turned copied mm moved leaky dots "
               "sums d", soft=ring_counts(1)) as (block, s, sb, ps):
        rows = sb("rows", [P, JG, G, P])
        idxs = sb("idxs", [P, JG, G], I32)
        hot, hotT = sb("hot", [P, 4, G, P]), sb("hotT", [P, 2, G, P])
        m, lk = sb("m", [P, 2, G, P]), sb("lk", [P, 2, G, P])
        lg = sb("lg", [P, 2, G])
        att = sb("att", [P, P])
        turned, mm, own = ps("turned", [P, 2, 512]), ps("mm", [P, 2, 512]), ps("own", [P, 2, 512])
        gat = [s["gat0"], s["gat1"], s["gat2"], s["gat3"]]
        sto = [s["st0"], s["st1"], s["st2"], s["st3"]]
        blk = block()

        @blk.sync
        def _(sp):
            sp.dma_start(att[:, :], row_vector(t["L3_gnn_att"])).then_inc(s["w"], 16)

            def store(r, g, j):
                await_(sp, s, gat[j], r * 64 + 64)
                sp.dma_start(k.rows_dram[ds(g, 1), :, :].rearrange("a p f -> (a p) f"),
                             rows[:, j].rearrange("p u f -> p (u f)")).then_inc(sto[j], 16)

            with sp.Fori(0, ROUNDS) as r:
                for j in range(JG):
                    store(r, r * JG + j, j)
            store(ROUNDS, ROUNDS * JG, 0)
            for j in range(JG):
                sp.wait_ge(sto[j], 16 * (ROUNDS + (1 if j == 0 else 0)))

        @blk.gpsimd
        def _(pool):
            gather_ring(nc, s, pool, k, idxs, rows, k.table, 1, D)

        @blk.tensor
        def _(pe):
            def turn(g, j):
                await_(pe, s, s["hot"], g + 1)
                await_(pe, s, s["copied"], g + 1)
                for u in range(G):
                    ins = nc.tensor.transpose(turned[:, j % 2, u * P:(u + 1) * P], hot[:, j % 4, u, :], k.ident[:, :])
                ins.then_inc(s["turned"], 1)

            def sides(r, g, j, where):
                d = j % 2
                await_(pe, s, s["copied"], g + 3)
                await_(pe, s, s["d"], g + 1)
                await_(pe, s, gat[j % JG], (r + j // JG) * 64 + 64)
                for u in range(G):
                    o = mm[:, d, u * P:(u + 1) * P]
                    nc.tensor.matmul(o, hotT[:, d, u, :], k.xr[:, ds(where[u] * P, P)], start=True, stop=False)
                    nc.tensor.matmul(o, k.ident[:, :], rows[:, j % JG, u, :], start=False, stop=True)
                    ins = nc.tensor.matmul(own[:, d, u:u + 1], hotT[:, d, u, :], k.selfl[:, ds(where[u], 1)],
                                           start=True, stop=True)
                ins.then_inc(s["mm"], 1)

            pe.sem_inc(s["turned"], 4)
            where, _ = load_registers(pe, k.blockrow[0:1, 0:G], "lb0", 0, BLOCKS - 1)
            turn(0, 0)
            turn(1, 1)
            sides(0, 0, 0, where)
            with pe.Fori(0, ROUNDS) as r:
                where, _ = load_registers(pe, k.blockrow[0:1, ds(r * UNROLL + G, UNROLL)], "lb", 0, BLOCKS - 1)
                for j in range(JG):
                    g = r * JG + j
                    turn(g + 2, j + 2)
                    sides(r, g + 1, j + 1, where[j * G:(j + 1) * G])

        @blk.scalar
        def _(act):
            def copy_turned(g, j):
                d = j % 2
                await_(act, s, s["turned"], g + 5)
                await_(act, s, s["mm"], g + 1)
                nc.scalar.copy(hotT[:, d], turned[:, d].rearrange("p (u e) -> p u e", e=P)).then_inc(s["copied"], 1)

            def move(r, g, j):
                d = j % 2
                await_(act, s, s["mm"], g + 3)
                await_(act, s, s["leaky"], g + 1)
                nc.scalar.copy(m[:, d], mm[:, d].rearrange("p (u f) -> p u f", f=P)).then_inc(s["moved"], 1)
                await_(act, s, sto[j % JG], (r + j // JG) * 16 + 16)
                refill(nc, s, k, act, idxs, g + JG, j % JG)

            act.sem_inc(s["copied"], 2)
            act.sem_inc(s["mm"], 2)
            act.sem_inc(s["leaky"], 2)
            for q in range(JG):
                refill(nc, s, k, act, idxs, q, q)
            copy_turned(0, 0)
            copy_turned(1, 1)
            move(0, 0, 0)
            with act.Fori(0, ROUNDS) as r:
                for j in range(JG):
                    g = r * JG + j
                    copy_turned(g + 2, j + 2)
                    move(r, g + 1, j + 1)

        @blk.vector
        def _(dve):
            def one_hot(g, j):
                await_(dve, s, s["turned"], g + 1)
                nc.vector.tensor_tensor(hot[:, j % 4], across(k.iota[:, :], G), along(k.loc[:, ds(g * G, G)], P),
                                        ALU.is_equal).then_inc(s["hot"], 1)

            def logits(g, j):
                d = j % 2
                await_(dve, s, s["moved"], g + 1)
                nc.vector.scalar_tensor_tensor(lk[:, d], m[:, d], 0.2, m[:, d], ALU.mult, ALU.max).then_inc(s["leaky"], 1)
                await_(dve, s, s["leaky"], g + 3)
                nc.vector.tensor_tensor(lk[:, d], lk[:, d], across(att[:, :], G), ALU.mult).then_inc(s["dots"], 1)
                await_(dve, s, s["dots"], g + 1)
                nc.vector.tensor_reduce(lg[:, d], lk[:, d], AX, ALU.add).then_inc(s["sums"], 1)
                await_(dve, s, s["sums"], g + 1)
                nc.vector.tensor_tensor(k.dlog[:, ds(g * G, G)], lg[:, d], own[:, d, 0:G], ALU.subtract
                                        ).then_inc(s["d"], 1)

            dve.sem_inc(s["d"], 2)
            dve.wait_ge(s["w"], 16)
            for q in range(3):
                one_hot(q, q)
            with dve.Fori(0, ROUNDS) as r:
                for j in range(JG):
                    g = r * JG + j
                    one_hot(g + 3, j + 3)
                    logits(g, j)
            dve.wait_ge(s["d"], ROUNDS * JG + 2)


def segment_maxima(nc, k):
    with phase(nc, "segmax", "v turned moved line keys back seg got ret exped row carry neg") as (block, s, sb, ps):
        d, valid, fwd, bwd = (k.xr[:, n * STEPS:(n + 1) * STEPS] for n in range(4))
        lines = k.xr[:, 4 * STEPS:5 * STEPS].rearrange("p (i e) -> p i e", e=P)
        same = k.xr[:, 5 * STEPS:7 * STEPS].rearrange("p (n c) -> p n c", n=2)
        key = sb("key", [P, 3, STEPS], I32)
        ab = sb("ab", [P, 2])
        abr = sb("abr", [1, 2, P])
        srow = sb("srow", [1, P + 2])
        carry = sb("carry", [P, 1])
        turned = ps("turned", [P, 2, 512])
        small = ps("small", [P, 512])
        small2 = ps("small2", [P, 512])
        blk = block()

        @blk.sync
        def _(sp):
            for n in range(3):
                sp.dma_start(key[:, n, :], k.key_dram[n:n + STEPS * P].rearrange("(q c) -> q c", q=P)
                             ).then_inc(s["keys"], 16)
            sp.wait_ge(s["moved"], KT)
            sp.dma_start(k.line_dram.rearrange("(i p e) -> p i e", p=P, e=P), lines[:, :, :]).then_inc(s["line"], 16)
            sp.wait_ge(s["line"], 16)
            sp.dma_start(d[:, :], k.line_dram.rearrange("(q c) -> q c", q=P)).then_inc(s["back"], 16)
            sp.wait_ge(s["seg"], 1)
            sp.dma_start(k.seg_dram.rearrange("(q c) -> q c", q=P), bwd[:, :]).then_inc(s["got"], 16)
            sp.wait_ge(s["got"], 16)
            sp.dma_start(lines[:, :, :], k.seg_dram.rearrange("(i p e) -> p i e", p=P, e=P)).then_inc(s["ret"], 16)
            sp.wait_ge(s["ret"], 16)

        @blk.vector
        def _(dve):
            step = [0]

            def then(ins):
                step[0] += 1
                ins.then_inc(s["v"], 1)
                dve.wait_ge(s["v"], step[0])

            then(nc.vector.tensor_scalar(valid[:, :], k.loc[:, 0:STEPS], 0.0, None, ALU.is_ge))
            then(nc.vector.scalar_tensor_tensor(valid[:, :], k.loc[:, 0:STEPS], float(P - 1), valid[:, :],
                                                ALU.is_le, ALU.mult))
            then(nc.vector.scalar_tensor_tensor(d[:, :], k.dlog[:, 0:STEPS], 0.0, valid[:, :], ALU.max, ALU.mult))
            dve.wait_ge(s["keys"], 48)
            then(nc.vector.tensor_tensor(same[:, 0, :], key[:, 1, :], key[:, 0, :], ALU.is_equal))
            then(nc.vector.tensor_tensor(same[:, 1, :], key[:, 1, :], key[:, 2, :], ALU.is_equal))
            dve.wait_ge(s["back"], 16)
            for n, (data, out) in enumerate(((d, fwd), (fwd, bwd))):
                back = n == 1
                turn = (lambda a: a[:, ::-1]) if back else (lambda a: a)
                sm, da, ou = turn(same[:, n, :]), turn(data[:, :]), turn(out[:, :])
                then(nc.vector.tensor_tensor_scan(ou, sm, da, 0.0, ALU.mult, ALU.max))
                then(nc.vector.tensor_reduce(ab[:, 0:1], same[:, n, :], AX, ALU.min))
                end = out[:, 0:1] if back else out[:, STEPS - 1:STEPS]
                nc.vector.tensor_copy(ab[:, 1:2], end).then_inc(s["carry"], 1)
                dve.wait_ge(s["row"], 2 * n + 1)
                then(nc.vector.tensor_copy(abr[:, 0, :], small[0:1, 0:P]))
                then(nc.vector.tensor_copy(abr[:, 1, :], small[0:1, P:2 * P]))
                then(nc.vector.memset(srow[:, :], 0.0))
                then(nc.vector.tensor_tensor_scan(turn(srow[:, 1:P + 1]), turn(abr[:, 0, :]), turn(abr[:, 1, :]), 0.0,
                                                  ALU.mult, ALU.max))
                dve.sem_inc(s["carry"], 1)
                dve.wait_ge(s["row"], 2 * n + 2)
                then(nc.vector.tensor_copy(carry[:, :], small2[:, 0:1]))
                then(nc.vector.tensor_tensor_scan(ou, sm, da, carry[:, 0:1], ALU.mult, ALU.max))
            dve.sem_inc(s["seg"], 1)
            for i in range(KT):
                dve.wait_ge(s["turned"], KT + i + 1)
                nc.vector.tensor_copy(fwd[:, i * P:(i + 1) * P], turned[:, i % 2, 0:P]).then_inc(s["moved"], 1)
            dve.wait_ge(s["moved"], 2 * KT)
            then(nc.vector.tensor_tensor(d[:, :], k.dlog[:, 0:STEPS], fwd[:, :], ALU.subtract))
            then(nc.vector.tensor_scalar(d[:, :], d[:, :], 0.0, None, ALU.min))
            dve.sem_inc(s["neg"], 1)
            then(nc.vector.memset(k.we[:, STEPS:TW, :], 0.0))

        @blk.scalar
        def _(act):
            for i in range(KT):
                act.wait_ge(s["turned"], i + 1)
                nc.scalar.copy(lines[:, i, :], turned[:, i % 2, 0:P]).then_inc(s["moved"], 1)
            act.wait_ge(s["neg"], 1)
            nc.scalar.activation(k.we[:, 0:STEPS, 0], d[:, :], ACT.Exp).then_inc(s["exped"], 1)
            nc.scalar.activation(k.we[:, 0:STEPS, 1], fwd[:, :], ACT.Exp, scale=-1.0).then_inc(s["exped"], 1)
            act.wait_ge(s["exped"], 2)

        @blk.tensor
        def _(pe):
            pe.wait_ge(s["v"], 3)
            for i in range(KT):
                if i >= 2:
                    pe.wait_ge(s["moved"], i - 1)
                nc.tensor.transpose(turned[:, i % 2, 0:P], d[:, i * P:(i + 1) * P], k.ident[:, :]).then_inc(s["turned"], 1)
            for n in range(2):
                pe.wait_ge(s["carry"], 2 * n + 1)
                nc.tensor.transpose(small[0:1, 0:P], ab[:, 0:1], k.ident[:, :])
                nc.tensor.transpose(small[0:1, P:2 * P], ab[:, 1:2], k.ident[:, :]).then_inc(s["row"], 1)
                pe.wait_ge(s["carry"], 2 * n + 2)
                lo = 2 if n else 0
                nc.tensor.matmul(small2[:, 0:1], srow[:, lo:lo + P], k.ones[0:1, 0:1], start=True, stop=True
                                 ).then_inc(s["row"], 1)
            pe.wait_ge(s["ret"], 16)
            pe.wait_ge(s["moved"], KT)
            for i in range(KT):
                if i >= 2:
                    pe.wait_ge(s["moved"], KT + i - 1)
                nc.tensor.transpose(turned[:, i % 2, 0:P], lines[:, i, :], k.ident[:, :]).then_inc(s["turned"], 1)


def edges_sum(nc, k):
    with phase(nc, "wsum", "in0 in1 in2 in3 hot cols scaled seg accd") as (block, s, sb, ps):
        rows = sb("rows", [P, JG, G * P])
        x = sb("x", [P, 2, G, W])
        hot = sb("hot", [P, 2, G, P])
        seg = ps("seg", [P, 2, 1024])
        ins_ = [s["in0"], s["in1"], s["in2"], s["in3"]]
        at = bank_at(P + 2)
        blk = block()

        @blk.sync
        def _(sp):
            def load(g, j):
                await_(sp, s, s["scaled"], g + 1)
                sp.dma_start(rows[:, j % JG, :], k.rows_dram[ds(g, 1), :, :].rearrange("a p f -> (a p) f")
                             ).then_inc(ins_[j % JG], 16)

            load(0, 0)
            with sp.Fori(0, ROUNDS) as r:
                for j in range(JG):
                    load(r * JG + j + 1, j + 1)

        @blk.scalar
        def _(act):
            def scale(r, g, j):
                d = j % 2
                await_(act, s, ins_[j % JG], (r + j // JG) * 16 + 16)
                await_(act, s, s["seg"], g + 1)
                wv = k.we[:, ds(g * G, G), :]
                nc.scalar.copy(x[:, d, :, P:P + 2], wv).then_inc(s["cols"], 1)
                await_(act, s, s["cols"], g + 1)
                for u in range(G):
                    ins = nc.scalar.activation(x[:, d, u, 0:P], rows[:, j % JG, u * P:(u + 1) * P], ACT.Copy,
                                               scale=x[:, d, u, P:P + 1])
                ins.then_inc(s["scaled"], 1)

            act.sem_inc(s["scaled"], JG)
            scale(0, 0, 0)
            with act.Fori(0, ROUNDS) as r:
                for j in range(JG):
                    scale(r, r * JG + j + 1, j + 1)

        @blk.tensor
        def _(pe):
            pe.sem_inc(s["seg"], 2)
            with pe.Fori(0, ROUNDS) as r:
                for j in range(JG):
                    g, d = r * JG + j, j % 2
                    await_(pe, s, s["hot"], g + 1)
                    await_(pe, s, s["scaled"], g + JG + 1)
                    await_(pe, s, s["accd"], g * G + G)
                    for u in range(G):
                        ins = nc.tensor.matmul(seg[:, d, at[u]:at[u] + P + 2], hot[:, d, u, :], x[:, d, u, 0:P + 2],
                                               start=True, stop=True)
                    ins.then_inc(s["seg"], 1)

        @blk.vector
        def _(dve):
            def one_hot(g, j):
                await_(dve, s, s["seg"], g + 1)
                nc.vector.tensor_tensor(hot[:, j % 2], across(k.iota[:, :], G), along(k.loc[:, ds(g * G, G)], P),
                                        ALU.is_equal).then_inc(s["hot"], 1)

            dve.sem_inc(s["accd"], 2 * G)
            one_hot(0, 0)
            with dve.Fori(0, ROUNDS) as r:
                where, _ = load_registers(dve, k.blockrow[0:1, ds(r * UNROLL, UNROLL)], "b_sum", 0, BLOCKS - 1)
                for j in range(JG):
                    g = r * JG + j
                    one_hot(g + 1, j + 1)
                    accumulate(nc, s, dve, k, seg[:, j % 2], g, where[j * G:(j + 1) * G], P + 2, at)
            dve.wait_ge(s["accd"], STEPS + 2 * G)


def node_out(nc, k, t, out):
    with phase(nc, "nout", "w used v once tot row sqd sq_sum rooted stored dst_free done", soft={"x_in": 32 * NR}) as (block, s, sb, ps):
        xl, c = sb("xl", [P, NB, P]), sb("c", [P, NB, P])
        dst = sb("dst", [P, NB, P])
        col = sb("col", [P, 4, NB])
        bias, lnw, lnb = sb("bias", [P, P]), sb("lnw", [P, P]), sb("lnb", [P, P])
        real = sb("real", [P, 1])
        part = sb("part", [P, BLOCKS])
        tot = sb("tot", [P, 2])
        mu, std = sb("mu", [P, 1]), sb("std", [P, 3])
        small = ps("small", [P, 2, 512])
        blk = block()
        PER, PER2 = 12, 3
        accv = k.acc[:, :].rearrange("p (b w) -> p b w", w=W)[:, :, 0:P]

        @blk.sync
        def _(sp):
            sp.dma_start(bias[:, :], row_vector(t["L3_gnn_bias"])).then_inc(s["w"], 16)
            sp.dma_start(lnw[:, :], row_vector(t["L3_gnn_ln_w"])).then_inc(s["w"], 16)
            sp.dma_start(lnb[:, :], row_vector(t["L3_gnn_ln_b"])).then_inc(s["w"], 16)
            with sp.Fori(0, NR) as i:
                await_(sp, s, s["done"], i + 1)
                sp.dma_start(rows_of(out, i), dst[:, :, :]).then_inc(s["stored"], 16)
                await_(sp, s, s["stored"], 16 * i + 16)
                sp.sem_inc(s["dst_free"], 1)

        @blk.gpsimd
        def _(pool):
            pool.sem_inc(s["used"], 1)
            for n, src in enumerate((k.table, k.x_dram)):
                with pool.Fori(0, NR) as i:
                    await_(pool, s, s["used"], i + n * NR + 1)
                    pool.dma_start(xl[:, :, :], rows_of(src, i)).then_inc(s["x_in"].sem, 16)

        @blk.vector
        def _(dve):
            step = [0]

            def once(ins):
                step[0] += 1
                ins.then_inc(s["once"], 1)
                dve.wait_ge(s["once"], step[0])

            dve.wait_ge(s["w"], 48)
            once(nc.vector.tensor_scalar(real[:, :], k.step_f[:, 0:1], float(LAST_ROWS), None, ALU.is_lt))
            with dve.Fori(0, NR) as i:
                then = Chain(dve, s, s["v"], i, PER)
                deg = k.deg[:, ds(i * NB, NB)]
                one = lambda f: acc_rows(k, i, 1, f).rearrange("p b a -> p (b a)")
                then(nc.vector.tensor_scalar(col[:, 0, :], deg, 1.0, None, ALU.max))
                then(nc.vector.tensor_scalar(col[:, 1, :], deg, 0.0, None, ALU.is_equal))
                then(nc.vector.reciprocal(col[:, 0, :], col[:, 0, :]))
                then(nc.vector.tensor_tensor(col[:, 0, :], col[:, 0, :], one(P + 1), ALU.mult))
                then(nc.vector.tensor_tensor(col[:, 0, :], col[:, 0, :], col[:, 1, :], ALU.add))
                then(nc.vector.tensor_tensor(col[:, 2, :], col[:, 0, :], one(P), ALU.add))
                then(nc.vector.reciprocal(col[:, 2, :], col[:, 2, :]))
                await_(dve, s, s["x_in"], 16 * i + 16)
                then(nc.vector.tensor_tensor(c[:, :, :], xl[:, :, :], along(col[:, 0, :], P), ALU.mult))
                dve.sem_inc(s["used"], 1)
                then(nc.vector.tensor_tensor(c[:, :, :], c[:, :, :], acc_rows(k, i), ALU.add))
                then(nc.vector.tensor_tensor(c[:, :, :], c[:, :, :], along(col[:, 2, :], P), ALU.mult))
                then(nc.vector.tensor_tensor(c[:, :, :], c[:, :, :], across(bias[:, :], NB), ALU.add))
                then(nc.vector.scalar_tensor_tensor(acc_rows(k, i), c[:, :, :], 0.01, c[:, :, :], ALU.mult, ALU.max))
                then.end()
            lastb = accv[:, BLOCKS - 1, :]
            once(nc.vector.tensor_scalar(lastb, lastb, real[:, 0:1], None, ALU.mult))
            once(nc.vector.tensor_reduce(part[:, :], accv, AX, ALU.add))
            nc.vector.tensor_reduce(tot[:, 0:1], part[:, :], AX, ALU.add).then_inc(s["tot"], 1)
            dve.wait_ge(s["row"], 1)
            once(nc.vector.tensor_scalar(mu[:, :], small[:, 0, 0:1], 1.0 / (N * D), None, ALU.mult))
            once(nc.vector.tensor_scalar(accv, accv, mu[:, 0:1], None, ALU.subtract))
            once(nc.vector.tensor_scalar(lastb, lastb, real[:, 0:1], None, ALU.mult))
            dve.sem_inc(s["tot"], 1)
            dve.sem_inc(s["dst_free"], 1)
            dve.wait_ge(s["row"], 2)
            nc.vector.tensor_scalar(std[:, 0:1], small[:, 1, 0:1], 1.0 / (N * D), None, ALU.mult).then_inc(s["tot"], 1)
            dve.wait_ge(s["rooted"], 1)
            once(nc.vector.tensor_scalar(std[:, 2:3], std[:, 1:2], 1e-5, None, ALU.add))
            once(nc.vector.reciprocal(std[:, 2:3], std[:, 2:3]))
            once(nc.vector.tensor_scalar(lnw[:, :], lnw[:, :], std[:, 2:3], None, ALU.mult))
            with dve.Fori(0, NR) as i:
                then = Chain(dve, s, s["sqd"], i, PER2)
                then(nc.vector.tensor_tensor(c[:, :, :], acc_rows(k, i), across(lnw[:, :], NB), ALU.mult))
                then(nc.vector.tensor_tensor(c[:, :, :], c[:, :, :], across(lnb[:, :], NB), ALU.add))
                await_(dve, s, s["x_in"], 16 * i + 16 * NR + 16)
                await_(dve, s, s["dst_free"], i + 1)
                then(nc.vector.tensor_tensor(dst[:, :, :], c[:, :, :], xl[:, :, :], ALU.add))
                dve.sem_inc(s["used"], 1)
                dve.sem_inc(s["done"], 1)
                then.end()

        @blk.scalar
        def _(act):
            act.wait_ge(s["tot"], 2)
            nc.scalar.activation(k.xr[:, :].rearrange("p (b f) -> p b f", f=P), accv, ACT.Square, accum_out=tot[:, 1:2]).then_inc(s["sq_sum"], 1)
            act.wait_ge(s["tot"], 3)
            nc.scalar.activation(std[:, 1:2], std[:, 0:1], ACT.Sqrt).then_inc(s["rooted"], 1)

        @blk.tensor
        def _(pe):
            pe.wait_ge(s["tot"], 1)
            nc.tensor.matmul(small[:, 0, 0:1], k.ones[:, :], tot[:, 0:1], start=True, stop=True).then_inc(s["row"], 1)
            pe.wait_ge(s["sq_sum"], 1)
            nc.tensor.matmul(small[:, 1, 0:1], k.ones[:, :], tot[:, 1:2], start=True, stop=True).then_inc(s["row"], 1)


def move_tables(nc, k, name, to_dram, order):
    with phase(nc, name, "moved") as (block, s, sb, ps):
        idx, loc, row = k.tables_dram[order]
        blk = block()

        @blk.sync
        def _(sp):
            for a, b in ((idx, k.idx[:, :]), (loc, k.loc[:, :]), (row, k.blockrow[:, :])):
                if to_dram:
                    sp.dma_start(a, b).then_inc(s["moved"], 16)
                else:
                    sp.dma_start(b, a).then_inc(s["moved"], 16)
            sp.wait_ge(s["moved"], 48)


def layers(nc, k, t, out):
    node_input(nc, k, t)
    for layer in range(L):
        edges_gine(nc, k, t, layer)
        mlp(nc, k, t, layer)
    edges_mean(nc, k)
    def sb(name, shape):
        return nc.alloc_sbuf_tensor(name, shape, F32)

    k.hsn = sb("hsn", [P, BLOCKS, 2 * HEADS])
    k.smax = sb("smax", [P, G * HEADS])
    node_mean(nc, k, t)
    move_tables(nc, k, "load_s", False, 1)
    edges_gat(nc, k)
    k.xr = sb("xr", [P, NP])
    k.selfl = sb("selfl", [P, BLOCKS])
    node_gat(nc, k, t)
    move_tables(nc, k, "load_d", False, 0)
    k.dlog, k.we = sb("dlog", [P, TW]), sb("we", [P, TW, 2])
    edges_logits(nc, k, t)
    segment_maxima(nc, k)
    edges_sum(nc, k)
    node_out(nc, k, t, out)



_SMALL = ["L0_gnn_W_atom", "L0_gnn_b_atom", "L0_gnn_W_bond", "L0_gnn_b_bond", "L0_gnn_eps", "L0_gnn_W1", "L0_gnn_b1",
          "L0_gnn_g1", "L0_gnn_be1", "L0_gnn_W2", "L0_gnn_b2", "L0_gnn_gn", "L0_gnn_bet", "L0_gnn_W_out",
          "L0_gnn_b_out", "L1_gnn_W_l", "L1_gnn_b_l", "L1_gnn_W_r", "L2_gnn_W", "L2_gnn_A_left", "L2_gnn_A_right",
          "L2_gnn_residual_projection", "L3_gnn_W_l", "L3_gnn_W_r", "L3_gnn_att", "L3_gnn_bias", "L3_gnn_ln_w",
          "L3_gnn_ln_b"]


def kernel(**inputs):
    import numpy as np
    import concourse.bacc as bacc
    from concourse.bass_utils import run_bass_kernel_spmd as run

    nc = bacc.Bacc("TRN2", target_bir_lowering=False, num_devices=1)
    arrays = {
        "x": np.pad(np.asarray(inputs["x"]), ((0, NP - N), (0, 0))),
        "edge_t": np.ascontiguousarray(np.pad(np.asarray(inputs["edge_attr_128"]), ((0, TILES * P - E), (0, 0)))
                                       .reshape(TILES, P, D).transpose(0, 2, 1)),
    }
    for name, pad in (("src", PAD_SRC), ("dst", PAD_DST)):
        rows = np.pad(np.asarray(inputs[name]), (0, TPAD * P - E), constant_values=pad).reshape(TPAD, P)
        arrays[name + "_rows"] = rows
        arrays[name + "_cols"] = np.ascontiguousarray(rows.T)
    for name in _SMALL:
        arrays[name] = np.ascontiguousarray(inputs[name])
    t = {name: nc.dram_tensor("in_" + name, a.shape, mybir.dt.from_np(a.dtype), kind="ExternalInput").ap()
         for name, a in arrays.items()}
    out = nc.dram_tensor("out_0", (NP, D), F32, kind="ExternalOutput").ap()
    program(nc, t, out)
    r = run(nc, [{"in_" + name: a for name, a in arrays.items()}], core_ids=[0])
    return r.results[0]["out_0"][:N]
```

```python
from contextlib import ExitStack, contextmanager

import concourse.bass as bass
from concourse import mybir

P = 128
N, E, D = 12500, 200000, 128
BLOCKS = -(-N // P)
NP = BLOCKS * P
TILES = -(-E // P)
UNROLL = 16
ROUNDS = -(-(TILES + BLOCKS - 1) // UNROLL)
STEPS = ROUNDS * UNROLL
G = 4
JG = UNROLL // G
TW = STEPS + 2 * UNROLL
KT = STEPS // P
SORT_ROUNDS = -(-TILES // UNROLL)
TPAD = SORT_ROUNDS * UNROLL
PAD_SRC = NP
PAD_DST = 20000
LAST_ROWS = N - (BLOCKS - 1) * P
W = 132
NB = 7
NR = BLOCKS // NB
L = 3
HID = 256
HEADS = 4
HD = 32
BN_EPS = 1e-5
LN_EPS = 1e-5
REC = STEPS * P + (TPAD - TILES + 1) * P
RADIX = 256

ALU = mybir.AluOpType
ACT = mybir.ActivationFunctionType
F32 = mybir.dt.float32
I32 = mybir.dt.int32
AX = mybir.AxisListType.X
ds = bass.ds


class Kept:
    pass


class Soft:

    def __init__(self, sem):
        self.sem, self.base = sem, 0


SOFT = []


@contextmanager
def phase(nc, name, sems, soft=()):
    with ExitStack() as ctx:
        names = sems.split() + ["gate"]
        first = SOFT[-1].sem.num + 1
        handles = [nc.alloc_semaphore(f"{name}_{n}", num=first + i) for i, n in enumerate(names)]
        s = {**dict(zip(names, handles)), **dict(zip(dict(soft), SOFT))}

        def sb(n, shape, dt=F32):
            return ctx.enter_context(nc.sbuf_tensor(f"{name}_{n}", shape, dt))

        def ps(n, shape, dt=F32):
            return ctx.enter_context(nc.psum_tensor(f"{name}_{n}", shape, dt))

        with ExitStack() as inner:
            yield (lambda: inner.enter_context(nc.Block())), s, sb, ps
        nc.all_engine_barrier(sems_to_clear=range(first, first + len(names)))
        for c, total in zip(SOFT, dict(soft).values()):
            c.base += total
        for h in handles:
            nc.release_semaphore(h)


def await_(eng, s, sem, value):
    if isinstance(sem, Soft):
        sem, value = sem.sem, value + sem.base
    eng.wait_ge(sem, value)
    eng.sem_inc(s["gate"], 1)


def wait_soft(eng, soft, value):
    eng.wait_ge(soft.sem, soft.base + value)


def along(ap, n):
    return ap.unsqueeze(2).to_broadcast([ap.shape[0], ap.shape[1], n])


def across(ap, k):
    return ap.unsqueeze(1).to_broadcast([ap.shape[0], k, ap.shape[1]])


def load_registers(eng, row, name, lo, hi):
    n = row.shape[1]
    regs = [eng.alloc_register(f"{name}{j}") for j in range(n)]
    eng.load(regs, row)
    return [eng.snap(r, min_val=lo, max_val=hi) for r in regs], regs


def constants(nc, k):
    with phase(nc, "const", "zeroed iota ones") as (block, s, sb, ps):
        blk = block()

        @blk.gpsimd
        def _(pool):
            nc.gpsimd.memset(k.ident[:, :], 0.0).then_inc(s["zeroed"], 1)
            nc.gpsimd.memset(k.ones[:, :], 1.0).then_inc(s["zeroed"], 1)
            nc.gpsimd.iota(k.iota_i[:, :], pattern=[[1, P]], base=0, channel_multiplier=0).then_inc(s["zeroed"], 1)
            nc.gpsimd.iota(k.step_i[:, :], pattern=[[P, KT]], base=0, channel_multiplier=1).then_inc(s["zeroed"], 1)
            pool.wait_ge(s["zeroed"], 4)
            nc.gpsimd.affine_select(out=k.ident[:, :], in_=k.ident[:, :], compare_op=ALU.not_equal, fill=1.0,
                                    base=0, pattern=[[-1, P]], channel_multiplier=1).then_inc(s["iota"], 1)
            nc.gpsimd.affine_select(out=k.not_before[:, :], in_=k.ones[:, :], compare_op=ALU.is_ge, fill=0.0,
                                    base=0, pattern=[[-1, P]], channel_multiplier=1).then_inc(s["iota"], 1)
            pool.wait_ge(s["iota"], 2)

        @blk.vector
        def _(dve):
            nc.vector.memset(k.zeros[:, :], 0.0).then_inc(s["ones"], 1)
            dve.wait_ge(s["zeroed"], 4)
            nc.vector.tensor_copy(k.iota[:, :], k.iota_i[:, :]).then_inc(s["ones"], 1)
            nc.vector.tensor_copy(k.step_f[:, :], k.step_i[:, :]).then_inc(s["ones"], 1)
            dve.wait_ge(s["ones"], 3)


MINE = (BLOCKS + 1) // 2 + 1


def histogram(nc, k, name, cols_dram, tiled):
    with phase(nc, name, "keys cnt sums m rows row_in done scat_in half keysf signs") as (block, s, sb, ps):
        keys = sb("keys", [P, TPAD], I32)
        keysf = sb("keysf", [P, TPAD])
        junk, junk_a = sb("junk", [P, TPAD]), sb("junk_a", [P, TPAD])
        half, signs = sb("half", [P, BLOCKS + 1]), sb("signs", [P, BLOCKS + 1])
        thr = sb("thr", [P, BLOCKS + 1])
        cnt = k.below
        start = sb("start", [P, BLOCKS + 1])
        lo_i = sb("lo_i", [P, BLOCKS + 1], I32)
        hi_i = sb("hi_i", [P, BLOCKS + 1], I32)
        lo = sb("lo", [P, BLOCKS + 1])
        hi = sb("hi", [P, BLOCKS + 1])
        some = sb("some", [P, BLOCKS])
        ntile = sb("ntile", [P, BLOCKS])
        incl = sb("incl", [P, BLOCKS])
        first = sb("first", [P, BLOCKS])
        m = sb("m", [P, KT, BLOCKS])
        m2 = sb("m2", [P, KT, BLOCKS])
        count = sb("count", [P, KT])
        firstsel = sb("firstsel", [P, KT])
        tilesel = sb("tilesel", [P, KT])
        over = sb("over", [P, KT])
        blk_i = sb("blk_i", [P, KT], I32)
        tile_i = k.tile_i
        locbase = k.locbase
        sums = ps("sums", [P, 512])
        dve_steps = [0]
        blk = block()

        if tiled:
            @blk.gpsimd
            def _(pool):
                scatter = Scatter(nc, k, s, sb, pool)
                scatter.round(0, wait=False)
                scatter.round(1)
                with pool.Fori(2, SCATTER_HIST) as i:
                    scatter.round(i)
                scatter.end(SCATTER_HIST)

        @blk.sync
        def _(sp):
            sp.dma_start(keys[:, :], cols_dram).then_inc(s["keys"], 16)
            sp.wait_ge(s["rows"], 1)
            sp.dma_start(k.blk_dram.rearrange("(i p) -> p i", p=P), blk_i[:, :],
                         allow_slow_non_contiguous=True).then_inc(s["row_in"], 16)
            sp.wait_ge(s["row_in"], 16)
            if tiled:
                sp.dma_start(k.tile_dram.rearrange("(i p) -> p i", p=P), tile_i[:, :],
                             allow_slow_non_contiguous=True).then_inc(s["row_in"], 16)
                sp.wait_ge(s["row_in"], 32)
                sp.dma_start(k.tilerow[:, 0:STEPS], k.tile_dram.rearrange("(a c) -> a c", a=1)).then_inc(s["done"], 16)
            sp.dma_start(k.blockrow[:, 0:STEPS], k.blk_dram.rearrange("(a c) -> a c", a=1)).then_inc(s["done"], 16)
            sp.wait_ge(s["done"], 32 if tiled else 16)

        @blk.tensor
        def _(pe):
            pe.wait_ge(s["cnt"], MINE + 1)
            nc.tensor.matmul(sums[:, 0:BLOCKS + 1], k.ones[:, :], cnt[:, :], start=True, stop=True).then_inc(s["sums"], 1)

        @blk.scalar
        def _(act):
            act.wait_ge(s["half"], 1)
            act.wait_ge(s["keysf"], 1)
            for n, b in enumerate(range(MINE, BLOCKS + 1)):
                nc.scalar.activation(junk_a[:, :], keysf[:, :], ACT.Sign, bias=half[:, b:b + 1], scale=-1.0,
                                     accum_out=signs[:, b:b + 1]).then_inc(s["signs"], 1)
                act.wait_ge(s["signs"], n + 1)

        @blk.vector
        def _(dve):
            def then(ins):
                dve_steps[0] += 1
                ins.then_inc(s["m"], 1)
                dve.wait_ge(s["m"], dve_steps[0])

            then(nc.vector.tensor_scalar(thr[:, 0:BLOCKS + 1], k.iota[:, 0:BLOCKS + 1], float(P), None, ALU.mult))
            nc.vector.tensor_scalar(half[:, :], k.iota[:, 0:BLOCKS + 1], float(P), -0.5, ALU.mult, ALU.add
                                    ).then_inc(s["half"], 1)
            dve.wait_ge(s["keys"], 16)
            nc.vector.tensor_copy(keysf[:, :], keys[:, :]).then_inc(s["keysf"], 1)
            dve.wait_ge(s["keysf"], 1)
            for b in range(MINE):
                nc.vector.tensor_scalar(junk[:, :], keysf[:, :], thr[:, b:b + 1], 0.0, ALU.is_lt, ALU.add,
                                        accum_out=cnt[:, b:b + 1]).then_inc(s["cnt"], 1)
                dve.wait_ge(s["cnt"], b + 1)
            dve.wait_ge(s["signs"], BLOCKS + 1 - MINE)
            nc.vector.tensor_scalar(cnt[:, MINE:], signs[:, MINE:], 0.5, TPAD / 2, ALU.mult, ALU.add
                                    ).then_inc(s["cnt"], 1)
            dve.wait_ge(s["sums"], 1)
            then(nc.vector.tensor_copy(start[:, :], sums[:, 0:BLOCKS + 1]))
            if tiled:
                then(nc.vector.tensor_copy(lo_i[:, :], start[:, :]))
                then(nc.vector.tensor_scalar(hi[:, :], start[:, :], float(P - 1), None, ALU.add))
                then(nc.vector.tensor_copy(hi_i[:, :], hi[:, :]))
                then(nc.vector.tensor_scalar(lo_i[:, :], lo_i[:, :], 7, None, ALU.arith_shift_right))
                then(nc.vector.tensor_scalar(hi_i[:, :], hi_i[:, :], 7, None, ALU.arith_shift_right))
                then(nc.vector.tensor_copy(lo[:, :], lo_i[:, :]))
                then(nc.vector.tensor_copy(hi[:, :], hi_i[:, :]))
                then(nc.vector.tensor_tensor(some[:, :], start[:, 1:BLOCKS + 1], start[:, 0:BLOCKS], ALU.is_gt))
                then(nc.vector.tensor_tensor(ntile[:, :], hi[:, 1:BLOCKS + 1], lo[:, 0:BLOCKS], ALU.subtract))
                then(nc.vector.tensor_tensor(ntile[:, :], ntile[:, :], some[:, :], ALU.mult))
            else:
                then(nc.vector.tensor_tensor(hi[:, 0:BLOCKS], start[:, 1:BLOCKS + 1], start[:, 0:BLOCKS], ALU.subtract))
                then(nc.vector.tensor_scalar(hi[:, 0:BLOCKS], hi[:, 0:BLOCKS], float(P - 1), None, ALU.add))
                then(nc.vector.tensor_copy(hi_i[:, 0:BLOCKS], hi[:, 0:BLOCKS]))
                then(nc.vector.tensor_scalar(hi_i[:, 0:BLOCKS], hi_i[:, 0:BLOCKS], 7, None, ALU.arith_shift_right))
                then(nc.vector.tensor_copy(ntile[:, :], hi_i[:, 0:BLOCKS]))
            then(nc.vector.tensor_tensor_scan(incl[:, :], ntile[:, :], k.zeros[:, 0:BLOCKS], 0.0, ALU.add, ALU.add))
            then(nc.vector.tensor_tensor(first[:, :], incl[:, :], ntile[:, :], ALU.subtract))
            then(nc.vector.tensor_tensor(m[:, :, :], across(first[:, :], KT), along(k.step_f[:, :], BLOCKS), ALU.is_le))
            then(nc.vector.tensor_reduce(count[:, :], m[:, :, :], AX, ALU.add))
            then(nc.vector.tensor_scalar(count[:, :], count[:, :], -1.0, None, ALU.add))
            then(nc.vector.tensor_copy(blk_i[:, :], count[:, :]))
            if tiled:
                then(nc.vector.tensor_tensor(m2[:, :, :], m[:, :, :], across(first[:, :], KT), ALU.mult))
                then(nc.vector.tensor_reduce(firstsel[:, :], m2[:, :, :], AX, ALU.max))
                then(nc.vector.tensor_tensor(m2[:, :, :], m[:, :, :], across(lo[:, 0:BLOCKS], KT), ALU.mult))
                then(nc.vector.tensor_reduce(tilesel[:, :], m2[:, :, :], AX, ALU.max))
                then(nc.vector.tensor_tensor(tilesel[:, :], tilesel[:, :], firstsel[:, :], ALU.subtract))
                then(nc.vector.tensor_tensor(tilesel[:, :], tilesel[:, :], k.step_f[:, :], ALU.add))
                then(nc.vector.tensor_scalar(tilesel[:, :], tilesel[:, :], float(TILES - 1), None, ALU.min))
                then(nc.vector.tensor_copy(tile_i[:, :], tilesel[:, :]))
                then(nc.vector.tensor_scalar(over[:, :], k.step_f[:, :], incl[:, BLOCKS - 1:BLOCKS], 1e6,
                                             ALU.is_ge, ALU.mult))
                then(nc.vector.scalar_tensor_tensor(locbase[:, :], count[:, :], float(P), over[:, :],
                                                    ALU.mult, ALU.add))
            else:
                then(nc.vector.tensor_scalar(k.sort_base[:, 0:BLOCKS], first[:, :], float(P), None, ALU.mult))
                then(nc.vector.memset(k.sort_base[:, BLOCKS:BLOCKS + 1], float(STEPS * P)))
            then(nc.vector.memset(k.blockrow[:, STEPS:TW], 0))
            then(nc.vector.memset(k.tilerow[:, STEPS:TW], 0))
            nc.vector.tensor_copy(junk[0:1, 0:1], k.zeros[0:1, 0:1]).then_inc(s["rows"], 1)
            dve.wait_ge(s["rows"], 1)


def step_tables(nc, k, name, from_sort):
    with phase(nc, name, "stored split conv turned out tail kept",
               soft=() if from_sort else {"rows": 32 * KT}) as (block, s, sb, ps):
        n = 2
        raw = sb("raw", [P, 2, 2 * P], I32)
        parts = sb("parts", [P, 2, 2 * P], I32)
        val = sb("val", [P, 2, 2 * P])
        ends = sb("ends", [1, 1], I32)
        turned = ps("turned", [P, 2, 4, P])
        blk = block()

        if from_sort:
            @blk.sync
            def _(sp):
                for i in range(KT):
                    if i >= n:
                        sp.wait_ge(s["conv"], 2 * (i - n + 1))
                    sp.dma_start(raw[:, i % n, 0:P], k.rec_dram[i * P * P:(i + 1) * P * P, :].rearrange(
                        "(p e) c -> p (e c)", p=P)).then_inc(s["stored"], 16)
                    sp.wait_ge(s["stored"], 16 * (i + 1))
        else:
            @blk.gpsimd
            def _(pool):
                for i in range(KT):
                    if i >= n:
                        pool.wait_ge(s["conv"], 2 * (i - n + 1))
                        pool.wait_ge(s["kept"], 16 * (i - n + 1))
                    off = bass.IndirectOffsetOnAxis(ap=k.tile_i[:, i:i + 1], axis=0)
                    pool.indirect_dma_start(raw[:, i % n, 0:P], None, k.src_rows, off).then_inc(s["rows"].sem, 16)
                    pool.indirect_dma_start(raw[:, i % n, P:2 * P], None, k.dst_rows, off).then_inc(s["rows"].sem, 16)
                    wait_soft(pool, s["rows"], 32 * (i + 1))

            @blk.sync
            def _(sp):
                line = k.key_dram[1:1 + STEPS * P].rearrange("(i p e) -> i p e", p=P, e=P)
                for i in range(KT):
                    wait_soft(sp, s["rows"], 32 * (i + 1))
                    sp.dma_start(line[i], raw[:, i % n, P:2 * P]).then_inc(s["kept"], 16)
                    sp.wait_ge(s["kept"], 16 * (i + 1))
                sp.wait_ge(s["tail"], 3)
                sp.dma_start(k.key_dram[0:1].rearrange("(a c) -> a c", a=1), ends[:, :]).then_inc(s["kept"], 16)
                sp.dma_start(k.key_dram[1 + STEPS * P:2 + STEPS * P].rearrange("(a c) -> a c", a=1),
                             ends[:, :]).then_inc(s["kept"], 16)
                sp.wait_ge(s["kept"], 16 * (KT + 2))

        @blk.vector
        def _(dve):
            for i in range(KT):
                if i >= n:
                    dve.wait_ge(s["turned"], i - n + 1)
                if from_sort:
                    dve.wait_ge(s["stored"], 16 * (i + 1))
                else:
                    wait_soft(dve, s["rows"], 32 * (i + 1))
                if from_sort:
                    nc.vector.tensor_scalar(parts[:, i % n, 0:P], raw[:, i % n, 0:P], 8, None,
                                            ALU.arith_shift_right).then_inc(s["split"], 1)
                    nc.vector.tensor_scalar(parts[:, i % n, P:2 * P], raw[:, i % n, 0:P], RADIX - 1, None,
                                            ALU.bitwise_and).then_inc(s["split"], 1)
                    dve.wait_ge(s["split"], 2 * i + 2)
                    nc.vector.tensor_copy(val[:, i % n, 0:P], parts[:, i % n, 0:P]).then_inc(s["conv"], 1)
                    nc.vector.tensor_copy(val[:, i % n, P:2 * P], parts[:, i % n, P:2 * P]).then_inc(s["conv"], 1)
                else:
                    nc.vector.tensor_scalar(val[:, i % n, 0:P], raw[:, i % n, 0:P], float(N - 1), None,
                                            ALU.min).then_inc(s["conv"], 1)
                    nc.vector.tensor_scalar(val[:, i % n, P:2 * P], raw[:, i % n, P:2 * P], k.locbase[:, i:i + 1],
                                            None, ALU.subtract).then_inc(s["conv"], 1)
            nc.vector.memset(k.idx[:, STEPS:TW], N if from_sort else 0).then_inc(s["tail"], 1)
            nc.vector.memset(k.loc[:, STEPS:TW], -1.0).then_inc(s["tail"], 1)
            nc.vector.memset(ends[:, :], -1).then_inc(s["tail"], 1)
            dve.wait_ge(s["tail"], 3)

        @blk.tensor
        def _(pe):
            for i in range(KT):
                pe.wait_ge(s["conv"], 2 * (i + 1))
                if i >= n:
                    pe.wait_ge(s["out"], 2 * (i - n + 1))
                nc.tensor.transpose(turned[:, i % n, 0, :], val[:, i % n, 0:P], k.ident[:, :])
                nc.tensor.transpose(turned[:, i % n, 1, :], val[:, i % n, P:2 * P], k.ident[:, :]).then_inc(s["turned"], 1)

        @blk.scalar
        def _(act):
            for i in range(KT):
                act.wait_ge(s["turned"], i + 1)
                nc.scalar.copy(k.idx[:, i * P:(i + 1) * P], turned[:, i % n, 0, :]).then_inc(s["out"], 1)
                nc.scalar.copy(k.loc[:, i * P:(i + 1) * P], turned[:, i % n, 1, :]).then_inc(s["out"], 1)
            act.wait_ge(s["out"], 2 * KT)


def places_by_source(nc, k):
    with phase(nc, "places", "keys ints blkf prefill filled prep base squared match counted picked added conv"
               ) as (block, s, sb, ps):
        src = sb("src", [P, TPAD], I32)
        dst = sb("dst", [P, TPAD], I32)
        blk_i = sb("blk_i", [P, TPAD], I32)
        blkf, dstf, local = (sb(n, [P, TPAD]) for n in ("blkf", "dstf", "local"))
        fill = sb("fill", [P, REC // P], I32)
        square, place = sb("square", [P, TPAD]), sb("place", [P, TPAD])
        match, count, pick = (sb(n, [P, 2, TPAD]) for n in ("match", "count", "pick"))
        zero_row = sb("zero_row", [P, TPAD])
        per = sb("per", [P, BLOCKS + 1])
        base = sb("base", [P, BLOCKS + 1])
        minus = sb("minus", [P, BLOCKS + 1])
        before = sb("before", [P, P])
        others = ps("others", [P, 512])
        blk = block()

        @blk.sync
        def _(sp):
            sp.dma_start(src[:, :], k.src_cols).then_inc(s["keys"], 16)
            sp.dma_start(dst[:, :], k.dst_cols).then_inc(s["keys"], 16)
            sp.wait_ge(s["prefill"], 1)
            sp.dma_start(k.rec_dram.rearrange("(p e) c -> p (e c)", p=P), fill[:, :]).then_inc(s["filled"], 16)
            sp.wait_ge(s["filled"], 16)

        @blk.tensor
        def _(pe):
            pe.wait_ge(s["prep"], 4)
            nc.tensor.matmul(others[:, 0:BLOCKS + 1], before[:, :], per[:, :], start=True, stop=True
                             ).then_inc(s["base"], 1)

        @blk.vector
        def _(dve):
            nc.vector.memset(fill[:, :], N * RADIX + RADIX - 1).then_inc(s["prefill"], 1)
            nc.vector.tensor_tensor(per[:, 0:BLOCKS], k.below[:, 1:BLOCKS + 1], k.below[:, 0:BLOCKS], ALU.subtract
                                    ).then_inc(s["prep"], 1)
            nc.vector.tensor_scalar(per[:, BLOCKS:BLOCKS + 1], k.below[:, BLOCKS:BLOCKS + 1], -1.0, float(TPAD),
                                    ALU.mult, ALU.add).then_inc(s["prep"], 1)
            nc.vector.tensor_scalar(before[:, :], k.not_before[:, :], -1.0, 1.0, ALU.mult, ALU.add).then_inc(s["prep"], 1)
            nc.vector.tensor_scalar(minus[:, :], k.iota[:, 0:BLOCKS + 1], -1.0, None, ALU.mult).then_inc(s["prep"], 1)
            nc.vector.memset(zero_row[:, :], 0.0).then_inc(s["prep"], 1)
            dve.wait_ge(s["keys"], 32)
            nc.vector.tensor_scalar(blk_i[:, :], src[:, :], 7, None, ALU.arith_shift_right).then_inc(s["ints"], 1)
            nc.vector.tensor_scalar(dstf[:, :], dst[:, :], float(N - 1), None, ALU.min).then_inc(s["ints"], 1)
            dve.wait_ge(s["ints"], 2)
            nc.vector.tensor_copy(blkf[:, :], blk_i[:, :]).then_inc(s["blkf"], 1)
            dve.wait_ge(s["blkf"], 1)
            nc.vector.scalar_tensor_tensor(local[:, :], blkf[:, :], float(-P), src[:, :], ALU.mult,
                                           ALU.add).then_inc(s["blkf"], 1)
            dve.wait_ge(s["blkf"], 2)
            nc.vector.scalar_tensor_tensor(k.rec[:, :], dstf[:, :], float(RADIX), local[:, :], ALU.mult, ALU.add
                                           ).then_inc(s["blkf"], 1)
            dve.wait_ge(s["base"], 1)
            nc.vector.scalar_tensor_tensor(base[:, :], others[:, 0:BLOCKS + 1], -1.0, k.sort_base[:, :], ALU.add,
                                           ALU.add).then_inc(s["blkf"], 1)
            dve.wait_ge(s["blkf"], 4)
            dve.wait_ge(s["prep"], 5)

            def pick_block(b, d):
                await_(dve, s, s["match"], b + 1)
                nc.vector.tensor_tensor_scan(count[:, d, :], match[:, d, :], zero_row[:, :], 0.0, ALU.add, ALU.add
                                             ).then_inc(s["counted"], 1)
                await_(dve, s, s["counted"], b + 1)
                await_(dve, s, s["added"], b + 1)
                nc.vector.scalar_tensor_tensor(pick[:, d, :], count[:, d, :], base[:, ds(b, 1)], match[:, d, :],
                                               ALU.add, ALU.mult).then_inc(s["picked"], 1)

            with dve.Fori(0, (BLOCKS + 1) // 2) as r:
                for d in range(2):
                    pick_block(2 * r + d, d)
            pick_block(BLOCKS, 0)
            dve.wait_ge(s["added"], BLOCKS + 3)
            nc.vector.tensor_copy(k.place[:, :], place[:, :]).then_inc(s["conv"], 1)
            dve.wait_ge(s["conv"], 1)

        @blk.scalar
        def _(act):
            def match_block(b, d):
                await_(act, s, s["picked"], b + 1)
                nc.scalar.activation(square[:, :], blkf[:, :], ACT.Square, bias=minus[:, ds(b, 1)]
                                     ).then_inc(s["squared"], 1)
                await_(act, s, s["squared"], b + 1)
                nc.scalar.activation(match[:, d, :], square[:, :], ACT.Relu, bias=k.ones[:, 0:1], scale=-1.0
                                     ).then_inc(s["match"], 1)
                await_(act, s, s["match"], b + 1)

            act.sem_inc(s["picked"], 2)
            act.wait_ge(s["prep"], 4)
            act.wait_ge(s["blkf"], 1)
            with act.Fori(0, (BLOCKS + 1) // 2) as r:
                for d in range(2):
                    match_block(2 * r + d, d)
            match_block(BLOCKS, 0)

        @blk.gpsimd
        def _(pool):
            nc.gpsimd.memset(place[:, :], 0.0).then_inc(s["added"], 1)
            pool.wait_ge(s["added"], 1)
            pool.sem_inc(s["added"], 1)

            def add_block(b, d):
                await_(pool, s, s["added"], b + 2)
                await_(pool, s, s["picked"], b + 3)
                nc.gpsimd.tensor_tensor(place[:, :], place[:, :], pick[:, d, :], ALU.add).then_inc(s["added"], 1)

            with pool.Fori(0, (BLOCKS + 1) // 2) as r:
                for d in range(2):
                    add_block(2 * r + d, d)
            add_block(BLOCKS, 0)


SCATTER_HIST, SCATTER_MLP, SCATTER_MEAN = 6, 17, 4
SCATTER_LAST = SORT_ROUNDS - SCATTER_HIST - 2 * SCATTER_MLP - SCATTER_MEAN - 3 * NR
HALF = UNROLL // 2


class Scatter:

    def __init__(self, nc, k, s, sb, pool):
        self.nc, self.k, self.s, self.pool, self.n = nc, k, s, pool, 0
        self.place = sb("scat_place", [P, 2, HALF], I32)
        self.rec = sb("scat_rec", [P, 2, HALF], I32)

    def round(self, i, wait=True):
        nc, k, s, pool = self.nc, self.k, self.s, self.pool
        for q, soft in enumerate(k.scat):
            t = (i + k.scattered) * UNROLL + q * HALF
            if wait:
                await_(pool, s, soft, i * (16 * HALF))
            nc.gpsimd.tensor_copy(self.place[:, q, :], k.place[:, ds(t, HALF)]).then_inc(s["scat_in"], 1)
            nc.gpsimd.tensor_copy(self.rec[:, q, :], k.rec[:, ds(t, HALF)]).then_inc(s["scat_in"], 1)
            await_(pool, s, s["scat_in"], i * 4 + 2 * q + 2)
            for u in range(HALF):
                pool.indirect_dma_start(k.rec_dram, bass.IndirectOffsetOnAxis(
                    ap=self.place[:, q, u:u + 1], axis=0), self.rec[:, q, u:u + 1], None).then_inc(soft.sem, 16)

    def end(self, rounds):
        k = self.k
        for soft in k.scat:
            wait_soft(self.pool, soft, 16 * HALF * rounds)
            soft.base += 16 * HALF * rounds
        k.scattered += rounds


def program(nc, t, out):
    def sb(name, shape, dt=F32):
        return nc.alloc_sbuf_tensor(name, shape, dt)

    k = Kept()
    first = min(nc.free_semaphores)
    SOFT[:] = [Soft(nc.alloc_semaphore(f"soft{i}", num=first + i)) for i in range(JG + 2)]
    k.scat, k.scattered = SOFT[JG:], 0
    k.ident, k.ones = sb("ident", [P, P]), sb("ones", [P, P])
    k.iota_i, k.iota = sb("iota_i", [P, P], I32), sb("iota", [P, P])
    k.not_before = sb("not_before", [P, P])
    k.step_i, k.step_f = sb("step_i", [P, KT], I32), sb("step_f", [P, KT])
    k.tile_i, k.locbase = sb("tile_i", [P, KT], I32), sb("locbase", [P, KT])
    k.sort_base = sb("sort_base", [P, BLOCKS + 1])
    k.below = sb("below", [P, BLOCKS + 1])
    k.place, k.rec = sb("place", [P, TPAD], I32), sb("rec", [P, TPAD], I32)
    k.zeros = sb("zeros", [P, P])
    k.idx, k.loc = sb("idx", [P, TW], I32), sb("loc", [P, TW])
    k.blockrow, k.tilerow = sb("blockrow", [1, TW], I32), sb("tilerow", [1, TW], I32)
    k.acc = sb("acc", [P, BLOCKS * W])
    k.rec_dram = nc.dram_tensor("rec_dram", (REC, 1), I32).ap()
    k.blk_dram = nc.dram_tensor("blk_dram", (STEPS,), I32).ap()
    k.tile_dram = nc.dram_tensor("tile_dram", (STEPS,), I32).ap()
    k.key_dram = nc.dram_tensor("key_dram", (STEPS * P + 2,), I32).ap()
    k.line_dram = nc.dram_tensor("line_dram", (STEPS * P,), F32).ap()
    k.seg_dram = nc.dram_tensor("seg_dram", (STEPS * P,), F32).ap()
    k.table = nc.dram_tensor("table", (NP, D), F32).ap()
    k.table_gat = nc.dram_tensor("table_gat", (NP, W), F32).ap()
    k.x_dram = nc.dram_tensor("x_dram", (NP, D), F32).ap()
    k.res_dram = nc.dram_tensor("res_dram", (NP, D), F32).ap()
    k.rows_dram = nc.dram_tensor("rows_dram", (ROUNDS * JG + 1, P, G * P), F32).ap()
    k.tables_dram = [(nc.dram_tensor(f"idx_dram{n}", (P, TW), I32).ap(),
                      nc.dram_tensor(f"loc_dram{n}", (P, TW), F32).ap(),
                      nc.dram_tensor(f"row_dram{n}", (1, TW), I32).ap()) for n in range(2)]
    k.src_rows, k.dst_rows, k.src_cols, k.dst_cols = t["src_rows"], t["dst_rows"], t["src_cols"], t["dst_cols"]
    k.deg = sb("deg", [P, BLOCKS])
    constants(nc, k)
    histogram(nc, k, "hist_s", t["src_cols"], False)
    places_by_source(nc, k)
    move_tables(nc, k, "keep_s", True, 1)
    histogram(nc, k, "hist_d", t["dst_cols"], True)
    step_tables(nc, k, "tab_d", False)
    move_tables(nc, k, "keep_d", True, 0)
    layers(nc, k, t, out)


def rows_of(dram, i):
    return dram.rearrange("(b p) f -> p b f", p=P)[:, ds(i * NB, NB), :]


def row_vector(v):
    return v.partition_broadcast(P)


class Chain:

    def __init__(self, eng, s, sem, i, per):
        self.eng, self.s, self.sem, self.i, self.per, self.n = eng, s, sem, i, per, 0

    def __call__(self, ins):
        self.n += 1
        ins.then_inc(self.sem, 1)
        await_(self.eng, self.s, self.sem, self.i * self.per + self.n)

    def end(self):
        assert self.n == self.per, (self.n, self.per)


def layer_norm_relu(nc, s, dve, then, i, x, c, sq, st, out):
    then(nc.vector.tensor_reduce(st[:, 0, :], x, AX, ALU.add))
    then(nc.vector.tensor_scalar(st[:, 0, :], st[:, 0, :], 1.0 / D, None, ALU.mult))
    then(nc.vector.tensor_tensor(c, x, along(st[:, 0, :], D), ALU.subtract))
    then(nc.vector.tensor_tensor(sq, c, c, ALU.mult))
    then(nc.vector.tensor_reduce(st[:, 1, :], sq, AX, ALU.add))
    nc.vector.tensor_scalar(st[:, 1, :], st[:, 1, :], 1.0 / D, LN_EPS, ALU.mult, ALU.add).then_inc(s["var"], 1)
    await_(dve, s, s["std"], i + 1)
    then(nc.vector.reciprocal(st[:, 3, :], st[:, 2, :]))
    then(nc.vector.scalar_tensor_tensor(out, c, 0.0, along(st[:, 3, :], D), ALU.max, ALU.mult))


LN_VECTOR = 7


def layer_norm_std(nc, s, act, i, st):
    await_(act, s, s["var"], i + 1)
    nc.scalar.activation(st[:, 2, :], st[:, 1, :], ACT.Sqrt).then_inc(s["std"], 1)


def blocks(ap, stride=P, width=P, n=NB):
    return ap.rearrange("p (b w) -> p b w", w=stride)[:, :, 0:width]


def node_input(nc, k, t):
    with phase(nc, "nin", "w x_free var std hn turned copied prod v stored used scat_in",
               soft={"x_in": 16 * NR}) as (block, s, sb, ps):
        x, c, sq, h = (sb(n, [P, NB, P]) for n in ("x", "c", "sq", "h"))
        st = sb("st", [P, 4, NB])
        hT = sb("hT", [P, NB * P])
        tab = sb("tab", [P, NB, P])
        w = sb("w", [P, P])
        b_atom, b_bond = sb("b_atom", [P, P]), sb("b_bond", [P, P])
        eps = sb("eps", [P, L])
        turned, prod = ps("turned", [P, 2, 512]), ps("prod", [P, 2, 512])
        blk = block()
        PER = LN_VECTOR + 3

        @blk.sync
        def _(sp):
            sp.dma_start(w[:, :], t["L0_gnn_W_atom"]).then_inc(s["w"], 16)
            sp.dma_start(b_atom[:, :], row_vector(t["L0_gnn_b_atom"])).then_inc(s["w"], 16)
            sp.dma_start(b_bond[:, :], row_vector(t["L0_gnn_b_bond"])).then_inc(s["w"], 16)
            sp.dma_start(eps[:, :], row_vector(t["L0_gnn_eps"])).then_inc(s["w"], 16)
            with sp.Fori(0, NR) as i:
                await_(sp, s, s["v"], (i + 1) * PER)
                sp.dma_start(rows_of(k.table, i), tab[:, :, :]).then_inc(s["stored"], 16)
                await_(sp, s, s["stored"], (i + 1) * 16)
                sp.sem_inc(s["used"], 1)

        @blk.gpsimd
        def _(pool):
            pool.sem_inc(s["x_free"], 1)
            scatter = Scatter(nc, k, s, sb, pool)
            with pool.Fori(0, NR) as i:
                await_(pool, s, s["x_free"], i + 1)
                pool.dma_start(x[:, :, :], rows_of(t["x"], i)).then_inc(s["x_in"].sem, 16)
                scatter.round(i)
            scatter.end(NR)

        @blk.vector
        def _(dve):
            dve.wait_ge(s["w"], 64)
            with dve.Fori(0, NR) as i:
                then = Chain(dve, s, s["v"], i, PER)
                await_(dve, s, s["x_in"], 16 * i + 16)
                layer_norm_relu(nc, s, dve, then, i, x[:, :, :], c[:, :, :], sq[:, :, :], st, h[:, :, :])
                dve.sem_inc(s["hn"], 1)
                dve.sem_inc(s["x_free"], 1)
                await_(dve, s, s["prod"], i + 1)
                p = blocks(prod[:, :, :].rearrange("p a b -> p (a b)")[:, 0:NB * P])
                then(nc.vector.tensor_tensor(h[:, :, :], p, across(b_atom[:, :], NB), ALU.add))
                then(nc.vector.scalar_tensor_tensor(acc_rows(k, i), h[:, :, :], eps[:, 0:1], h[:, :, :],
                                                    ALU.mult, ALU.add))
                await_(dve, s, s["used"], i + 1)
                then(nc.vector.tensor_tensor(tab[:, :, :], h[:, :, :], across(b_bond[:, :], NB), ALU.add))
                then.end()

        @blk.scalar
        def _(act):
            act.sem_inc(s["used"], 1)
            with act.Fori(0, NR) as i:
                layer_norm_std(nc, s, act, i, st)
                await_(act, s, s["turned"], i + 1)
                nc.scalar.copy(hT[:, :], turned[:, :, :].rearrange("p a b -> p (a b)")[:, 0:NB * P]
                               ).then_inc(s["copied"], 1)

        @blk.tensor
        def _(pe):
            pe.wait_ge(s["w"], 64)
            tv = turned[:, :, :].rearrange("p a b -> p (a b)")
            pv = prod[:, :, :].rearrange("p a b -> p (a b)")
            with pe.Fori(0, NR) as i:
                await_(pe, s, s["hn"], i + 1)
                for b in range(NB):
                    ins = nc.tensor.transpose(tv[:, b * P:(b + 1) * P], h[:, b, :], k.ident[:, :])
                ins.then_inc(s["turned"], 1)
                await_(pe, s, s["copied"], i + 1)
                for b in range(NB):
                    ins = nc.tensor.matmul(pv[:, b * P:(b + 1) * P], hT[:, b * P:(b + 1) * P], w[:, :],
                                           start=True, stop=True)
                ins.then_inc(s["prod"], 1)


def acc_rows(k, i, width=D, first=0):
    return k.acc[:, ds(i * (NB * W), NB * W)].rearrange("p (b w) -> p b w", w=W)[:, :, first:first + width]


def flat(psum):
    return psum.rearrange("p a b -> p (a b)")


HALVES = ((0, 512), (512, NB * P - 512))


def batch_norm(nc, s, dve, stats, agg, scale, bias, gain, shift, n, first):
    step = [first]

    def then(ins):
        step[0] += 1
        ins.then_inc(s["bn"], 1)
        dve.wait_ge(s["bn"], step[0])

    for h in range(n):
        then(nc.vector.bn_aggr(agg[:, h, 0:2], stats[:, h, :, :].rearrange("p c s -> p (c s)")))
    nc.vector.tensor_scalar(agg[:, 0:n, 2], agg[:, 0:n, 1], BN_EPS, None, ALU.add).then_inc(s["bn_var"], 1)
    dve.wait_ge(s["bn_std"], 1 if first == 0 else 2)
    then(nc.vector.reciprocal(agg[:, 0:n, 2], agg[:, 0:n, 3]))
    then(nc.vector.tensor_tensor(scale, agg[:, 0:n, 2], gain, ALU.mult))
    then(nc.vector.tensor_tensor(agg[:, 0:n, 3], agg[:, 0:n, 0], scale, ALU.mult))
    then(nc.vector.tensor_tensor(bias, shift, agg[:, 0:n, 3], ALU.subtract))
    dve.sem_inc(s["bn_out"], 1)
    return step[0]


def mlp(nc, k, t, layer):
    last = layer == L - 1
    with phase(nc, f"mlp{layer}", "w staged turned copied mm1 ev1 bn bn_var bn_std bn_out act1 mm2 ev2 act2 rows done "
               "stored used x_free var std hn turned2 copied2 prod v bnst st_free scat_in",
               soft={"x_in": 16 * NR} if last else ()) as (block, s, sb, ps):
        z1 = sb("z1", [P, 2, NP])
        w1, w2 = sb("w1", [P, HID]), sb("w2", [P, 2, D])
        cols = sb("cols", [P, 3, 2])
        cols2 = sb("cols2", [P, 3])
        zT = sb("zT", [P, NB * P])
        stats1 = sb("stats1", [P, 2, 2 * NR, 6])
        stats2 = sb("stats2", [P, 1, 2 * NR + 1, 6])
        agg = sb("agg", [P, 2, 4])
        norm = sb("norm", [P, 2, 2])
        norm2 = sb("norm2", [P, 2, 1])
        rowv = sb("rowv", [P, 2, P])
        eps = sb("eps", [P, L])
        tab = sb("tab", [P, NB, P])
        turned = ps("turned", [P, 2, 512])
        z = ps("z", [P, 4, 512])
        prod = ps("prod", [P, 2, 512])
        hT = zT
        if last:
            zf = z1[:, :, :].rearrange("p a b -> p (a b)")
            n = NB * P
            x, c, sq, hn = (zf[:, j * n:(j + 1) * n].rearrange("p (b f) -> p b f", f=P) for j in range(4))
            wo, wr = zf[:, 4 * n:4 * n + P], zf[:, 4 * n + P:4 * n + 2 * P]
            bo, bl = zf[:, 4 * n + 2 * P:4 * n + 3 * P], zf[:, 4 * n + 3 * P:4 * n + 4 * P]
            hT2 = zf[:, 5 * n:6 * n]
            st = sb("st", [P, 4, NB])
        full = [(i, b, n) for i in range(NR) for b, n in ((0, 4), (4, 3))]
        blk = block()
        NW = 3 + 6 + 3 + 2

        @blk.sync
        def _(sp):
            sp.dma_start(w1[:, :], t["L0_gnn_W1"][layer]).then_inc(s["w"], 16)
            sp.dma_start(w2[:, :, :], t["L0_gnn_W2"][layer].rearrange("(h p) n -> p h n", p=P)).then_inc(s["w"], 16)
            sp.dma_start(eps[:, :], row_vector(t["L0_gnn_eps"])).then_inc(s["w"], 16)
            for n, v in enumerate((t["L0_gnn_b1"], t["L0_gnn_g1"], t["L0_gnn_be1"])):
                for h in range(2):
                    sp.dma_start(cols[:, n, h:h + 1], v[layer, h * P:(h + 1) * P].rearrange("(p a) -> p a", a=1)
                                 ).then_inc(s["w"], 16)
            for n, v in enumerate((t["L0_gnn_b2"], t["L0_gnn_gn"], t["L0_gnn_bet"])):
                sp.dma_start(cols2[:, n:n + 1], v[layer].rearrange("(p a) -> p a", a=1)).then_inc(s["w"], 16)
            sp.dma_start(rowv[:, 0, :], row_vector(t["L0_gnn_b_bond"])).then_inc(s["w"], 16)
            sp.dma_start(rowv[:, 1, :], row_vector(t["L0_gnn_b_bond"])).then_inc(s["w"], 16)
            if last:
                sp.wait_ge(s["ev2"], NR + 1)
                sp.dma_start(wo, t["L0_gnn_W_out"]).then_inc(s["w"], 16)
                sp.dma_start(wr, t["L1_gnn_W_r"]).then_inc(s["w"], 16)
                sp.dma_start(bo, row_vector(t["L0_gnn_b_out"])).then_inc(s["w"], 16)
                sp.dma_start(bl, row_vector(t["L1_gnn_b_l"])).then_inc(s["w"], 16)
            with sp.Fori(0, NR) as i:
                if last:
                    await_(sp, s, s["hn"], i + 1)
                    sp.dma_start(rows_of(k.table, i), hn).then_inc(s["stored"], 16)
                    await_(sp, s, s["done"], i + 1)
                    sp.dma_start(rows_of(k.x_dram, i), tab[:, :, :]).then_inc(s["stored"], 16)
                    await_(sp, s, s["stored"], (i + 1) * 32)
                else:
                    await_(sp, s, s["done"], i + 1)
                    sp.dma_start(rows_of(k.table, i), tab[:, :, :]).then_inc(s["stored"], 16)
                    await_(sp, s, s["stored"], (i + 1) * 16)
                sp.sem_inc(s["used"], 1)

        @blk.gpsimd
        def _(pool):
            scatter = Scatter(nc, k, s, sb, pool)
            alone = SCATTER_LAST if last else SCATTER_MLP
            with pool.Fori(0, alone) as i:
                scatter.round(i)
            if last:
                pool.sem_inc(s["x_free"], 1)
                pool.wait_ge(s["ev2"], NR + 1)
                with pool.Fori(0, NR) as i:
                    await_(pool, s, s["x_free"], i + 1)
                    pool.dma_start(x, rows_of(t["x"], i)).then_inc(s["x_in"].sem, 16)
                    scatter.round(i + alone)
            scatter.end(alone + (NR if last else 0))

        @blk.tensor
        def _(pe):
            pe.wait_ge(s["w"], 16 * NW)
            tv, zv, pv = flat(turned[:, :, :]), z, flat(prod[:, :, :])
            with pe.Fori(0, NR) as i:
                await_(pe, s, s["staged"], i + 1)
                for b in range(NB):
                    ins = nc.tensor.transpose(tv[:, b * P:(b + 1) * P], tab[:, b, :], k.ident[:, :])
                ins.then_inc(s["turned"], 1)
                await_(pe, s, s["copied"], i + 1)
                await_(pe, s, s["ev1"], 2 * i + 2)
                for h in range(2):
                    for j, (c0, n) in enumerate(HALVES):
                        ins = nc.tensor.matmul(z[:, 2 * h + j, 0:n], w1[:, h * P:(h + 1) * P], zT[:, c0:c0 + n],
                                               start=True, stop=True)
                ins.then_inc(s["mm1"], 1)
            with pe.Fori(0, NR) as i:
                await_(pe, s, s["act1"], i + 1)
                await_(pe, s, s["ev2"], i + 1)
                for j, (c0, n) in enumerate(HALVES):
                    for h in range(2):
                        ins = nc.tensor.matmul(z[:, j, 0:n], w2[:, h, :], z1[:, h, ds(i * (NB * P) + c0, n)],
                                               start=h == 0, stop=h == 1)
                ins.then_inc(s["mm2"], 1)
            if last:
                pe.wait_ge(s["w"], 16 * (NW + 4))
            with pe.Fori(0, NR) as i:
                await_(pe, s, s["act2"], i + 1)
                await_(pe, s, s["rows"], i + 1)
                for b in range(NB):
                    if last:
                        ins = nc.tensor.matmul(pv[:, b * P:(b + 1) * P], hT[:, b * P:(b + 1) * P], wo,
                                               start=True, stop=True)
                    else:
                        ins = nc.tensor.transpose(pv[:, b * P:(b + 1) * P], hT[:, b * P:(b + 1) * P], k.ident[:, :])
                ins.then_inc(s["prod"], 1)
                if last:
                    await_(pe, s, s["hn"], i + 1)
                    for b in range(NB):
                        ins = nc.tensor.transpose(tv[:, b * P:(b + 1) * P], hn[:, b, :], k.ident[:, :])
                    ins.then_inc(s["turned2"], 1)
                    await_(pe, s, s["copied2"], i + 1)
                    for b in range(NB):
                        ins = nc.tensor.matmul(z[:, b // 4, b % 4 * P:b % 4 * P + P], hT2[:, b * P:(b + 1) * P], wr,
                                               start=True, stop=True)
                    ins.then_inc(s["mm2"], 1)

        @blk.scalar
        def _(act):
            act.sem_inc(s["ev1"], 2)
            act.sem_inc(s["ev2"], 1)
            act.sem_inc(s["rows"], 1)
            act.sem_inc(s["used"], 1)
            act.wait_ge(s["w"], 16 * NW)
            with act.Fori(0, NR) as i:
                await_(act, s, s["turned"], i + 2)
                nc.scalar.copy(zT[:, :], flat(turned[:, :, :])[:, 0:NB * P]).then_inc(s["copied"], 1)
                await_(act, s, s["mm1"], i + 1)
                for h in range(2):
                    nc.scalar.activation(z1[:, h, ds(i * (NB * P), NB * P)],
                                         flat(z[:, 2 * h:2 * h + 2, :])[:, 0:NB * P], ACT.Identity,
                                         bias=cols[:, 0, h:h + 1]).then_inc(s["ev1"], 1)
            act.wait_ge(s["bn_var"], 1)
            nc.scalar.activation(agg[:, 0:2, 3], agg[:, 0:2, 2], ACT.Sqrt).then_inc(s["bn_std"], 1)
            act.wait_ge(s["bn_out"], 1)
            with act.Fori(0, NR) as i:
                for h in range(2):
                    ins = nc.scalar.activation(z1[:, h, ds(i * (NB * P), NB * P)],
                                               z1[:, h, ds(i * (NB * P), NB * P)], ACT.Relu,
                                               bias=norm[:, 1, h:h + 1], scale=norm[:, 0, h:h + 1])
                ins.then_inc(s["act1"], 1)
                await_(act, s, s["mm2"], i + 1)
                nc.scalar.activation(acc_rows(k, i), blocks(flat(z[:, 0:2, :])[:, 0:NB * P]), ACT.Identity,
                                     bias=cols2[:, 0:1]).then_inc(s["ev2"], 1)
            act.wait_ge(s["bn_var"], 2)
            nc.scalar.activation(agg[:, 0:1, 3], agg[:, 0:1, 2], ACT.Sqrt).then_inc(s["bn_std"], 1)
            act.wait_ge(s["bn_out"], 2)
            with act.Fori(0, NR) as i:
                await_(act, s, s["bnst"], i + 1)
                nc.scalar.activation(blocks(hT[:, :]), acc_rows(k, i), ACT.Relu,
                                     bias=norm2[:, 1, 0:1], scale=norm2[:, 0, 0:1]).then_inc(s["act2"], 1)
                await_(act, s, s["prod"], i + 1)
                act.sem_inc(s["bnst"], 1)
                if last:
                    layer_norm_std(nc, s, act, i, st)
                    await_(act, s, s["turned2"], i + 1)
                    nc.scalar.copy(hT2, flat(turned[:, :, :])[:, 0:NB * P]).then_inc(s["copied2"], 1)

        @blk.vector
        def _(dve):
            dve.sem_inc(s["bnst"], 1)
            dve.wait_ge(s["w"], 16 * NW)

            def stats_1(i, c, n=NB * P // 2):
                for h in range(2):
                    nc.vector.bn_stats(stats1[:, h, ds(2 * i + c, 1), :].rearrange("p a s -> p (a s)"),
                                       z1[:, h, ds(i * (NB * P) + c * (NB * P // 2), n)]).then_inc(s["st_free"], 1)

            def stage(i):
                await_(dve, s, s["turned"], i + 1)
                nc.vector.tensor_copy(tab[:, :, :], acc_rows(k, i)).then_inc(s["staged"], 1)

            dve.sem_inc(s["turned"], 1)
            stage(0)
            with dve.Fori(0, NR - 1) as i:
                stage(i + 1)
                await_(dve, s, s["ev1"], 2 * i + 4)
                stats_1(i, 0)
                stats_1(i, 1)
            dve.wait_ge(s["ev1"], 2 * NR + 2)
            stats_1(NR - 1, 0)
            stats_1(NR - 1, 1, N - (NR - 1) * NB * P - NB * P // 2)
            dve.wait_ge(s["st_free"], 4 * NR)
            n = batch_norm(nc, s, dve, stats1, agg, norm[:, 0, :], norm[:, 1, :], cols[:, 1, :], cols[:, 2, :], 2, 0)

            def stats_2(i, g, b, n, w=P, m=None):
                nc.vector.bn_stats(stats2[:, 0, ds(g, 1), :].rearrange("p a s -> p (a s)"),
                                   acc_rows(k, i)[:, b:b + n, 0:w]).then_inc(s["st_free"], 1)

            with dve.Fori(0, NR - 1) as i:
                await_(dve, s, s["ev2"], i + 2)
                stats_2(i, 2 * i, 0, 4)
                stats_2(i, 2 * i + 1, 4, 3)
            dve.wait_ge(s["ev2"], NR + 1)
            stats_2(NR - 1, 2 * NR - 2, 0, 4)
            stats_2(NR - 1, 2 * NR - 1, 4, 2)
            stats_2(NR - 1, 2 * NR, 6, 1, LAST_ROWS)
            dve.wait_ge(s["st_free"], 6 * NR + 1)
            n = batch_norm(nc, s, dve, stats2, agg, norm2[:, 0, :], norm2[:, 1, :], cols2[:, 1:2], cols2[:, 2:3], 1, n)
            PER = LN_VECTOR + 4 if last else 2
            if last:
                dve.wait_ge(s["w"], 16 * (NW + 4))
            with dve.Fori(0, NR) as i:
                then = Chain(dve, s, s["v"], i, PER)
                await_(dve, s, s["prod"], i + 1)
                p = blocks(flat(prod[:, :, :])[:, 0:NB * P])
                if last:
                    await_(dve, s, s["x_in"], 16 * i + 16)
                    await_(dve, s, s["used"], i + 1)
                    then(nc.vector.tensor_tensor(x, x, p, ALU.add))
                    dve.sem_inc(s["rows"], 1)
                    then(nc.vector.tensor_tensor(tab[:, :, :], x, across(bo, NB), ALU.add))
                    layer_norm_relu(nc, s, dve, then, i, tab[:, :, :], c, sq, st, hn)
                    dve.sem_inc(s["hn"], 1)
                    dve.sem_inc(s["x_free"], 1)
                    await_(dve, s, s["mm2"], NR + i + 1)
                    then(nc.vector.tensor_tensor(tab[:, :, :], tab[:, :, :], across(bl, NB), ALU.add))
                    then(nc.vector.tensor_tensor(tab[:, :, :], tab[:, :, :], blocks(flat(z[:, 0:2, :])[:, 0:NB * P]),
                                                 ALU.add))
                else:
                    then(nc.vector.tensor_scalar(acc_rows(k, i), p, eps[:, layer + 1:layer + 2], None, ALU.mult))
                    then(nc.vector.tensor_tensor(acc_rows(k, i), acc_rows(k, i), p, ALU.add))
                    await_(dve, s, s["used"], i + 1)
                    nc.vector.tensor_tensor(tab[:, :, :], p, across(rowv[:, 0, :], NB), ALU.add).then_inc(s["rows"], 1)
                    await_(dve, s, s["rows"], i + 2)
                dve.sem_inc(s["done"], 1)
                then.end()
            if last:
                nc.vector.memset(k.acc[:, :], 0.0).then_inc(s["bn"], 1)
                dve.wait_ge(s["bn"], n + 1)


def ring_counts(lead):
    return {f"gat{q}": 64 * (ROUNDS + (1 if q < lead else 0)) for q in range(JG)}


def gather_ring(nc, s, pool, k, idxs, rows, table, lead, width):
    gat = [s["gat0"], s["gat1"], s["gat2"], s["gat3"]]

    def gather(g, q):
        await_(pool, s, s["idx_ready"], g + 1)
        for u in range(G):
            pool.indirect_dma_start(rows[:, q, u, 0:width], None, table,
                                    bass.IndirectOffsetOnAxis(ap=idxs[:, q, u:u + 1], axis=0)).then_inc(gat[q].sem, 16)

    for g in range(lead):
        gather(g, g)
    with pool.Fori(0, ROUNDS) as r:
        for q in range(JG):
            gather(r * JG + q + lead, (q + lead) % JG)
    for q in range(JG):
        wait_soft(pool, gat[q], 64 * (ROUNDS + (1 if q < lead else 0)))


def refill(nc, s, k, act, idxs, m, q):
    nc.scalar.copy(idxs[:, q, :], k.idx[:, ds(m * G, G)]).then_inc(s["idx_ready"], 1)


def edges_gine(nc, k, t, layer):
    with phase(nc, f"gine{layer}", "w ea0 ea1 ea2 ea3 idx_ready hot bond added relu seg accd",
               soft=ring_counts(1)) as (block, s, sb, ps):
        rows = sb("rows", [P, JG, G, P])
        ea = sb("ea", [P, JG, G, P])
        idxs = sb("idxs", [P, JG, G], I32)
        hot = sb("hot", [P, 2, G, P])
        msg = sb("msg", [P, 2, G, P])
        w = sb("w", [P, P])
        bond, seg = ps("bond", [P, 2, 512]), ps("seg", [P, 2, 512])
        ea_in = [s["ea0"], s["ea1"], s["ea2"], s["ea3"]]
        gat = [s["gat0"], s["gat1"], s["gat2"], s["gat3"]]
        blk = block()

        @blk.sync
        def _(sp):
            sp.dma_start(w[:, :], t["L0_gnn_W_bond"]).then_inc(s["w"], 16)

            def load(g, q, tiles):
                await_(sp, s, s["bond"], g + 1)
                for u in range(G):
                    sp.dma_start(ea[:, q, u, :], t["edge_t"][ds(tiles[u], 1), :, :].rearrange("a f e -> (a f) e")
                                 ).then_inc(ea_in[q], 16)

            tiles, _ = load_registers(sp, k.tilerow[0:1, 0:G], f"t0_{layer}", 0, TILES - 1)
            load(0, 0, tiles)
            with sp.Fori(0, ROUNDS) as r:
                tiles, _ = load_registers(sp, k.tilerow[0:1, ds(r * UNROLL + G, UNROLL)], f"t_{layer}", 0, TILES - 1)
                for j in range(JG):
                    load(r * JG + j + 1, (j + 1) % JG, tiles[j * G:(j + 1) * G])

        @blk.gpsimd
        def _(pool):
            gather_ring(nc, s, pool, k, idxs, rows, k.table, 1, D)

        @blk.tensor
        def _(pe):
            def edge_product(r, g, j):
                d = j % 2
                await_(pe, s, ea_in[j % JG], (r + j // JG) * 64 + 64)
                await_(pe, s, s["added"], g + 1)
                for u in range(G):
                    ins = nc.tensor.matmul(bond[:, d, u * P:(u + 1) * P], ea[:, j % JG, u, :], w[:, :],
                                           start=True, stop=True)
                ins.then_inc(s["bond"], 1)

            def segment_sums(g, j):
                d = j % 2
                await_(pe, s, s["hot"], g + 1)
                await_(pe, s, s["relu"], g + 1)
                await_(pe, s, s["accd"], g * G + G)
                for u in range(G):
                    ins = nc.tensor.matmul(seg[:, d, u * P:(u + 1) * P], hot[:, d, u, :], msg[:, d, u, :],
                                           start=True, stop=True)
                ins.then_inc(s["seg"], 1)

            pe.sem_inc(s["bond"], JG)
            pe.sem_inc(s["seg"], 2)
            pe.wait_ge(s["w"], 16)
            edge_product(0, 0, 0)
            with pe.Fori(0, ROUNDS) as r:
                for j in range(JG):
                    g = r * JG + j
                    edge_product(r, g + 1, j + 1)
                    segment_sums(g, j)

        @blk.scalar
        def _(act):
            def relu(g, j):
                await_(act, s, s["added"], g + 3)
                nc.scalar.activation(msg[:, j % 2], msg[:, j % 2], ACT.Relu).then_inc(s["relu"], 1)
                refill(nc, s, k, act, idxs, g + JG, j % JG)

            for m in range(JG):
                refill(nc, s, k, act, idxs, m, m)
            relu(0, 0)
            with act.Fori(0, ROUNDS) as r:
                for j in range(JG):
                    relu(r * JG + j + 1, j + 1)

        @blk.vector
        def _(dve):
            def messages(r, g, j):
                d = j % 2
                await_(dve, s, s["seg"], g + 1)
                nc.vector.tensor_tensor(hot[:, d], across(k.iota[:, :], G), along(k.loc[:, ds(g * G, G)], P),
                                        ALU.is_equal).then_inc(s["hot"], 1)
                await_(dve, s, s["bond"], g + JG + 1)
                await_(dve, s, gat[j % JG], (r + j // JG) * 64 + 64)
                nc.vector.tensor_tensor(msg[:, d], rows[:, j % JG], bond[:, d].rearrange("p (u f) -> p u f", f=P),
                                        ALU.add).then_inc(s["added"], 1)

            dve.sem_inc(s["added"], 2)
            dve.sem_inc(s["accd"], 2 * G)
            messages(0, 0, 0)
            with dve.Fori(0, ROUNDS) as r:
                where, _ = load_registers(dve, k.blockrow[0:1, ds(r * UNROLL, UNROLL)], f"b_{layer}", 0, BLOCKS - 1)
                for j in range(JG):
                    g = r * JG + j
                    messages(r, g + 1, j + 1)
                    accumulate(nc, s, dve, k, seg[:, j % 2], g, where[j * G:(j + 1) * G], D,
                               [u * P for u in range(G)])
            dve.wait_ge(s["accd"], STEPS + 2 * G)


def accumulate(nc, s, dve, k, seg, g, where, width, at, credits=2, between=None, slots=2):
    await_(dve, s, s["seg"], g + 1 + credits)
    for u in range(G):
        a = k.acc[:, ds(where[u] * W, width)]
        dve.wait_ge(s["accd"], g * G + u + slots * G)
        nc.vector.tensor_tensor(a, a, seg[:, at[u]:at[u] + width], ALU.add).then_inc(s["accd"], 1)
        if between:
            between(u)


def bank_at(width):
    return [(u // 2) * 512 + (u % 2) * 256 for u in range(G)]


def edges_mean(nc, k):
    with phase(nc, "mean", "idx_ready hot seg accd one", soft=ring_counts(1)) as (block, s, sb, ps):
        rows = sb("rows", [P, JG, G, W])
        idxs = sb("idxs", [P, JG, G], I32)
        hot = sb("hot", [P, 2, G, P])
        seg = ps("seg", [P, 2, 1024])
        gat = [s["gat0"], s["gat1"], s["gat2"], s["gat3"]]
        at = bank_at(P + 1)
        blk = block()

        @blk.gpsimd
        def _(pool):
            gather_ring(nc, s, pool, k, idxs, rows, k.table, 1, D)

        @blk.tensor
        def _(pe):
            pe.sem_inc(s["seg"], 2)
            pe.wait_ge(s["one"], 1)
            with pe.Fori(0, ROUNDS) as r:
                for j in range(JG):
                    g, d = r * JG + j, j % 2
                    await_(pe, s, gat[j], r * 64 + 64)
                    await_(pe, s, s["hot"], g + 1)
                    await_(pe, s, s["accd"], g * G + G)
                    for u in range(G):
                        ins = nc.tensor.matmul(seg[:, d, at[u]:at[u] + P + 1], hot[:, d, u, :],
                                               rows[:, j, u, 0:P + 1], start=True, stop=True)
                    ins.then_inc(s["seg"], 1)

        @blk.scalar
        def _(act):
            for m in range(JG):
                refill(nc, s, k, act, idxs, m, m)
            with act.Fori(0, ROUNDS) as r:
                for j in range(JG):
                    g = r * JG + j
                    await_(act, s, s["seg"], g + 3)
                    refill(nc, s, k, act, idxs, g + JG, j)

        @blk.vector
        def _(dve):
            def one_hot(g, j):
                await_(dve, s, s["seg"], g + 1)
                nc.vector.tensor_tensor(hot[:, j % 2], across(k.iota[:, :], G), along(k.loc[:, ds(g * G, G)], P),
                                        ALU.is_equal).then_inc(s["hot"], 1)

            nc.vector.memset(rows[:, :, :, P:P + 1], 1.0).then_inc(s["one"], 1)
            dve.sem_inc(s["accd"], 2 * G)
            one_hot(0, 0)
            with dve.Fori(0, ROUNDS) as r:
                where, _ = load_registers(dve, k.blockrow[0:1, ds(r * UNROLL, UNROLL)], "b_mean", 0, BLOCKS - 1)
                for j in range(JG):
                    g = r * JG + j
                    one_hot(g + 1, j + 1)
                    accumulate(nc, s, dve, k, seg[:, j % 2], g, where[j * G:(j + 1) * G], P + 1, at)
            dve.wait_ge(s["accd"], STEPS + 2 * G)


def node_mean(nc, k, t):
    with phase(nc, "nmean", "w wa var std hn turned copied prod v stored used done staged deg tab_in "
               "moved row top scat_in x_used", soft={"x_in0": 8 * NR, "x_in1": 8 * NR}) as (block, s, sb, ps):
        c, sq, h = (sb(n, [P, NB, P]) for n in ("c", "sq", "h"))
        xs = sb("x", [P, 2, NB, P])
        st = sb("st", [P, 4, NB])
        hT = sb("hT", [P, NB * P])
        tabg = sb("tabg", [P, NB, W])
        res = sb("res", [P, NB, P])
        wl, wrp = sb("wl", [P, P]), sb("wrp", [P, P])
        wcat = sb("wcat", [P, P + 2 * HEADS])
        av = sb("av", [P, 2, P])
        prodw = sb("prodw", [P, 2, P])
        rdeg = sb("rdeg", [P, NB])
        ht = sb("ht", [P, BLOCKS, HEADS])
        padmask = sb("padmask", [P, 1])
        top = sb("top", [P, HEADS])
        topr = sb("topr", [HEADS, 2])
        diag = sb("diag", [HEADS, HEADS])
        topb = sb("topb", [P, HEADS])
        turned, prod = ps("turned", [P, 2, 512]), ps("prod", [P, 2, 512])
        big = ps("big", [P, 3, 512])
        small = ps("small", [P, 512])
        blk = block()
        PER = 3 + LN_VECTOR + 1

        @blk.sync
        def _(sp):
            sp.dma_start(wl[:, :], t["L1_gnn_W_l"]).then_inc(s["w"], 16)
            sp.dma_start(wrp[:, :], t["L2_gnn_residual_projection"]).then_inc(s["w"], 16)
            sp.dma_start(wcat[:, 0:P], t["L2_gnn_W"]).then_inc(s["w"], 16)
            for n, a in enumerate((t["L2_gnn_A_right"], t["L2_gnn_A_left"])):
                sp.dma_start(av[:, n, :], row_vector(a.rearrange("h d a -> (h d a)"))).then_inc(s["w"], 16)
            with sp.Fori(0, NR // 2) as r:
                for d in range(2):
                    i = 2 * r + d
                    await_(sp, s, s["hn"], i + 1)
                    sp.dma_start(rows_of(k.x_dram, i), xs[:, d]).then_inc(s["stored"], 16)
                    await_(sp, s, s["stored"], 48 * i + 16)
                    sp.sem_inc(s["x_used"], 1)
                    await_(sp, s, s["done"], 3 * i + 3)
                    sp.dma_start(rows_of(k.table_gat, i), tabg[:, :, :]).then_inc(s["stored"], 16)
                    sp.dma_start(rows_of(k.res_dram, i), res[:, :, :]).then_inc(s["stored"], 16)
                    await_(sp, s, s["stored"], 48 * i + 48)
                    sp.sem_inc(s["used"], 1)
            sp.wait_ge(s["moved"], 1)
            sp.dma_start(k.table_gat[(BLOCKS - 1) * P:NP, D:W], ht[:, BLOCKS - 1, :]).then_inc(s["stored"], 16)
            sp.wait_ge(s["stored"], 48 * NR + 16)

        @blk.gpsimd
        def _(pool):
            scatter = Scatter(nc, k, s, sb, pool)
            with pool.Fori(0, NR // 2) as r:
                for d in range(2):
                    await_(pool, s, s["x_used"], 2 * r + d + 1)
                    pool.dma_start(xs[:, d], rows_of(k.x_dram, 2 * r + d)).then_inc(s[f"x_in{d}"].sem, 16)
                    scatter.round(2 * r + d)
            with pool.Fori(NR, NR + SCATTER_MEAN) as i:
                scatter.round(i)
            scatter.end(NR + SCATTER_MEAN)

        @blk.vector
        def _(dve):
            step = [0]

            def once(ins):
                step[0] += 1
                ins.then_inc(s["wa"], 1)
                dve.wait_ge(s["wa"], step[0])

            dve.wait_ge(s["w"], 80)
            for n in range(2):
                once(nc.vector.tensor_tensor(prodw[:, n, :], wcat[:, 0:P], av[:, n, :], ALU.mult))
                once(nc.vector.tensor_reduce(wcat[:, P + n * HEADS:P + (n + 1) * HEADS],
                                             prodw[:, n, :].rearrange("p (h d) -> p h d", d=HD), AX, ALU.add))
            once(nc.vector.tensor_scalar(padmask[:, :], k.step_f[:, 0:1], float(LAST_ROWS), -1e30, ALU.is_ge, ALU.mult))
            with dve.Fori(0, NR // 2) as r:
                for d in range(2):
                    i = 2 * r + d
                    then = Chain(dve, s, s["v"], i, PER)
                    nc.vector.tensor_copy(k.deg[:, ds(i * NB, NB)], acc_rows(k, i, 1, P).rearrange("p b a -> p (b a)")
                                          ).then_inc(s["deg"], 1)
                    then(nc.vector.tensor_scalar(rdeg[:, :], acc_rows(k, i, 1, P).rearrange("p b a -> p (b a)"), 1.0, None,
                                                 ALU.max))
                    then(nc.vector.reciprocal(rdeg[:, :], rdeg[:, :]))
                    nc.vector.tensor_tensor(h[:, :, :], acc_rows(k, i), along(rdeg[:, :], P), ALU.mult).then_inc(s["staged"], 1)
                    await_(dve, s, s[f"x_in{d}"], 16 * r + 16)
                    await_(dve, s, s["prod"], 2 * i + 1)
                    then(nc.vector.tensor_tensor(xs[:, d], xs[:, d], blocks(flat(prod[:, :, :])[:, 0:NB * P]), ALU.add))
                    layer_norm_relu(nc, s, dve, then, i, xs[:, d], c[:, :, :], sq[:, :, :], st, h[:, :, :])
                    dve.sem_inc(s["hn"], 1)
                    await_(dve, s, s["tab_in"], i + 1)
                    then(nc.vector.tensor_copy(ht[:, ds(i * NB, NB), :], tabg[:, :, P:W]))
                    dve.sem_inc(s["done"], 1)
                    then.end()
            once(nc.vector.tensor_scalar(ht[:, BLOCKS - 1, :], ht[:, BLOCKS - 1, :], padmask[:, 0:1], None, ALU.add))
            dve.sem_inc(s["moved"], 1)
            nc.vector.tensor_reduce(top[:, :], ht[:, :, :].rearrange("p b h -> p h b"), AX, ALU.max).then_inc(s["top"], 1)
            dve.wait_ge(s["row"], 1)
            once(nc.vector.tensor_reduce(topr[:, 0:1], small[0:HEADS, 0:P], AX, ALU.max))
            nc.vector.tensor_scalar(diag[:, :], k.ident[0:HEADS, 0:HEADS], topr[:, 0:1], None, ALU.mult
                                    ).then_inc(s["top"], 1)
            dve.wait_ge(s["row"], 2)
            once(nc.vector.tensor_copy(topb[:, :], small[:, P:P + HEADS]))
            dve.wait_ge(s["done"], 3 * NR)
            dve.wait_ge(s["stored"], 48 * NR + 16)
            once(nc.vector.tensor_tensor(ht[:, :, :], k.hsn[:, :, 0:HEADS], across(topb[:, :], BLOCKS), ALU.add))
            nc.vector.memset(k.acc[:, :], 0.0).then_inc(s["top"], 1)
            once(nc.vector.scalar_tensor_tensor(k.hsn[:, :, HEADS:], ht[:, :, :], 0.2, ht[:, :, :], ALU.mult, ALU.max))
            once(nc.vector.memset(k.smax[:, :], -1e30))
            dve.wait_ge(s["top"], 3)

        @blk.scalar
        def _(act):
            act.sem_inc(s["used"], 1)
            act.sem_inc(s["x_used"], 2)
            with act.Fori(0, NR) as i:
                await_(act, s, s["turned"], 2 * i + 1)
                nc.scalar.copy(hT[:, :], flat(turned[:, :, :])[:, 0:NB * P]).then_inc(s["copied"], 1)
                layer_norm_std(nc, s, act, i, st)
                await_(act, s, s["turned"], 2 * i + 2)
                nc.scalar.copy(hT[:, :], flat(turned[:, :, :])[:, 0:NB * P]).then_inc(s["copied"], 1)
                await_(act, s, s["prod"], 2 * i + 2)
                await_(act, s, s["used"], i + 1)
                nc.scalar.copy(tabg[:, 0:6, :].rearrange("p (q r) c -> p q r c", r=3),
                               big[:, 0:2, 0:3 * (P + 8)].rearrange("p q (r c) -> p q r c", r=3)[:, :, :, 0:W])
                nc.scalar.copy(tabg[:, 6:7, :], big[:, 2:3, 0:W]).then_inc(s["tab_in"], 1)
                nc.scalar.copy(k.hsn[:, ds(i * NB, NB), :][:, 0:6, 0:HEADS].rearrange("p (q r) h -> p q r h", r=3),
                               big[:, 0:2, 0:3 * (P + 8)].rearrange("p q (r c) -> p q r c", r=3)[:, :, :, W:W + HEADS])
                nc.scalar.copy(k.hsn[:, ds(i * NB + 6, 1), 0:HEADS], big[:, 2:3, W:W + HEADS]).then_inc(s["done"], 1)
                nc.scalar.copy(res[:, :, :], blocks(flat(prod[:, :, :])[:, 0:NB * P])).then_inc(s["done"], 1)

        @blk.tensor
        def _(pe):
            pe.wait_ge(s["w"], 80)
            pe.wait_ge(s["wa"], 5)
            tv, pv = flat(turned[:, :, :]), flat(prod[:, :, :])
            with pe.Fori(0, NR) as i:
                await_(pe, s, s["staged"], i + 1)
                for b in range(NB):
                    ins = nc.tensor.transpose(tv[:, b * P:(b + 1) * P], h[:, b, :], k.ident[:, :])
                ins.then_inc(s["turned"], 1)
                await_(pe, s, s["copied"], 2 * i + 1)
                for b in range(NB):
                    ins = nc.tensor.matmul(pv[:, b * P:(b + 1) * P], hT[:, b * P:(b + 1) * P], wl[:, :],
                                           start=True, stop=True)
                ins.then_inc(s["prod"], 1)
                await_(pe, s, s["hn"], i + 1)
                for b in range(NB):
                    ins = nc.tensor.transpose(tv[:, b * P:(b + 1) * P], h[:, b, :], k.ident[:, :])
                ins.then_inc(s["turned"], 1)
                await_(pe, s, s["copied"], 2 * i + 2)
                for b in range(NB):
                    nc.tensor.matmul(big[:, b // 3, b % 3 * (P + 8):(b % 3 + 1) * (P + 8)], hT[:, b * P:(b + 1) * P],
                                     wcat[:, :], start=True, stop=True)
                    ins = nc.tensor.matmul(pv[:, b * P:(b + 1) * P], hT[:, b * P:(b + 1) * P], wrp[:, :],
                                           start=True, stop=True)
                ins.then_inc(s["prod"], 1)
                await_(pe, s, s["done"], 3 * i + 3)
            pe.wait_ge(s["top"], 1)
            nc.tensor.transpose(small[0:HEADS, 0:P], top[:, :], k.ident[:, :]).then_inc(s["row"], 1)
            pe.wait_ge(s["top"], 2)
            nc.tensor.matmul(small[:, P:P + HEADS], k.ones[0:HEADS, :], diag[:, :], start=True, stop=True
                             ).then_inc(s["row"], 1)


def edges_gat(nc, k):
    with phase(nc, "gat", "idx_ready hot turned copied left sc score_step score exped scaled seg accd",
               soft=ring_counts(2)) as (block, s, sb, ps):
        rows = sb("rows", [P, JG, G, W])
        idxs = sb("idxs", [P, JG, G], I32)
        hot, hotT = sb("hot", [P, 4, G, P]), sb("hotT", [P, 2, G, P])
        t0, sc, ex = (sb(n, [P, 2, G, HEADS]) for n in ("t0", "sc", "ex"))
        part = sb("part", [P, 2, G, W])
        turned, left = ps("turned", [P, 2, 512]), ps("left", [P, 2, 512])
        seg = ps("seg", [P, 2, 1024])
        gat = [s["gat0"], s["gat1"], s["gat2"], s["gat3"]]
        at = bank_at(W)
        blk = block()

        @blk.gpsimd
        def _(pool):
            gather_ring(nc, s, pool, k, idxs, rows, k.table_gat, 2, W)

        @blk.tensor
        def _(pe):
            def turn(g, j):
                await_(pe, s, s["hot"], g + 1)
                await_(pe, s, s["copied"], g + 1)
                for u in range(G):
                    ins = nc.tensor.transpose(turned[:, j % 2, u * P:(u + 1) * P], hot[:, j % 4, u, :], k.ident[:, :])
                ins.then_inc(s["turned"], 1)

            def left_scores(g, j, where):
                await_(pe, s, s["copied"], g + 3)
                await_(pe, s, s["score"], g + 1)
                for u in range(G):
                    ins = nc.tensor.matmul(left[:, j % 2, u * 8:(u + 1) * 8], hotT[:, j % 2, u, :],
                                           k.hsn[:, ds(where[u], 1), :].rearrange("p b h -> p (b h)"),
                                           start=True, stop=True)
                ins.then_inc(s["left"], 1)

            def segment_sums(g, j):
                d = j % 2
                await_(pe, s, s["scaled"], g + 1)
                await_(pe, s, s["accd"], g * G + G)
                for u in range(G):
                    ins = nc.tensor.matmul(seg[:, d, at[u]:at[u] + W], hot[:, j % 4, u, :], part[:, d, u, :],
                                           start=True, stop=True)
                ins.then_inc(s["seg"], 1)

            pe.sem_inc(s["seg"], 4)
            where, _ = load_registers(pe, k.blockrow[0:1, 0:3 * G], "pb0", 0, BLOCKS - 1)
            turn(0, 0)
            turn(1, 1)
            left_scores(0, 0, where[0:G])
            turn(2, 2)
            left_scores(1, 1, where[G:2 * G])
            left_scores(2, 2, where[2 * G:3 * G])
            segment_sums(0, 0)
            with pe.Fori(0, ROUNDS) as r:
                where, _ = load_registers(pe, k.blockrow[0:1, ds(r * UNROLL + 3 * G, UNROLL)], "pb", 0, BLOCKS - 1)
                for j in range(JG):
                    g = r * JG + j
                    turn(g + 3, j + 3)
                    segment_sums(g + 1, j + 1)
                    left_scores(g + 3, j + 3, where[j * G:(j + 1) * G])

        @blk.scalar
        def _(act):
            def copy_turned(g, j):
                d = j % 2
                await_(act, s, s["turned"], g + 1)
                await_(act, s, s["left"], g + 1)
                nc.scalar.copy(hotT[:, d], turned[:, d].rearrange("p (u e) -> p u e", e=P)).then_inc(s["copied"], 1)

            def weights_of(g, j):
                d = j % 2
                await_(act, s, s["sc"], g + 1)
                await_(act, s, s["seg"], g + 3)
                nc.scalar.activation(part[:, d, :, P:W], ex[:, d], ACT.Exp).then_inc(s["exped"], 1)

            def next_indices(g, j):
                await_(act, s, s["scaled"], g + 1)
                refill(nc, s, k, act, idxs, g + JG, j % JG)

            act.sem_inc(s["copied"], 2)
            act.sem_inc(s["left"], 2)
            for m in range(JG):
                refill(nc, s, k, act, idxs, m, m)
            for m in range(3):
                copy_turned(m, m)
            for m in range(2):
                weights_of(m, m)
                next_indices(m, m)
            with act.Fori(0, ROUNDS) as r:
                for j in range(JG):
                    g = r * JG + j
                    copy_turned(g + 3, j + 3)
                    weights_of(g + 2, j + 2)
                    next_indices(g + 2, j + 2)

        @blk.vector
        def _(dve):
            def one_hot(g, j):
                await_(dve, s, s["seg"], g + 1)
                nc.vector.tensor_tensor(hot[:, j % 4], across(k.iota[:, :], G), along(k.loc[:, ds(g * G, G)], P),
                                        ALU.is_equal).then_inc(s["hot"], 1)

            def score_step(r, g, j, n):
                d = j % 2
                lv = left[:, d, 0:G * 8].rearrange("p (u c) -> p u c", c=8)
                if n == 0:
                    await_(dve, s, s["left"], g + 3)
                    await_(dve, s, gat[j % JG], (r + j // JG) * 64 + 64)
                    nc.vector.tensor_tensor(t0[:, d], rows[:, j % JG, :, P:W], lv[:, :, 0:HEADS], ALU.add
                                            ).then_inc(s["score_step"], 1)
                elif n == 1:
                    await_(dve, s, s["score_step"], 2 * g + 1)
                    nc.vector.scalar_tensor_tensor(sc[:, d], t0[:, d], 0.2, t0[:, d], ALU.mult, ALU.max
                                                   ).then_inc(s["score_step"], 1)
                elif n == 2:
                    await_(dve, s, s["score_step"], 2 * g + 2)
                    nc.vector.tensor_tensor(ex[:, d], sc[:, d], lv[:, :, HEADS:8], ALU.subtract).then_inc(s["sc"], 1)
                else:
                    await_(dve, s, s["score"], g + 2)
                    nc.vector.tensor_tensor(k.smax[:, :], k.smax[:, :], sc[:, d].rearrange("p u h -> p (u h)"),
                                            ALU.max).then_inc(s["score"], 1)

            def scale(g, j):
                await_(dve, s, s["exped"], g + 1)
                hv = rows[:, j % JG, :, 0:P].rearrange("p u (h c) -> p u h c", c=HD)
                ov = part[:, j % 2, :, 0:P].rearrange("p u (h c) -> p u h c", c=HD)
                wv = part[:, j % 2, :, P:W].unsqueeze(3).to_broadcast([P, G, HEADS, HD])
                nc.vector.tensor_tensor(ov, hv, wv, ALU.mult).then_inc(s["scaled"], 1)

            dve.sem_inc(s["score"], 2)
            dve.sem_inc(s["accd"], 2 * G)
            for m in range(3):
                one_hot(m, m)
            for m in range(2):
                for n in range(4):
                    score_step(0, m, m, n)
                scale(m, m)
            with dve.Fori(0, ROUNDS) as r:
                where, _ = load_registers(dve, k.blockrow[0:1, ds(r * UNROLL, UNROLL)], "b_gat", 0, BLOCKS - 1)
                for j in range(JG):
                    g = r * JG + j
                    one_hot(g + 3, j + 3)
                    score_step(r, g + 2, j + 2, 0)

                    def next_scores(u):
                        if u < 3:
                            score_step(r, g + 2, j + 2, u + 1)

                    accumulate(nc, s, dve, k, seg[:, j % 2], g, where[j * G:(j + 1) * G], W, at, 4, next_scores)
                    scale(g + 2, j + 2)
            dve.wait_ge(s["accd"], STEPS + 2 * G)
            dve.wait_ge(s["score"], ROUNDS * JG + 4)


def node_gat(nc, k, t):
    with phase(nc, "ngat", "w once row top var std hn turned copied prod v stored used done right_read low "
               "expd x_used", soft={"x_in0": 16 * NR, "x_in1": 16 * NR}) as (block, s, sb, ps):
        c, sq, h = (sb(n, [P, NB, P]) for n in ("c", "sq", "h"))
        xs, ress = sb("x", [P, 2, NB, P]), sb("res", [P, 2, NB, P])
        st = sb("st", [P, 4, NB])
        hT = sb("hT", [P, NB * P])
        tab = sb("tab", [P, NB, P])
        wl, wr, att = sb("wl", [P, P]), sb("wr", [P, P]), sb("att", [P, P])
        e1, den = sb("e1", [P, NB, HEADS]), sb("den", [P, NB, HEADS])
        top = sb("top", [P, 1])
        topr = sb("topr", [1, 1])
        topb = sb("topb", [P, 1])
        turned, prod = ps("turned", [P, 2, 512]), ps("prod", [P, 2, 512])
        right = ps("right", [P, 2, 512])
        small = ps("small", [P, 512])
        blk = block()
        PER = 7 + LN_VECTOR + 4

        @blk.sync
        def _(sp):
            sp.dma_start(wl[:, :], t["L3_gnn_W_l"]).then_inc(s["w"], 16)
            sp.dma_start(wr[:, :], t["L3_gnn_W_r"]).then_inc(s["w"], 16)
            sp.dma_start(att[:, :], row_vector(t["L3_gnn_att"])).then_inc(s["w"], 16)
            with sp.Fori(0, NR // 2) as r:
                for d in range(2):
                    i = 2 * r + d
                    await_(sp, s, s["hn"], i + 1)
                    sp.dma_start(rows_of(k.x_dram, i), xs[:, d]).then_inc(s["stored"], 16)
                    await_(sp, s, s["stored"], 32 * i + 16)
                    sp.sem_inc(s["x_used"], 1)
                    await_(sp, s, s["done"], 2 * i + 2)
                    sp.dma_start(rows_of(k.table, i), tab[:, :, :]).then_inc(s["stored"], 16)
                    await_(sp, s, s["stored"], 32 * i + 32)
                    sp.sem_inc(s["used"], 1)

        @blk.gpsimd
        def _(pool):
            with pool.Fori(0, NR // 2) as r:
                for d in range(2):
                    await_(pool, s, s["x_used"], 2 * r + d + 1)
                    pool.dma_start(xs[:, d], rows_of(k.x_dram, 2 * r + d)).then_inc(s[f"x_in{d}"].sem, 16)
                    pool.dma_start(ress[:, d], rows_of(k.res_dram, 2 * r + d)).then_inc(s[f"x_in{d}"].sem, 16)

        @blk.vector
        def _(dve):
            step = [0]

            def once(ins):
                step[0] += 1
                ins.then_inc(s["once"], 1)
                dve.wait_ge(s["once"], step[0])

            dve.wait_ge(s["w"], 48)
            nc.vector.tensor_reduce(top[:, :], k.smax[:, :], AX, ALU.max).then_inc(s["top"], 1)
            dve.wait_ge(s["row"], 1)
            nc.vector.tensor_reduce(topr[:, :], small[0:1, 0:P], AX, ALU.max).then_inc(s["top"], 1)
            dve.wait_ge(s["row"], 2)
            once(nc.vector.tensor_copy(topb[:, :], small[:, P:P + 1]))
            with dve.Fori(0, NR // 2) as r:
                for d in range(2):
                    i = 2 * r + d
                    then = Chain(dve, s, s["v"], i, PER)
                    then(nc.vector.tensor_scalar(e1[:, :, :], k.hsn[:, ds(i * NB, NB), HEADS:8], -1.0, topb[:, 0:1],
                                                 ALU.mult, ALU.add))
                    nc.vector.tensor_scalar(e1[:, :, :], e1[:, :, :], 80.0, None, ALU.min).then_inc(s["low"], 1)
                    await_(dve, s, s["expd"], 2 * i + 1)
                    then(nc.vector.scalar_tensor_tensor(den[:, :, :], e1[:, :, :], 1e-8, acc_rows(k, i, HEADS, P),
                                                        ALU.mult, ALU.add))
                    then(nc.vector.reciprocal(den[:, :, :], den[:, :, :]))
                    then(nc.vector.tensor_tensor(c[:, :, :].rearrange("p b (h d) -> p b h d", d=HD),
                                                 acc_rows(k, i).rearrange("p b (h d) -> p b h d", d=HD),
                                                 den[:, :, :].unsqueeze(3).to_broadcast([P, NB, HEADS, HD]), ALU.mult))
                    await_(dve, s, s[f"x_in{d}"], 32 * r + 32)
                    then(nc.vector.tensor_tensor(c[:, :, :], c[:, :, :], ress[:, d], ALU.add))
                    nc.vector.tensor_scalar(sq[:, :, :], c[:, :, :], 0.0, None, ALU.min).then_inc(s["low"], 1)
                    then(nc.vector.scalar_tensor_tensor(xs[:, d], c[:, :, :], 0.0, xs[:, d], ALU.max, ALU.add))
                    await_(dve, s, s["expd"], 2 * i + 2)
                    then(nc.vector.scalar_tensor_tensor(xs[:, d], sq[:, :, :], -1.0, xs[:, d], ALU.add, ALU.add))
                    layer_norm_relu(nc, s, dve, then, i, xs[:, d], c[:, :, :], sq[:, :, :], st, h[:, :, :])
                    dve.sem_inc(s["hn"], 1)
                    await_(dve, s, s["done"], 2 * i + 1)
                    then(nc.vector.tensor_tensor(c[:, :, :], tab[:, :, :], blocks(flat(right[:, :, :])[:, 0:NB * P]),
                                                 ALU.add))
                    dve.sem_inc(s["right_read"], 1)
                    then(nc.vector.scalar_tensor_tensor(sq[:, :, :], c[:, :, :], 0.2, c[:, :, :], ALU.mult, ALU.max))
                    then(nc.vector.tensor_tensor(sq[:, :, :], sq[:, :, :], across(att[:, :], NB), ALU.mult))
                    then(nc.vector.tensor_reduce(k.selfl[:, ds(i * NB, NB)], sq[:, :, :], AX, ALU.add))
                    then.end()
            nc.vector.memset(k.acc[:, :], 0.0).then_inc(s["top"], 1)
            dve.wait_ge(s["top"], 3)

        @blk.scalar
        def _(act):
            act.sem_inc(s["used"], 1)
            act.sem_inc(s["x_used"], 2)
            with act.Fori(0, NR) as i:
                await_(act, s, s["low"], 2 * i + 1)
                nc.scalar.activation(e1[:, :, :], e1[:, :, :], ACT.Exp).then_inc(s["expd"], 1)
                await_(act, s, s["low"], 2 * i + 2)
                nc.scalar.activation(sq[:, :, :], sq[:, :, :], ACT.Exp).then_inc(s["expd"], 1)
                layer_norm_std(nc, s, act, i, st)
                await_(act, s, s["turned"], i + 1)
                nc.scalar.copy(hT[:, :], flat(turned[:, :, :])[:, 0:NB * P]).then_inc(s["copied"], 1)
                await_(act, s, s["prod"], i + 1)
                await_(act, s, s["used"], i + 1)
                nc.scalar.copy(tab[:, :, :], blocks(flat(prod[:, :, :])[:, 0:NB * P])).then_inc(s["done"], 1)
                await_(act, s, s["right_read"], i + 1)
                nc.scalar.copy(k.xr[:, ds(i * (NB * P), NB * P)], flat(right[:, :, :])[:, 0:NB * P]).then_inc(s["done"], 1)

        @blk.tensor
        def _(pe):
            pe.wait_ge(s["w"], 48)
            pe.wait_ge(s["top"], 1)
            nc.tensor.transpose(small[0:1, 0:P], top[:, :], k.ident[:, :]).then_inc(s["row"], 1)
            pe.wait_ge(s["top"], 2)
            nc.tensor.matmul(small[:, P:P + 1], k.ones[0:1, :], topr[:, :], start=True, stop=True).then_inc(s["row"], 1)
            tv, pv, rv = (flat(a[:, :, :]) for a in (turned, prod, right))
            with pe.Fori(0, NR) as i:
                await_(pe, s, s["hn"], i + 1)
                for b in range(NB):
                    ins = nc.tensor.transpose(tv[:, b * P:(b + 1) * P], h[:, b, :], k.ident[:, :])
                ins.then_inc(s["turned"], 1)
                await_(pe, s, s["copied"], i + 1)
                for b in range(NB):
                    nc.tensor.matmul(pv[:, b * P:(b + 1) * P], hT[:, b * P:(b + 1) * P], wl[:, :],
                                     start=True, stop=True)
                    ins = nc.tensor.matmul(rv[:, b * P:(b + 1) * P], hT[:, b * P:(b + 1) * P], wr[:, :],
                                           start=True, stop=True)
                ins.then_inc(s["prod"], 1)
                await_(pe, s, s["done"], 2 * i + 2)


def edges_logits(nc, k, t):
    with phase(nc, "logit", "w st0 st1 st2 st3 idx_ready hot turned copied mm moved leaky dots "
               "sums d", soft=ring_counts(1)) as (block, s, sb, ps):
        rows = sb("rows", [P, JG, G, P])
        idxs = sb("idxs", [P, JG, G], I32)
        hot, hotT = sb("hot", [P, 4, G, P]), sb("hotT", [P, 2, G, P])
        m, lk = sb("m", [P, 2, G, P]), sb("lk", [P, 2, G, P])
        lg = sb("lg", [P, 2, G])
        att = sb("att", [P, P])
        turned, mm, own = ps("turned", [P, 2, 512]), ps("mm", [P, 2, 512]), ps("own", [P, 2, 512])
        gat = [s["gat0"], s["gat1"], s["gat2"], s["gat3"]]
        sto = [s["st0"], s["st1"], s["st2"], s["st3"]]
        blk = block()

        @blk.sync
        def _(sp):
            sp.dma_start(att[:, :], row_vector(t["L3_gnn_att"])).then_inc(s["w"], 16)

            def store(r, g, j):
                await_(sp, s, gat[j], r * 64 + 64)
                sp.dma_start(k.rows_dram[ds(g, 1), :, :].rearrange("a p f -> (a p) f"),
                             rows[:, j].rearrange("p u f -> p (u f)")).then_inc(sto[j], 16)

            with sp.Fori(0, ROUNDS) as r:
                for j in range(JG):
                    store(r, r * JG + j, j)
            store(ROUNDS, ROUNDS * JG, 0)
            for j in range(JG):
                sp.wait_ge(sto[j], 16 * (ROUNDS + (1 if j == 0 else 0)))

        @blk.gpsimd
        def _(pool):
            gather_ring(nc, s, pool, k, idxs, rows, k.table, 1, D)

        @blk.tensor
        def _(pe):
            def turn(g, j):
                await_(pe, s, s["hot"], g + 1)
                await_(pe, s, s["copied"], g + 1)
                for u in range(G):
                    ins = nc.tensor.transpose(turned[:, j % 2, u * P:(u + 1) * P], hot[:, j % 4, u, :], k.ident[:, :])
                ins.then_inc(s["turned"], 1)

            def sides(r, g, j, where):
                d = j % 2
                await_(pe, s, s["copied"], g + 3)
                await_(pe, s, s["d"], g + 1)
                await_(pe, s, gat[j % JG], (r + j // JG) * 64 + 64)
                for u in range(G):
                    o = mm[:, d, u * P:(u + 1) * P]
                    nc.tensor.matmul(o, hotT[:, d, u, :], k.xr[:, ds(where[u] * P, P)], start=True, stop=False)
                    nc.tensor.matmul(o, k.ident[:, :], rows[:, j % JG, u, :], start=False, stop=True)
                    ins = nc.tensor.matmul(own[:, d, u:u + 1], hotT[:, d, u, :], k.selfl[:, ds(where[u], 1)],
                                           start=True, stop=True)
                ins.then_inc(s["mm"], 1)

            pe.sem_inc(s["turned"], 4)
            where, _ = load_registers(pe, k.blockrow[0:1, 0:G], "lb0", 0, BLOCKS - 1)
            turn(0, 0)
            turn(1, 1)
            sides(0, 0, 0, where)
            with pe.Fori(0, ROUNDS) as r:
                where, _ = load_registers(pe, k.blockrow[0:1, ds(r * UNROLL + G, UNROLL)], "lb", 0, BLOCKS - 1)
                for j in range(JG):
                    g = r * JG + j
                    turn(g + 2, j + 2)
                    sides(r, g + 1, j + 1, where[j * G:(j + 1) * G])

        @blk.scalar
        def _(act):
            def copy_turned(g, j):
                d = j % 2
                await_(act, s, s["turned"], g + 5)
                await_(act, s, s["mm"], g + 1)
                nc.scalar.copy(hotT[:, d], turned[:, d].rearrange("p (u e) -> p u e", e=P)).then_inc(s["copied"], 1)

            def move(r, g, j):
                d = j % 2
                await_(act, s, s["mm"], g + 3)
                await_(act, s, s["leaky"], g + 1)
                nc.scalar.copy(m[:, d], mm[:, d].rearrange("p (u f) -> p u f", f=P)).then_inc(s["moved"], 1)
                await_(act, s, sto[j % JG], (r + j // JG) * 16 + 16)
                refill(nc, s, k, act, idxs, g + JG, j % JG)

            act.sem_inc(s["copied"], 2)
            act.sem_inc(s["mm"], 2)
            act.sem_inc(s["leaky"], 2)
            for q in range(JG):
                refill(nc, s, k, act, idxs, q, q)
            copy_turned(0, 0)
            copy_turned(1, 1)
            move(0, 0, 0)
            with act.Fori(0, ROUNDS) as r:
                for j in range(JG):
                    g = r * JG + j
                    copy_turned(g + 2, j + 2)
                    move(r, g + 1, j + 1)

        @blk.vector
        def _(dve):
            def one_hot(g, j):
                await_(dve, s, s["turned"], g + 1)
                nc.vector.tensor_tensor(hot[:, j % 4], across(k.iota[:, :], G), along(k.loc[:, ds(g * G, G)], P),
                                        ALU.is_equal).then_inc(s["hot"], 1)

            def logits(g, j):
                d = j % 2
                await_(dve, s, s["moved"], g + 1)
                nc.vector.scalar_tensor_tensor(lk[:, d], m[:, d], 0.2, m[:, d], ALU.mult, ALU.max).then_inc(s["leaky"], 1)
                await_(dve, s, s["leaky"], g + 3)
                nc.vector.tensor_tensor(lk[:, d], lk[:, d], across(att[:, :], G), ALU.mult).then_inc(s["dots"], 1)
                await_(dve, s, s["dots"], g + 1)
                nc.vector.tensor_reduce(lg[:, d], lk[:, d], AX, ALU.add).then_inc(s["sums"], 1)
                await_(dve, s, s["sums"], g + 1)
                nc.vector.tensor_tensor(k.dlog[:, ds(g * G, G)], lg[:, d], own[:, d, 0:G], ALU.subtract
                                        ).then_inc(s["d"], 1)

            dve.sem_inc(s["d"], 2)
            dve.wait_ge(s["w"], 16)
            for q in range(3):
                one_hot(q, q)
            with dve.Fori(0, ROUNDS) as r:
                for j in range(JG):
                    g = r * JG + j
                    one_hot(g + 3, j + 3)
                    logits(g, j)
            dve.wait_ge(s["d"], ROUNDS * JG + 2)


def segment_maxima(nc, k):
    with phase(nc, "segmax", "v turned moved line keys back seg got ret exped row carry neg") as (block, s, sb, ps):
        d, valid, fwd, bwd = (k.xr[:, n * STEPS:(n + 1) * STEPS] for n in range(4))
        lines = k.xr[:, 4 * STEPS:5 * STEPS].rearrange("p (i e) -> p i e", e=P)
        same = k.xr[:, 5 * STEPS:7 * STEPS].rearrange("p (n c) -> p n c", n=2)
        key = sb("key", [P, 3, STEPS], I32)
        ab = sb("ab", [P, 2])
        abr = sb("abr", [1, 2, P])
        srow = sb("srow", [1, P + 2])
        carry = sb("carry", [P, 1])
        turned = ps("turned", [P, 2, 512])
        small = ps("small", [P, 512])
        small2 = ps("small2", [P, 512])
        blk = block()

        @blk.sync
        def _(sp):
            for n in range(3):
                sp.dma_start(key[:, n, :], k.key_dram[n:n + STEPS * P].rearrange("(q c) -> q c", q=P)
                             ).then_inc(s["keys"], 16)
            sp.wait_ge(s["moved"], KT)
            sp.dma_start(k.line_dram.rearrange("(i p e) -> p i e", p=P, e=P), lines[:, :, :]).then_inc(s["line"], 16)
            sp.wait_ge(s["line"], 16)
            sp.dma_start(d[:, :], k.line_dram.rearrange("(q c) -> q c", q=P)).then_inc(s["back"], 16)
            sp.wait_ge(s["seg"], 1)
            sp.dma_start(k.seg_dram.rearrange("(q c) -> q c", q=P), bwd[:, :]).then_inc(s["got"], 16)
            sp.wait_ge(s["got"], 16)
            sp.dma_start(lines[:, :, :], k.seg_dram.rearrange("(i p e) -> p i e", p=P, e=P)).then_inc(s["ret"], 16)
            sp.wait_ge(s["ret"], 16)

        @blk.vector
        def _(dve):
            step = [0]

            def then(ins):
                step[0] += 1
                ins.then_inc(s["v"], 1)
                dve.wait_ge(s["v"], step[0])

            then(nc.vector.tensor_scalar(valid[:, :], k.loc[:, 0:STEPS], 0.0, None, ALU.is_ge))
            then(nc.vector.scalar_tensor_tensor(valid[:, :], k.loc[:, 0:STEPS], float(P - 1), valid[:, :],
                                                ALU.is_le, ALU.mult))
            then(nc.vector.scalar_tensor_tensor(d[:, :], k.dlog[:, 0:STEPS], 0.0, valid[:, :], ALU.max, ALU.mult))
            dve.wait_ge(s["keys"], 48)
            then(nc.vector.tensor_tensor(same[:, 0, :], key[:, 1, :], key[:, 0, :], ALU.is_equal))
            then(nc.vector.tensor_tensor(same[:, 1, :], key[:, 1, :], key[:, 2, :], ALU.is_equal))
            dve.wait_ge(s["back"], 16)
            for n, (data, out) in enumerate(((d, fwd), (fwd, bwd))):
                back = n == 1
                turn = (lambda a: a[:, ::-1]) if back else (lambda a: a)
                sm, da, ou = turn(same[:, n, :]), turn(data[:, :]), turn(out[:, :])
                then(nc.vector.tensor_tensor_scan(ou, sm, da, 0.0, ALU.mult, ALU.max))
                then(nc.vector.tensor_reduce(ab[:, 0:1], same[:, n, :], AX, ALU.min))
                end = out[:, 0:1] if back else out[:, STEPS - 1:STEPS]
                nc.vector.tensor_copy(ab[:, 1:2], end).then_inc(s["carry"], 1)
                dve.wait_ge(s["row"], 2 * n + 1)
                then(nc.vector.tensor_copy(abr[:, 0, :], small[0:1, 0:P]))
                then(nc.vector.tensor_copy(abr[:, 1, :], small[0:1, P:2 * P]))
                then(nc.vector.memset(srow[:, :], 0.0))
                then(nc.vector.tensor_tensor_scan(turn(srow[:, 1:P + 1]), turn(abr[:, 0, :]), turn(abr[:, 1, :]), 0.0,
                                                  ALU.mult, ALU.max))
                dve.sem_inc(s["carry"], 1)
                dve.wait_ge(s["row"], 2 * n + 2)
                then(nc.vector.tensor_copy(carry[:, :], small2[:, 0:1]))
                then(nc.vector.tensor_tensor_scan(ou, sm, da, carry[:, 0:1], ALU.mult, ALU.max))
            dve.sem_inc(s["seg"], 1)
            for i in range(KT):
                dve.wait_ge(s["turned"], KT + i + 1)
                nc.vector.tensor_copy(fwd[:, i * P:(i + 1) * P], turned[:, i % 2, 0:P]).then_inc(s["moved"], 1)
            dve.wait_ge(s["moved"], 2 * KT)
            then(nc.vector.tensor_tensor(d[:, :], k.dlog[:, 0:STEPS], fwd[:, :], ALU.subtract))
            then(nc.vector.tensor_scalar(d[:, :], d[:, :], 0.0, None, ALU.min))
            dve.sem_inc(s["neg"], 1)
            then(nc.vector.memset(k.we[:, STEPS:TW, :], 0.0))

        @blk.scalar
        def _(act):
            for i in range(KT):
                act.wait_ge(s["turned"], i + 1)
                nc.scalar.copy(lines[:, i, :], turned[:, i % 2, 0:P]).then_inc(s["moved"], 1)
            act.wait_ge(s["neg"], 1)
            nc.scalar.activation(k.we[:, 0:STEPS, 0], d[:, :], ACT.Exp).then_inc(s["exped"], 1)
            nc.scalar.activation(k.we[:, 0:STEPS, 1], fwd[:, :], ACT.Exp, scale=-1.0).then_inc(s["exped"], 1)
            act.wait_ge(s["exped"], 2)

        @blk.tensor
        def _(pe):
            pe.wait_ge(s["v"], 3)
            for i in range(KT):
                if i >= 2:
                    pe.wait_ge(s["moved"], i - 1)
                nc.tensor.transpose(turned[:, i % 2, 0:P], d[:, i * P:(i + 1) * P], k.ident[:, :]).then_inc(s["turned"], 1)
            for n in range(2):
                pe.wait_ge(s["carry"], 2 * n + 1)
                nc.tensor.transpose(small[0:1, 0:P], ab[:, 0:1], k.ident[:, :])
                nc.tensor.transpose(small[0:1, P:2 * P], ab[:, 1:2], k.ident[:, :]).then_inc(s["row"], 1)
                pe.wait_ge(s["carry"], 2 * n + 2)
                lo = 2 if n else 0
                nc.tensor.matmul(small2[:, 0:1], srow[:, lo:lo + P], k.ones[0:1, 0:1], start=True, stop=True
                                 ).then_inc(s["row"], 1)
            pe.wait_ge(s["ret"], 16)
            pe.wait_ge(s["moved"], KT)
            for i in range(KT):
                if i >= 2:
                    pe.wait_ge(s["moved"], KT + i - 1)
                nc.tensor.transpose(turned[:, i % 2, 0:P], lines[:, i, :], k.ident[:, :]).then_inc(s["turned"], 1)


def edges_sum(nc, k):
    with phase(nc, "wsum", "in0 in1 in2 in3 hot cols scaled seg accd") as (block, s, sb, ps):
        rows = sb("rows", [P, JG, G * P])
        x = sb("x", [P, 4, G, W])
        hot = sb("hot", [P, 4, G, P])
        seg = ps("seg", [P, 4, 1024])
        ins_ = [s["in0"], s["in1"], s["in2"], s["in3"]]
        at = bank_at(P + 2)
        blk = block()

        @blk.sync
        def _(sp):
            def load(g, j):
                await_(sp, s, s["scaled"], g + 1)
                sp.dma_start(rows[:, j % JG, :], k.rows_dram[ds(g, 1), :, :].rearrange("a p f -> (a p) f")
                             ).then_inc(ins_[j % JG], 16)

            load(0, 0)
            with sp.Fori(0, ROUNDS) as r:
                for j in range(JG):
                    load(r * JG + j + 1, j + 1)

        @blk.scalar
        def _(act):
            def scale(r, g, j):
                d = j % 4
                await_(act, s, ins_[j % JG], (r + j // JG) * 16 + 16)
                await_(act, s, s["seg"], g + 1)
                wv = k.we[:, ds(g * G, G), :]
                nc.scalar.copy(x[:, d, :, P:P + 2], wv).then_inc(s["cols"], 1)
                await_(act, s, s["cols"], g + 1)
                for u in range(G):
                    ins = nc.scalar.activation(x[:, d, u, 0:P], rows[:, j % JG, u * P:(u + 1) * P], ACT.Copy,
                                               scale=x[:, d, u, P:P + 1])
                ins.then_inc(s["scaled"], 1)

            act.sem_inc(s["scaled"], JG)
            scale(0, 0, 0)
            with act.Fori(0, ROUNDS) as r:
                for j in range(JG):
                    scale(r, r * JG + j + 1, j + 1)

        @blk.tensor
        def _(pe):
            pe.sem_inc(s["seg"], 4)
            with pe.Fori(0, ROUNDS) as r:
                for j in range(JG):
                    g, d = r * JG + j, j % 4
                    await_(pe, s, s["hot"], G * g + G)
                    await_(pe, s, s["scaled"], g + JG + 1)
                    await_(pe, s, s["accd"], g * G + G)
                    for u in range(G):
                        ins = nc.tensor.matmul(seg[:, d, at[u]:at[u] + P + 2], hot[:, j % 4, u, :], x[:, d, u, 0:P + 2],
                                               start=True, stop=True)
                    ins.then_inc(s["seg"], 1)

        @blk.vector
        def _(dve):
            def one_hot(g, j, u):
                if u == 0:
                    await_(dve, s, s["seg"], g + 1)
                nc.vector.tensor_scalar(hot[:, j % 4, u, :], k.iota[:, :], k.loc[:, ds(g * G + u, 1)], None,
                                        ALU.is_equal).then_inc(s["hot"], 1)

            dve.sem_inc(s["accd"], 4 * G)
            for j in range(3):
                for u in range(G):
                    one_hot(j, j, u)
            with dve.Fori(0, ROUNDS) as r:
                where, _ = load_registers(dve, k.blockrow[0:1, ds(r * UNROLL, UNROLL)], "b_sum", 0, BLOCKS - 1)
                for j in range(JG):
                    g = r * JG + j
                    accumulate(nc, s, dve, k, seg[:, j % 4], g, where[j * G:(j + 1) * G], P + 2, at, 4,
                               lambda u: one_hot(g + 3, j + 3, u), 4)
            dve.wait_ge(s["accd"], STEPS + 4 * G)


def node_out(nc, k, t, out):
    with phase(nc, "nout", "w used v once tot row sqd sq_sum rooted stored dst_free done", soft={"x_in": 32 * NR}) as (block, s, sb, ps):
        xl, c = sb("xl", [P, NB, P]), sb("c", [P, NB, P])
        dst = sb("dst", [P, NB, P])
        col = sb("col", [P, 4, NB])
        bias, lnw, lnb = sb("bias", [P, P]), sb("lnw", [P, P]), sb("lnb", [P, P])
        real = sb("real", [P, 1])
        part = sb("part", [P, BLOCKS])
        tot = sb("tot", [P, 2])
        mu, std = sb("mu", [P, 1]), sb("std", [P, 3])
        small = ps("small", [P, 2, 512])
        blk = block()
        PER, PER2 = 12, 3
        accv = k.acc[:, :].rearrange("p (b w) -> p b w", w=W)[:, :, 0:P]

        @blk.sync
        def _(sp):
            sp.dma_start(bias[:, :], row_vector(t["L3_gnn_bias"])).then_inc(s["w"], 16)
            sp.dma_start(lnw[:, :], row_vector(t["L3_gnn_ln_w"])).then_inc(s["w"], 16)
            sp.dma_start(lnb[:, :], row_vector(t["L3_gnn_ln_b"])).then_inc(s["w"], 16)
            with sp.Fori(0, NR) as i:
                await_(sp, s, s["done"], i + 1)
                sp.dma_start(rows_of(out, i), dst[:, :, :]).then_inc(s["stored"], 16)
                await_(sp, s, s["stored"], 16 * i + 16)
                sp.sem_inc(s["dst_free"], 1)

        @blk.gpsimd
        def _(pool):
            pool.sem_inc(s["used"], 1)
            for n, src in enumerate((k.table, k.x_dram)):
                with pool.Fori(0, NR) as i:
                    await_(pool, s, s["used"], i + n * NR + 1)
                    pool.dma_start(xl[:, :, :], rows_of(src, i)).then_inc(s["x_in"].sem, 16)

        @blk.vector
        def _(dve):
            step = [0]

            def once(ins):
                step[0] += 1
                ins.then_inc(s["once"], 1)
                dve.wait_ge(s["once"], step[0])

            dve.wait_ge(s["w"], 48)
            once(nc.vector.tensor_scalar(real[:, :], k.step_f[:, 0:1], float(LAST_ROWS), None, ALU.is_lt))
            with dve.Fori(0, NR) as i:
                then = Chain(dve, s, s["v"], i, PER)
                deg = k.deg[:, ds(i * NB, NB)]
                one = lambda f: acc_rows(k, i, 1, f).rearrange("p b a -> p (b a)")
                then(nc.vector.tensor_scalar(col[:, 0, :], deg, 1.0, None, ALU.max))
                then(nc.vector.tensor_scalar(col[:, 1, :], deg, 0.0, None, ALU.is_equal))
                then(nc.vector.reciprocal(col[:, 0, :], col[:, 0, :]))
                then(nc.vector.tensor_tensor(col[:, 0, :], col[:, 0, :], one(P + 1), ALU.mult))
                then(nc.vector.tensor_tensor(col[:, 0, :], col[:, 0, :], col[:, 1, :], ALU.add))
                then(nc.vector.tensor_tensor(col[:, 2, :], col[:, 0, :], one(P), ALU.add))
                then(nc.vector.reciprocal(col[:, 2, :], col[:, 2, :]))
                await_(dve, s, s["x_in"], 16 * i + 16)
                then(nc.vector.tensor_tensor(c[:, :, :], xl[:, :, :], along(col[:, 0, :], P), ALU.mult))
                dve.sem_inc(s["used"], 1)
                then(nc.vector.tensor_tensor(c[:, :, :], c[:, :, :], acc_rows(k, i), ALU.add))
                then(nc.vector.tensor_tensor(c[:, :, :], c[:, :, :], along(col[:, 2, :], P), ALU.mult))
                then(nc.vector.tensor_tensor(c[:, :, :], c[:, :, :], across(bias[:, :], NB), ALU.add))
                then(nc.vector.scalar_tensor_tensor(acc_rows(k, i), c[:, :, :], 0.01, c[:, :, :], ALU.mult, ALU.max))
                then.end()
            lastb = accv[:, BLOCKS - 1, :]
            once(nc.vector.tensor_scalar(lastb, lastb, real[:, 0:1], None, ALU.mult))
            once(nc.vector.tensor_reduce(part[:, :], accv, AX, ALU.add))
            nc.vector.tensor_reduce(tot[:, 0:1], part[:, :], AX, ALU.add).then_inc(s["tot"], 1)
            dve.wait_ge(s["row"], 1)
            once(nc.vector.tensor_scalar(mu[:, :], small[:, 0, 0:1], 1.0 / (N * D), None, ALU.mult))
            once(nc.vector.tensor_scalar(accv, accv, mu[:, 0:1], None, ALU.subtract))
            once(nc.vector.tensor_scalar(lastb, lastb, real[:, 0:1], None, ALU.mult))
            dve.sem_inc(s["tot"], 1)
            dve.sem_inc(s["dst_free"], 1)
            dve.wait_ge(s["row"], 2)
            nc.vector.tensor_scalar(std[:, 0:1], small[:, 1, 0:1], 1.0 / (N * D), None, ALU.mult).then_inc(s["tot"], 1)
            dve.wait_ge(s["rooted"], 1)
            once(nc.vector.tensor_scalar(std[:, 2:3], std[:, 1:2], 1e-5, None, ALU.add))
            once(nc.vector.reciprocal(std[:, 2:3], std[:, 2:3]))
            once(nc.vector.tensor_scalar(lnw[:, :], lnw[:, :], std[:, 2:3], None, ALU.mult))
            with dve.Fori(0, NR) as i:
                then = Chain(dve, s, s["sqd"], i, PER2)
                then(nc.vector.tensor_tensor(c[:, :, :], acc_rows(k, i), across(lnw[:, :], NB), ALU.mult))
                then(nc.vector.tensor_tensor(c[:, :, :], c[:, :, :], across(lnb[:, :], NB), ALU.add))
                await_(dve, s, s["x_in"], 16 * i + 16 * NR + 16)
                await_(dve, s, s["dst_free"], i + 1)
                then(nc.vector.tensor_tensor(dst[:, :, :], c[:, :, :], xl[:, :, :], ALU.add))
                dve.sem_inc(s["used"], 1)
                dve.sem_inc(s["done"], 1)
                then.end()

        @blk.scalar
        def _(act):
            act.wait_ge(s["tot"], 2)
            nc.scalar.activation(k.xr[:, :].rearrange("p (b f) -> p b f", f=P), accv, ACT.Square, accum_out=tot[:, 1:2]).then_inc(s["sq_sum"], 1)
            act.wait_ge(s["tot"], 3)
            nc.scalar.activation(std[:, 1:2], std[:, 0:1], ACT.Sqrt).then_inc(s["rooted"], 1)

        @blk.tensor
        def _(pe):
            pe.wait_ge(s["tot"], 1)
            nc.tensor.matmul(small[:, 0, 0:1], k.ones[:, :], tot[:, 0:1], start=True, stop=True).then_inc(s["row"], 1)
            pe.wait_ge(s["sq_sum"], 1)
            nc.tensor.matmul(small[:, 1, 0:1], k.ones[:, :], tot[:, 1:2], start=True, stop=True).then_inc(s["row"], 1)


def move_tables(nc, k, name, to_dram, order):
    with phase(nc, name, "moved") as (block, s, sb, ps):
        idx, loc, row = k.tables_dram[order]
        pairs = [(row, k.blockrow[:, :])]
        if order == 0:
            pairs += [(idx, k.idx[:, :]), (loc, k.loc[:, :])]
        blk = block()

        @blk.sync
        def _(sp):
            for a, b in pairs:
                if to_dram:
                    sp.dma_start(a, b).then_inc(s["moved"], 16)
                else:
                    sp.dma_start(b, a).then_inc(s["moved"], 16)
            sp.wait_ge(s["moved"], 16 * len(pairs))


def layers(nc, k, t, out):
    node_input(nc, k, t)
    for layer in range(L):
        edges_gine(nc, k, t, layer)
        mlp(nc, k, t, layer)
    edges_mean(nc, k)
    def sb(name, shape):
        return nc.alloc_sbuf_tensor(name, shape, F32)

    k.hsn = sb("hsn", [P, BLOCKS, 2 * HEADS])
    k.smax = sb("smax", [P, G * HEADS])
    node_mean(nc, k, t)
    step_tables(nc, k, "tab_s", True)
    move_tables(nc, k, "load_s", False, 1)
    edges_gat(nc, k)
    k.xr = sb("xr", [P, NP])
    k.selfl = sb("selfl", [P, BLOCKS])
    node_gat(nc, k, t)
    move_tables(nc, k, "load_d", False, 0)
    k.dlog, k.we = sb("dlog", [P, TW]), sb("we", [P, TW, 2])
    edges_logits(nc, k, t)
    segment_maxima(nc, k)
    edges_sum(nc, k)
    node_out(nc, k, t, out)



_SMALL = ["L0_gnn_W_atom", "L0_gnn_b_atom", "L0_gnn_W_bond", "L0_gnn_b_bond", "L0_gnn_eps", "L0_gnn_W1", "L0_gnn_b1",
          "L0_gnn_g1", "L0_gnn_be1", "L0_gnn_W2", "L0_gnn_b2", "L0_gnn_gn", "L0_gnn_bet", "L0_gnn_W_out",
          "L0_gnn_b_out", "L1_gnn_W_l", "L1_gnn_b_l", "L1_gnn_W_r", "L2_gnn_W", "L2_gnn_A_left", "L2_gnn_A_right",
          "L2_gnn_residual_projection", "L3_gnn_W_l", "L3_gnn_W_r", "L3_gnn_att", "L3_gnn_bias", "L3_gnn_ln_w",
          "L3_gnn_ln_b"]


def kernel(**inputs):
    import numpy as np
    import concourse.bacc as bacc
    from concourse.bass_utils import run_bass_kernel_spmd as run

    nc = bacc.Bacc("TRN2", target_bir_lowering=False, num_devices=1)
    arrays = {
        "x": np.pad(np.asarray(inputs["x"]), ((0, NP - N), (0, 0))),
        "edge_t": np.ascontiguousarray(np.pad(np.asarray(inputs["edge_attr_128"]), ((0, TILES * P - E), (0, 0)))
                                       .reshape(TILES, P, D).transpose(0, 2, 1)),
    }
    for name, pad in (("src", PAD_SRC), ("dst", PAD_DST)):
        rows = np.pad(np.asarray(inputs[name]), (0, TPAD * P - E), constant_values=pad).reshape(TPAD, P)
        arrays[name + "_rows"] = rows
        arrays[name + "_cols"] = np.ascontiguousarray(rows.T)
    for name in _SMALL:
        arrays[name] = np.ascontiguousarray(inputs[name])
    t = {name: nc.dram_tensor("in_" + name, a.shape, mybir.dt.from_np(a.dtype), kind="ExternalInput").ap()
         for name, a in arrays.items()}
    out = nc.dram_tensor("out_0", (NP, D), F32, kind="ExternalOutput").ap()
    program(nc, t, out)
    r = run(nc, [{"in_" + name: a for name, a in arrays.items()}], core_ids=[0])
    return r.results[0]["out_0"][:N]
```
